# Optimizing a Trainium2 kernel written in Bass

```python
import numpy as np
import jax
import jax.numpy as jnp

def _softmax(x, axis=-1):
    return jax.nn.softmax(x, axis=axis)

def _gelu(x):
    return jax.nn.gelu(x, approximate=True)

def _silu(x):
    return jax.nn.silu(x)

def _sigmoid(x):
    return jax.nn.sigmoid(x)

def _layernorm(x, axis=-1, eps=1e-05):
    m = jnp.mean(x, axis=axis, keepdims=True)
    v = jnp.var(x, axis=axis, keepdims=True)
    return (x - m) / jnp.sqrt(v + eps)

def _scatter_add(tgt, idx, src, axis=0):
    return tgt.at[idx].add(src)

def _segment_sum(src, seg, n):
    return jax.ops.segment_sum(src, seg, n)
kernel_name = 'mk_flamingo_gated_d2_seqx_r4_d7c4d1'

def setup_inputs(seed: int=0):
    np.random.seed(seed)
    _w = jnp.asarray

    def _rec_inputs():
        import jax
        import jax.numpy as jnp
        _rk = jax.random.key(seed)
        x = 7.22e-05 + 1 * jax.random.normal(jax.random.fold_in(_rk, 1), (4, 1024, 256), jnp.float32)
        _lenS = 1024 - jax.random.randint(jax.random.fold_in(_rk, 7), (4,), 0, max(1, 1024 // 4) + 1, jnp.int32)
        _lenS2 = 77 - jax.random.randint(jax.random.fold_in(_rk, 8), (4,), 0, max(1, 77 // 4) + 1, jnp.int32)
        _ctx_768P = jax.random.normal(jax.random.fold_in(_rk, 11), (4, 16, 192), jnp.float32)
        _ctx_768c = jax.random.dirichlet(jax.random.fold_in(_rk, 511), 0.3 * jnp.ones((16,), jnp.float32), (4, 77))
        _ctx_768t = jnp.einsum('bsk,bkd->bsd', _ctx_768c, _ctx_768P)
        _ctx_768t = _ctx_768t * jax.lax.rsqrt(jnp.mean(jnp.square(_ctx_768t)) + 1e-12) * 0.953939
        ctx_768 = -0.000191848 + 0.999787 * (_ctx_768t + 0.3 * jax.random.normal(jax.random.fold_in(_rk, 611), (4, 77, 192), jnp.float32))
        _g = jax.random.normal(jax.random.fold_in(_rk, 9001), (2, 2), jnp.float32)
        _g = jnp.sign(_g) * jnp.maximum(jnp.abs(_g), 1.0) + (_g == 0) * 1.0
        g_xattn = _g[0]
        g_ffn = _g[1]
        return (x, ctx_768, g_xattn, g_ffn)
    x, ctx_768, g_xattn, g_ffn = _rec_inputs()

    def _L0_xattn_setup():
        import jax, jax.numpy as jnp
        import numpy as np
        B, LQ, LK = (4, 512, 512)
        D1, D2, H = (256, 192, 256)
        key = jax.random.key(seed)
        ks = jax.random.split(key, 9)
        s1, s2, sh = (1.0 / np.sqrt(D1), 1.0 / np.sqrt(D2), 1.0 / np.sqrt(H))
        return {'query': jax.random.normal(ks[0], (B, LQ, D1), jnp.float32), 'key': jax.random.normal(ks[1], (B, LK, D2), jnp.float32), 'value': jax.random.normal(ks[2], (B, LK, D2), jnp.float32), 'Wq': jax.random.normal(ks[3], (D1, H), jnp.float32) * s1, 'bq': jax.random.normal(ks[4], (H,), jnp.float32) * s1, 'Wk': jax.random.normal(ks[5], (D2, H), jnp.float32) * s2, 'bk': jax.random.normal(ks[6], (H,), jnp.float32) * s2, 'Wv': jax.random.normal(ks[7], (D2, H), jnp.float32) * s2, 'bv': jax.random.normal(ks[8], (H,), jnp.float32) * s2}
    _L0_xattn_all = _L0_xattn_setup()
    _L0_xattn_in = {k: v for k, v in _L0_xattn_all.items() if k in ('Wq', 'bq', 'Wk', 'bk', 'Wv', 'bv')}
    del _L0_xattn_all

    def _L0_ffn_setup():
        import jax, jax.numpy as jnp
        import numpy as np
        DIM = 256
        N_EXPERTS = 8
        D_FF = 512
        TOP_K = 2
        key = jax.random.key(seed)
        ks = jax.random.split(key, 5)
        s = 0.02
        return {'x': jax.random.normal(ks[0], (2, 512, DIM), dtype=jnp.float32), 'gate_w': jax.random.normal(ks[1], (N_EXPERTS, DIM), dtype=jnp.float32) * s, 'w1': jax.random.normal(ks[2], (N_EXPERTS, D_FF, DIM), dtype=jnp.float32) * s, 'w2': jax.random.normal(ks[3], (N_EXPERTS, DIM, D_FF), dtype=jnp.float32) * s, 'w3': jax.random.normal(ks[4], (N_EXPERTS, D_FF, DIM), dtype=jnp.float32) * s}
    _L0_ffn_all = _L0_ffn_setup()
    _L0_ffn_in = {k: v for k, v in _L0_ffn_all.items() if k in ('gate_w', 'w1', 'w2', 'w3')}
    del _L0_ffn_all

    def _L1_xattn_setup():
        import jax, jax.numpy as jnp
        import numpy as np
        HEADS = 16
        DIM_HEAD = 64
        SCALE = DIM_HEAD ** (-0.5)
        key = jax.random.key(seed)
        ks = jax.random.split(key, 7)
        B, SQ, SKV, QD, CD, ID = (4, 1024, 256, 256, 192, HEADS * DIM_HEAD)
        s = lambda d: 1.0 / np.sqrt(d)
        return {'x': jax.random.normal(ks[0], (B, SQ, QD), jnp.float32), 'context': jax.random.normal(ks[1], (B, SKV, CD), jnp.float32), 'Wq': jax.random.normal(ks[2], (QD, ID), jnp.float32) * s(QD), 'Wk': jax.random.normal(ks[3], (CD, ID), jnp.float32) * s(CD), 'Wv': jax.random.normal(ks[4], (CD, ID), jnp.float32) * s(CD), 'Wo': jax.random.normal(ks[5], (ID, QD), jnp.float32) * s(ID), 'bo': jnp.zeros((QD,), jnp.float32)}
    _L1_xattn_all = _L1_xattn_setup()
    _L1_xattn_in = {k: v for k, v in _L1_xattn_all.items() if k in ('Wq', 'Wk', 'Wv', 'Wo', 'bo')}
    del _L1_xattn_all

    def _L1_ffn_setup():
        import jax, jax.numpy as jnp
        import numpy as np
        CAPACITY = 2
        B, S, D, E, I = (4, 1024, 256, 8, 1024)
        key = jax.random.key(seed)
        k0, k1, k2, k3, k4 = jax.random.split(key, 5)
        x = jax.random.normal(k0, (B, S, D), dtype=jnp.float32)
        gate_w = jax.random.normal(k1, (E, D), dtype=jnp.float32) * 0.006
        w_gate = jax.random.normal(k2, (E, I, D), dtype=jnp.float32) * (1.0 / np.sqrt(D))
        w_up = jax.random.normal(k3, (E, I, D), dtype=jnp.float32) * (1.0 / np.sqrt(D))
        w_down = jax.random.normal(k4, (E, D, I), dtype=jnp.float32) * (1.0 / np.sqrt(I))
        return {'x': x, 'gate_w': gate_w, 'w_gate': w_gate, 'w_up': w_up, 'w_down': w_down}
    _L1_ffn_all = _L1_ffn_setup()
    _L1_ffn_in = {k: v for k, v in _L1_ffn_all.items() if k in ('gate_w', 'w_gate', 'w_up', 'w_down')}
    del _L1_ffn_all
    return {'x': x, 'ctx_768': ctx_768, 'g_xattn': g_xattn, 'g_ffn': g_ffn, 'L0_xattn_Wq': _L0_xattn_in['Wq'], 'L0_xattn_bq': _L0_xattn_in['bq'], 'L0_xattn_Wk': _L0_xattn_in['Wk'], 'L0_xattn_bk': _L0_xattn_in['bk'], 'L0_xattn_Wv': _L0_xattn_in['Wv'], 'L0_xattn_bv': _L0_xattn_in['bv'], 'L0_ffn_gate_w': _L0_ffn_in['gate_w'], 'L0_ffn_w1': _L0_ffn_in['w1'], 'L0_ffn_w2': _L0_ffn_in['w2'], 'L0_ffn_w3': _L0_ffn_in['w3'], 'L1_xattn_Wq': _L1_xattn_in['Wq'], 'L1_xattn_Wk': _L1_xattn_in['Wk'], 'L1_xattn_Wv': _L1_xattn_in['Wv'], 'L1_xattn_Wo': _L1_xattn_in['Wo'], 'L1_xattn_bo': _L1_xattn_in['bo'], 'L1_ffn_gate_w': _L1_ffn_in['gate_w'], 'L1_ffn_w_gate': _L1_ffn_in['w_gate'], 'L1_ffn_w_up': _L1_ffn_in['w_up'], 'L1_ffn_w_down': _L1_ffn_in['w_down']}

def reference(x, ctx_768, g_xattn, g_ffn, L0_xattn_Wq, L0_xattn_bq, L0_xattn_Wk, L0_xattn_bk, L0_xattn_Wv, L0_xattn_bv, L0_ffn_gate_w, L0_ffn_w1, L0_ffn_w2, L0_ffn_w3, L1_xattn_Wq, L1_xattn_Wk, L1_xattn_Wv, L1_xattn_Wo, L1_xattn_bo, L1_ffn_gate_w, L1_ffn_w_gate, L1_ffn_w_up, L1_ffn_w_down):
    import jax
    import jax.numpy as jnp

    def _L0_xattn_ref(query, key, value, Wq, bq, Wk, bk, Wv, bv):
        import jax, jax.numpy as jnp
        import numpy as np
        B, LQ, LK = (4, 512, 512)
        D1, D2, H = (256, 192, 256)
        q = jnp.einsum('bqd,dh->bqh', query, Wq) + bq
        k = jnp.einsum('bkd,dh->bkh', key, Wk) + bk
        v = jnp.einsum('bkd,dh->bkh', value, Wv) + bv
        scores = jnp.einsum('bqh,bkh->bqk', q, k)
        weights = jax.nn.softmax(scores, axis=-1)
        return jnp.einsum('bqk,bkh->bqh', weights, v)

    def _L0_ffn_ref(x, gate_w, w1, w2, w3):
        import jax, jax.numpy as jnp
        import numpy as np
        DIM = 256
        N_EXPERTS = 8
        D_FF = 512
        TOP_K = 2
        orig_shape = x.shape
        xf = x.reshape(-1, orig_shape[-1])
        scores = jnp.einsum('td,ed->te', xf, gate_w)
        probs = jax.nn.softmax(scores.astype(jnp.float32), axis=-1)
        weights, idx = jax.lax.top_k(probs, TOP_K)
        weights = weights / jnp.sum(weights, axis=-1, keepdims=True)
        weights = weights.astype(x.dtype)
        x1 = jax.nn.silu(jnp.einsum('td,efd->tef', xf, w1))
        x3 = jnp.einsum('td,efd->tef', xf, w3)
        out_all = jnp.einsum('tef,edf->ted', x1 * x3, w2)
        expert_outs = jnp.take_along_axis(out_all, idx[:, :, None], axis=1)
        result = jnp.einsum('tkd,tk->td', expert_outs, weights)
        return result.reshape(orig_shape)

    def _L1_xattn_ref(x, context, Wq, Wk, Wv, Wo, bo):
        import jax, jax.numpy as jnp
        import numpy as np
        HEADS = 16
        DIM_HEAD = 64
        SCALE = DIM_HEAD ** (-0.5)
        b, sq, _ = x.shape

        def split_heads(t):
            return t.reshape(b, -1, HEADS, DIM_HEAD).transpose(0, 2, 1, 3)
        q = split_heads(x @ Wq)
        k = split_heads(context @ Wk)
        v = split_heads(context @ Wv)
        sim = jnp.einsum('bhid,bhjd->bhij', q, k) * SCALE
        attn = jax.nn.softmax(sim, axis=-1)
        out = jnp.einsum('bhij,bhjd->bhid', attn, v)
        out = out.transpose(0, 2, 1, 3).reshape(b, sq, HEADS * DIM_HEAD)
        return out @ Wo + bo

    def _L1_ffn_ref(x, gate_w, w_gate, w_up, w_down):
        import jax, jax.numpy as jnp
        import numpy as np
        CAPACITY = 2
        B, S, D = x.shape
        E = gate_w.shape[0]
        k = S // E * CAPACITY
        logits = jnp.einsum('bsd,ed->bse', x, gate_w)
        affinity = jax.nn.softmax(logits, axis=-1)
        affinity = jnp.transpose(affinity, (0, 2, 1))
        gating, idx = jax.lax.top_k(affinity, k)
        bidx = jnp.arange(B)[:, None, None]
        x_in = x[bidx, idx]
        h = jax.nn.silu(jnp.einsum('bekd,eid->beki', x_in, w_gate)) * jnp.einsum('bekd,eid->beki', x_in, w_up)
        x_e = jnp.einsum('beki,edi->bekd', h, w_down)
        out = jnp.zeros_like(x).at[bidx, idx].add(gating[..., None] * x_e)
        return out
    x = x + jnp.tanh(g_xattn[0]) * _L0_xattn_ref(_layernorm(x, axis=-1), ctx_768, ctx_768, L0_xattn_Wq, L0_xattn_bq, L0_xattn_Wk, L0_xattn_bk, L0_xattn_Wv, L0_xattn_bv)
    x = x + jnp.tanh(g_ffn[0]) * _L0_ffn_ref(_layernorm(x, axis=-1), L0_ffn_gate_w, L0_ffn_w1, L0_ffn_w2, L0_ffn_w3)
    x = x + jnp.tanh(g_xattn[1]) * _L1_xattn_ref(_layernorm(x, axis=-1), ctx_768, L1_xattn_Wq, L1_xattn_Wk, L1_xattn_Wv, L1_xattn_Wo, L1_xattn_bo)
    x = x + jnp.tanh(g_ffn[1]) * _L1_ffn_ref(_layernorm(x, axis=-1), L1_ffn_gate_w, L1_ffn_w_gate, L1_ffn_w_up, L1_ffn_w_down)
    return x

_drawn_inputs = setup_inputs


def setup_inputs(seed=0):
    import zlib

    import numpy as np

    out = dict(_drawn_inputs(seed))
    spreads = {'g_ffn': (-1.0, 0.6), 'L1_xattn_bo': (0.0, 0.1)}
    factors = {'L0_xattn_bk': 8.0,
     'L0_ffn_gate_w': 5.887,
     'L0_ffn_w1': 5.301,
     'L0_ffn_w2': 5.206,
     'L0_ffn_w3': 5.235}
    for name, (base, spread) in spreads.items():
        noise = np.random.default_rng([zlib.crc32(name.encode()), seed]).standard_normal(out[name].shape)
        drawn = base * np.exp(spread * noise) if base else spread * noise
        out[name] = jnp.asarray(drawn.astype(out[name].dtype))
    for name, factor in factors.items():
        out[name] = (out[name] * factor).astype(out[name].dtype)
    return out
```

```python
from contextlib import ExitStack

import concourse.bass as bass
from concourse import mybir

F32 = mybir.dt.float32
F16 = mybir.dt.float16
BF16 = mybir.dt.bfloat16
I32 = mybir.dt.int32
U32 = mybir.dt.uint32
ALU = mybir.AluOpType
ACT = mybir.ActivationFunctionType
AX = mybir.AxisListType

P = 128
B, S, D = 4, 1024, 256
LK, DC = 77, 192
NKEY = B * LK
T = B * S // P
KD = D // P
E = 8
F0 = 512
F1 = 1024
GT = 4
NG = T // GT
EPS = 1e-5

SX = 256.0
SW = 256.0
SM = 64.0
SV = 64.0
SP = 256.0
SH = 16.0

BR = 256
REG = B * S + BR
NB0 = (2 * B * S + E * (BR - 1)) // BR
W0E = 2 * KD * F0 + (F0 // P) * D


def wait(e, sem, value):
    if not isinstance(value, int) or value > 0:
        e.wait_ge(sem, value)


class Chain:

    def __init__(self, engine, sem, turn, steps):
        self.engine, self.sem, self.base, self.steps, self.n = engine, sem, turn * steps, steps, 0

    def __call__(self, ins):
        self.n += 1
        ins.then_inc(self.sem, 1)
        self.engine.wait_ge(self.sem, self.base + self.n)

    def end(self):
        assert self.n == self.steps, (self.n, self.steps)


def pipeline(e, n, depth, work, unroll=2, straight=False):
    def step(j, phase):
        for lag, fn in work:
            item = j - lag
            if isinstance(item, int) and not 0 <= item < n:
                continue
            fn(item, (phase - lag) % unroll)

    first = depth + 1
    turns = (n - first) // unroll
    if turns < 2 or straight:
        turns = 0
    for j in range(min(first, n + depth - 1)):
        step(j, j % unroll)
    if turns:
        with e.Fori(0, turns) as u:
            for c in range(unroll):
                step(u * unroll + (first + c), (first + c) % unroll)
    for j in range(first + turns * unroll, n + depth - 1):
        step(j, j % unroll)


def mm3(pe, o, lh, ll, rh, rl, first, stop):
    pe.matmul(o, lh, rh, start=first, stop=False)
    pe.matmul(o, lh, rl, start=False, stop=False)
    return pe.matmul(o, ll, rh, start=False, stop=stop)


def least(a, limit):
    return min(a, limit) if isinstance(a, int) else a


def in_order(e, steps, order, n, straight=False):
    pipeline(e, n, max(lag for _, lag in order) + 1, [(lag, steps[name]) for name, lag in order], straight=straight)


def before(item, mine, other, order, n):
    names = [name for name, _ in order]
    ahead = dict(order)[mine] - dict(order)[other] + (names.index(other) < names.index(mine))
    return least(item + ahead, n)


def program(nc, a, out, x_rows, y_rows, n_rows):
    ctx = ExitStack()
    with ctx:
        def sb(name, shape, dt=F32, on=ctx):
            return on.enter_context(nc.sbuf_tensor(name, shape, dt))

        def ps(name, shape, dt=F32, on=ctx):
            return on.enter_context(nc.psum_tensor(name, shape, dt))

        def sem(name):
            return ctx.enter_context(nc.semaphore(name))

        X = sb("X", [P, T, D])
        ident = sb("ident", [P, P])
        th = sb("th", [P, 4])
        wts = sb("wts", [P, 2, T])
        islot = sb("islot", [P, 2, T], I32)
        aff = sb("aff", [P, S // P, B, E])
        gval = sb("gval", [P, 2 * S // E // P, B * E])
        gidx = sb("gidx", [P, 2 * S // E // P, B * E], I32)
        mhalf = sb("mhalf", [P, GT])

        l0 = ExitStack()
        Wh = sb("Wh", [P, E * W0E], F16, l0)
        Wl = sb("Wl", [P, E * W0E], F16, l0)
        blkrow = sb("blkrow", [P, NB0], I32, l0)
        blkw = sb("blkw", [P, NB0], I32, l0)
        padrow = sb("padrow", [P, E], I32, l0)
        a0 = ExitStack()
        stage = sb("stage", [P, 2, W0E], F32, a0)
        ctxT = stage[:, 0, 0:2 * NKEY].rearrange("p (k n) -> p k n", k=2)
        wk = stage[:, 0, 1024:1536].rearrange("p (k n) -> p k n", k=2)
        wv = stage[:, 0, 1536:2048].rearrange("p (k n) -> p k n", k=2)
        wqT = stage[:, 0, 2048:2560].rearrange("p (k n) -> p k n", k=2)
        KT = stage[:, 1, 0:2 * NKEY].rearrange("p (k n) -> p k n", k=2)
        bqs = sb("bqs", [P, KD], F32, a0)
        bks = sb("bks", [P, KD], F32, a0)
        bvs = sb("bvs", [1, D], F32, a0)
        gts = sb("gts", [P, KD, E], F32, a0)
        gth = sb("gth", [P, KD, E], F16, a0)
        gtl = sb("gtl", [P, KD, E], F16, a0)
        Mh = sb("Mh", [P, KD, NKEY], F16, a0)
        Ml = sb("Ml", [P, KD, NKEY], F16, a0)
        c0 = sb("c0", [1, NKEY], F32, a0)
        Vh = sb("Vh", [LK, B, D], F16, a0)
        Vl = sb("Vl", [LK, B, D], F16, a0)
        ones1 = sb("ones1", [1, P], F32, a0)
        trib = sb("trib", [P, P], BF16, a0)
        onesb = sb("onesb", [P, P], BF16, a0)
        iota8 = sb("iota8", [P, E], F32, a0)
        reg8 = sb("reg8", [P, E], F32, a0)
        thr = sb("thr", [P, E, 16], F32, a0)
        tri8 = sb("tri8", [P, E, E], F32, a0)
        iotaj = sb("iotaj", [P, NB0], F32, a0)
        base = sb("base", [P, E], F32, a0)
        st = [sb(f"st{n}", [P, GT, 6], F32, a0) for n in range(2)]
        mv = [sb(f"mv{n}", [P, 2, GT, 2], F32, a0) for n in range(2)]
        rstd = [sb(f"rstd{n}", [P, 2, GT], F32, a0) for n in range(2)]
        xa = sb("xa", [P, GT, D], F32, a0)
        xc = sb("xc", [P, 2, GT, D], F32, a0)
        xth = [sb(f"xth{n}", [P, 2, KD, GT * P], F16, a0) for n in range(2)]
        xtl = [sb(f"xtl{n}", [P, 2, KD, GT * P], F16, a0) for n in range(2)]
        smax = sb("smax", [P, GT], F32, a0)
        pr = sb("pr", [P, 2, GT, LK], F32, a0)
        ssum = sb("ssum", [P, GT], F32, a0)
        cf = sb("cf", [P, 2, GT], F32, a0)
        pth = sb("pth", [LK, GT * P], F16, a0)
        ptl = sb("ptl", [LK, GT * P], F16, a0)
        lg = sb("lg", [P, GT, E], F32, a0)
        top = sb("top", [P, T, E], F32, a0)
        ix = sb("ix", [P, GT, E], U32, a0)
        ixf = sb("ixf", [P, GT, E], F32, a0)
        pick = sb("pick", [P, 2, T, E], F32, a0)
        mx = sb("mx", [P, GT, E], F32, a0)
        both = sb("both", [P, GT, E], BF16, a0)
        rank = sb("rank", [P, T, E], F32, a0)
        prod = sb("prod", [P, 2, GT, E], F32, a0)
        slotf = sb("slotf", [P, 2, GT], F32, a0)
        slots = sb("slots", [P, 2, 2, GT], I32, a0)
        cnt = sb("cnt", [P, E], F32, a0)
        more = sb("more", [P, E, 16], F32, a0)
        nblk = sb("nblk", [P, E], F32, a0)
        tri8n = sb("tri8n", [P, E, E], F32, a0)
        cum = sb("cum", [P, E], F32, a0)
        adj = sb("adj", [P, E], F32, a0)
        done = sb("done", [P, NB0, E], F32, a0)
        done2 = sb("done2", [P, NB0, E], F32, a0)
        ej = sb("ej", [P, NB0], F32, a0)
        mj = sb("mj", [P, NB0], F32, a0)
        lt = sb("lt", [P, NB0], F32, a0)
        slotT = sb("slotT", [P, 2, T], F32, a0)

        pa = ExitStack()
        psT = ps("psT", [P, KD, GT * P], F32, pa)
        psS = ps("psS", [P, 512], F32, pa)
        psP = ps("psP", [P, GT * P], F32, pa)
        psO = ps("psO", [P, GT, D], F32, pa)
        psL = ps("psL", [P, 512], F32, pa)
        psR = ps("psR", [P, 512], F32, pa)
        pa.close()

        s_x = [sem(f"s_x{g}") for g in range(NG)]
        s_w = sem("s_w")
        s_setpe = sem("s_setpe")
        s_setact = sem("s_setact")
        s_pc = sem("s_pc")
        out_rows = out.rearrange("b s d -> (b s) d")
        xv = a["x"].rearrange("b (t p) d -> p (b t) d", p=P)
        with nc.Block() as block:
            @block.sync
            def _(sp):
                sp.dma_start(ctxT[:, 0, :], a["ctxT"][0:P, :]).then_inc(s_w, 16)
                sp.dma_start(ctxT[0:DC - P, 1, :], a["ctxT"][P:DC, :]).then_inc(s_w, 16)
                for dst, name in ((wk, "wk0"), (wv, "wv0")):
                    sp.dma_start(dst[:, 0, :], a[name][0:P, :]).then_inc(s_w, 16)
                    sp.dma_start(dst[0:DC - P, 1, :], a[name][P:DC, :]).then_inc(s_w, 16)
                sp.dma_start(wqT, a["wqT0"].rearrange("(k p) d -> p k d", p=P)).then_inc(s_w, 16)
                sp.dma_start(bqs[:], a["bq0"]).then_inc(s_w, 16)
                sp.dma_start(bks[:], a["bk0"]).then_inc(s_w, 16)
                sp.dma_start(bvs[:], a["bv0"]).then_inc(s_w, 16)
                sp.dma_start(gts[:], a["gate0"]).then_inc(s_w, 16)
                sp.dma_start(th[:, 0:2], a["g_xattn"].partition_broadcast(P)).then_inc(s_w, 16)
                sp.dma_start(th[:, 2:4], a["g_ffn"].partition_broadcast(P)).then_inc(s_w, 16)
                for g in range(NG):
                    sp.dma_start(X[:, GT * g:GT * g + GT, :], xv[:, GT * g:GT * g + GT, :]).then_inc(s_x[g], 16)

            W_ALL = 13 * 16

            @block.gpsimd
            def _(pool):
                ch = Chain(pool, s_pc, 0, 9)
                ch(pool.memset(ident[:], 0.0))
                ch(pool.affine_select(out=ident[:], in_=ident[:], compare_op=ALU.not_equal, fill=1.0,
                                      base=0, pattern=[[-1, P]], channel_multiplier=1))
                pool.memset(ones1[:], 1.0)
                pool.memset(mhalf[:], -0.5)
                ch(pool.memset(onesb[:], 1.0))
                ch(pool.affine_select(out=trib[:], in_=onesb[:], compare_op=ALU.is_gt, fill=0.0,
                                      base=0, pattern=[[1, P]], channel_multiplier=-1))
                ch(pool.memset(tri8[:], 1.0))
                ch(pool.affine_select(out=tri8[:], in_=tri8[:], compare_op=ALU.is_ge, fill=0.0,
                                      base=0, pattern=[[1, E], [-1, E]], channel_multiplier=0))
                pool.iota(iota8[:], [[1, E]], base=0, channel_multiplier=0, allow_small_or_imprecise_dtypes=True)
                pool.iota(reg8[:], [[REG, E]], base=0, channel_multiplier=0, allow_small_or_imprecise_dtypes=True)
                ch(pool.iota(base[:], [[REG, E]], base=0, channel_multiplier=0, allow_small_or_imprecise_dtypes=True))
                ch(pool.iota(thr[:], [[0, E], [BR, 16]], base=0, channel_multiplier=0,
                             allow_small_or_imprecise_dtypes=True))
                ch(pool.iota(iotaj[:], [[1, NB0]], base=0, channel_multiplier=0, allow_small_or_imprecise_dtypes=True))
                ch.end()

            @block.tensor
            def _(pe):
                pe.wait_ge(s_w, W_ALL)
                pe.wait_ge(s_pc, 9)
                for m in range(KD):
                    pe.matmul(psT[:, m, 0:NKEY], wk[:, 0, m * P:(m + 1) * P], ctxT[:, 0, :], start=True, stop=False)
                    pe.matmul(psT[:, m, 0:NKEY], wk[0:DC - P, 1, m * P:(m + 1) * P], ctxT[0:DC - P, 1, :],
                              start=False, stop=True).then_inc(s_setpe, 1)
                for b in range(B):
                    o = psO[0:LK, b, :]
                    pe.matmul(o, ctxT[:, 0, b * LK:(b + 1) * LK], wv[:, 0, :], start=True, stop=False)
                    pe.matmul(o, ctxT[0:DC - P, 1, b * LK:(b + 1) * LK], wv[0:DC - P, 1, :], start=False, stop=False)
                    pe.matmul(o, ones1[0:1, 0:LK], bvs[:], start=False, stop=True).then_inc(s_setpe, 1)
                pe.wait_ge(s_setact, 2)
                for m in range(KD):
                    o = (psS, psP)[m][:, 0:NKEY]
                    for k in range(KD):
                        last = pe.matmul(o, wqT[:, k, m * P:(m + 1) * P], KT[:, k, :], start=(k == 0), stop=(k == KD - 1))
                    last.then_inc(s_setpe, 1)
                for k in range(KD):
                    last = pe.matmul(psL[0:1, 0:NKEY], bqs[:, k:k + 1], KT[:, k, :], start=(k == 0), stop=(k == KD - 1))
                last.then_inc(s_setpe, 1)

            @block.scalar
            def _(act):
                for m in range(KD):
                    act.wait_ge(s_setpe, m + 1)
                    act.activation(KT[:, m, :], psT[:, m, 0:NKEY], ACT.Identity, bias=bks[:, m:m + 1]).then_inc(s_setact, 1)
                for b in range(B):
                    act.wait_ge(s_setpe, 4 + b // 2 * 2)
                    act.activation(Vh[:, b, :], psO[0:LK, b, :], ACT.Copy, scale=SV).then_inc(s_setact, 1)
                for m in range(KD):
                    act.wait_ge(s_setpe, 7 + m)
                    act.activation(Mh[:, m, :], (psS, psP)[m][:, 0:NKEY], ACT.Copy, scale=SM).then_inc(s_setact, 1)
                act.wait_ge(s_setpe, 9)
                act.activation(c0[:], psL[0:1, 0:NKEY], ACT.Copy, scale=SX * SM).then_inc(s_setact, 1)
                act.activation(gth[:], gts[:], ACT.Copy, scale=SW).then_inc(s_setact, 1)
                act.activation(th[:], th[:], ACT.Tanh).then_inc(s_setact, 1)

            @block.vector
            def _(dve):
                for b in range(B):
                    dve.wait_ge(s_setact, 4 + b // 2 * 2)
                    dve.scalar_tensor_tensor(Vl[:, b, :], psO[0:LK, b, :], SV, Vh[:, b, :], ALU.mult, ALU.subtract)
                for m in range(KD):
                    dve.wait_ge(s_setact, 7 + m)
                    dve.scalar_tensor_tensor(Ml[:, m, :], (psS, psP)[m][:, 0:NKEY], SM, Mh[:, m, :],
                                             ALU.mult, ALU.subtract)
                dve.wait_ge(s_setact, 10)
                dve.scalar_tensor_tensor(gtl[:], gts[:], SW, gth[:], ALU.mult, ALU.subtract)

        s_ws = [sem(f"s_ws{n}") for n in range(2)]
        s_we = sem("s_we")
        s_wh = sem("s_wh")
        s_wl = sem("s_wl")
        s_wp = sem("s_wp")
        s_st = [sem(f"s_st{n}") for n in range(2)]
        s_mv = [sem(f"s_mv{n}") for n in range(2)]
        s_rstd = [sem(f"s_rstd{n}") for n in range(2)]
        s_xn = [sem(f"s_xn{n}") for n in range(2)]
        s_xt = [sem(f"s_xt{n}") for n in range(2)]
        s_xh = [sem(f"s_xh{n}") for n in range(2)]
        s_xl = [sem(f"s_xl{n}") for n in range(2)]
        s_sc = sem("s_sc")
        s_smax = sem("s_smax")
        s_sub = sem("s_sub")
        s_exp = sem("s_exp")
        s_cf = sem("s_cf")
        s_pt = sem("s_pt")
        s_pth = sem("s_pth")
        s_ptl = sem("s_ptl")
        s_av = sem("s_av")
        s_res = sem("s_res")
        s_lg = sem("s_lg")
        s_route = sem("s_route")
        s_both = sem("s_both")
        s_rk = sem("s_rk")
        s_slot = sem("s_slot")
        s_sct = [sem(f"s_sct{n}") for n in range(2)]
        s_zero = sem("s_zero")
        s_fin = sem("s_fin")
        s_blk = sem("s_blk")
        s_fin2 = sem("s_fin2")
        s_pad = sem("s_pad")
        ROUTE = 10
        HW = W0E // 2
        PE0_ORDER = [("transpose_probs", 2), ("logits", 4), ("ranks", 4), ("transposes_out", 3), ("scores", 1), ("attend", 2),
                     ("transposes_in", 0)]
        ACT0_ORDER = [("high_out", 3), ("exps", 1), ("high_in", 0), ("probs_high", 1), ("weights_high", 3)]
        DVE0_ORDER = [("softmax", 2), ("residual", 3), ("stats_in", 0), ("stats_out", 3), ("choose", 4), ("low_in", 1),
                      ("place", 4), ("normalise_out", 3), ("weights_low", 5), ("probs_low", 2), ("denominators", 2),
                      ("normalise_in", 0), ("low_out", 3)]
        POOL0_ORDER = [("rstd_out", 4), ("rstd_in", 1), ("scatter", 5), ("weights_low", 5)]
        prodT = xa[:, 2:4, :].rearrange("p a (t e) -> p a t e", e=E)

        with nc.Block() as block:
            @block.sync
            def _(sp):
                def load_weights(g, par):
                    wait(sp, s_wl, g - 1)
                    wait(sp, s_wp, g - 1)
                    sp.dma_start(stage[:, par, :], a["w0"][g]).then_inc(s_ws[par], 16)
                for g in range(E):
                    load_weights(g, g % 2)
                sp.wait_ge(s_zero, 1)
                sp.wait_ge(s_blk, 1)
                zeros = xa[:, 0:2, :]
                for e in range(E):
                    row = sp.value_load(padrow[0:1, e:e + 1], min_val=0, max_val=E * REG - BR)
                    sp.dma_start(x_rows[bass.ds(row, BR), :].rearrange("(n p) d -> p n d", p=P), zeros).then_inc(s_pad, 16)
                sp.dma_start(x_rows[E * REG:E * REG + BR, :].rearrange("(n p) d -> p n d", p=P), zeros).then_inc(s_pad, 16)
                sp.wait_ge(s_pad, 16 * (E + 1))

            @block.gpsimd
            def _(pool):
                def rstd_of(n):
                    def run(g, par):
                        pool.wait_ge(s_mv[n], GT * g + GT)
                        pool.tensor_scalar(rstd[n][:, par, :], mv[n][:, par, :, 1], EPS, None, ALU.add).then_inc(s_rstd[n], 1)
                        pool.wait_ge(s_rstd[n], 2 * g + 1)
                        pool.tensor_tensor(rstd[n][:, par, :], rstd[n][:, par, :], mhalf[:], ALU.pow).then_inc(s_rstd[n], 1)
                    return run

                def weights_low(g, par):
                    pool.wait_ge(s_wh, g + 1)
                    pool.tensor_tensor(Wl[:, bass.ds(g * W0E + HW, HW)], stage[:, par, HW:], Wh[:, bass.ds(g * W0E + HW, HW)],
                                       ALU.subtract).then_inc(s_wp, 1)

                def scatter(g, par):
                    pool.wait_ge(s_slot, g + 1)
                    for k in range(GT):
                        for c in range(2):
                            pool.indirect_dma_start(x_rows[:, :], bass.IndirectOffsetOnAxis(slots[:, par, c, k:k + 1], 0),
                                                    xc[:, par, k, :], None, bounds_check=E * REG - 1,
                                                    oob_is_err=True).then_inc(s_sct[par], 16)
                steps = dict(rstd_out=rstd_of(1), rstd_in=rstd_of(0), weights_low=weights_low, scatter=scatter)
                in_order(pool, steps, POOL0_ORDER, NG, straight=True)
                for n in range(2):
                    pool.wait_ge(s_sct[n], 16 * T)
                pool.memset(xa[:, 0:2, :], 0.0).then_inc(s_zero, 1)

            @block.scalar
            def _(act):
                def high(n):
                    def run(g, par):
                        wait(act, s_lg if n else s_sc, g - 1)
                        for k in range(KD):
                            act.wait_ge(s_xt[n], KD * g + k + 1)
                            act.activation(xth[n][:, par, k, :], psT[:, k, :], ACT.Copy, scale=SX).then_inc(s_xh[n], 1)
                    return run

                def weights_high(g, par):
                    act.wait_ge(s_ws[par], 16 * (g // 2) + 16)
                    act.activation(stage[:, par, :], stage[:, par, :], ACT.Copy, scale=SW).then_inc(s_we, 1)
                    act.wait_ge(s_we, g + 1)
                    act.activation(Wh[:, bass.ds(g * W0E, W0E)], stage[:, par, :], ACT.Copy).then_inc(s_wh, 1)

                def exps(g, par):
                    act.wait_ge(s_sub, g + 1)
                    act.activation(pr[:, par, :, :], pr[:, par, :, :], ACT.Exp, scale=1.0 / (SX * SM)).then_inc(s_exp, 1)

                def probs_high(g, par):
                    wait(act, s_av, g)
                    act.wait_ge(s_pt, g + 1)
                    act.activation(pth[:], psP[0:LK, :], ACT.Copy, scale=SP).then_inc(s_pth, 1)

                steps = dict(high_in=high(0), high_out=high(1), exps=exps, probs_high=probs_high, weights_high=weights_high)
                in_order(act, steps, ACT0_ORDER, NG, straight=True)
                act.wait_ge(s_fin, 1)
                act.activation(wts[:, 1, :], wts[:, 0, :], ACT.Exp, scale=1.0 / (SX * SW)).then_inc(s_fin, 1)

            @block.tensor
            def _(pe):
                def transposes(n):
                    def run(g, par):
                        pe.wait_ge(s_xn[n], GT * g + GT)
                        src = xa[:, :, :] if n == 0 else xc[:, par, :, :]
                        for k in range(KD):
                            mine, other = (("transposes_in", "transposes_out"), ("transposes_out", "transposes_in"))[n]
                            if g > 0:
                                pe.wait_ge(s_xl[n], KD * (g - 1) + k + 1)
                            begun = before(g, mine, other, PE0_ORDER, NG)
                            if begun > 0:
                                pe.wait_ge(s_xl[1 - n], KD * (begun - 1) + k + 1)
                            for i in range(GT):
                                last = pe.transpose(psT[:, k, i * P:(i + 1) * P], src[:, i, k * P:(k + 1) * P], ident[:])
                            last.then_inc(s_xt[n], 1)
                    return run

                def scores(g, par):
                    pe.wait_ge(s_xl[0], KD * g + KD)
                    wait(pe, s_sub, g)
                    b = g // 2
                    for i in range(GT):
                        o = psS[:, i * LK:(i + 1) * LK]
                        t = slice(i * P, (i + 1) * P)
                        keys = bass.ds(b * LK, LK)
                        pe.matmul(o, ones1[:], c0[:, keys], start=True, stop=False)
                        for k in range(KD):
                            last = mm3(pe, o, xth[0][:, par, k, t], xtl[0][:, par, k, t], Mh[:, k, keys], Ml[:, k, keys],
                                       False, k == KD - 1)
                    last.then_inc(s_sc, 1)

                def transpose_probs(g, par):
                    pe.wait_ge(s_exp, g + 1)
                    wait(pe, s_ptl, g)
                    for i in range(GT):
                        last = pe.transpose(psP[0:LK, i * P:(i + 1) * P], pr[:, par, i, :], ident[:])
                    last.then_inc(s_pt, 1)

                def attend(g, par):
                    pe.wait_ge(s_ptl, g + 1)
                    wait(pe, s_res, GT * g)
                    vb = bass.ds((g // 2) * D, D)
                    for i in range(GT):
                        t = slice(i * P, (i + 1) * P)
                        last = mm3(pe, psO[:, i, :], pth[:, t], ptl[:, t], Vh2[:, vb], Vl2[:, vb], True, True)
                    last.then_inc(s_av, 1)

                def logits(g, par):
                    pe.wait_ge(s_xl[1], KD * g + KD)
                    wait(pe, s_route, ROUTE * g)
                    for i in range(GT):
                        t = slice(i * P, (i + 1) * P)
                        for k in range(KD):
                            last = mm3(pe, psL[:, i * E:(i + 1) * E], xth[1][:, par, k, t], xtl[1][:, par, k, t],
                                       gth[:, k, :], gtl[:, k, :], k == 0, k == KD - 1)
                    last.then_inc(s_lg, 1)

                def ranks(g, par):
                    pe.wait_ge(s_both, g + 1)
                    for i in range(GT + 1):
                        o = psR[:, i * E:(i + 1) * E]
                        for j in range(min(i, GT)):
                            last = pe.matmul(o, onesb[:], both[:, j, :], start=(j == 0), stop=(i == GT and j == GT - 1))
                        if i < GT:
                            last = pe.matmul(o, trib[:], both[:, i, :], start=(i == 0), stop=True)
                    last.then_inc(s_rk, 1)
                Vh2 = Vh[:, :, :].rearrange("p b d -> p (b d)")
                Vl2 = Vl[:, :, :].rearrange("p b d -> p (b d)")
                steps = dict(transposes_in=transposes(0), transposes_out=transposes(1), scores=scores,
                             transpose_probs=transpose_probs, attend=attend, logits=logits, ranks=ranks)
                in_order(pe, steps, PE0_ORDER, NG, straight=True)

            @block.vector
            def _(dve):
                def stats(n):
                    def run(g, par):
                        if n == 0:
                            dve.wait_ge(s_x[g], 16)
                        else:
                            dve.wait_ge(s_res, GT * g + GT)
                        rows = X[:, bass.ds(GT * g, GT), :]
                        for i in range(GT):
                            dve.bn_stats(st[n][:, i, :], rows[:, i, :]).then_inc(s_st[n], 1)
                        for i in range(GT):
                            dve.wait_ge(s_st[n], GT * g + i + 1)
                            dve.bn_aggr(mv[n][:, par, i, :], st[n][:, i, :]).then_inc(s_mv[n], 1)
                    return run

                def normalise(n):
                    def run(g, par):
                        rows = X[:, bass.ds(GT * g, GT), :]
                        dve.wait_ge(s_rstd[n], 2 * g + 2)
                        if n == 0:
                            wait(dve, s_xt[0], KD * g)
                        else:
                            wait(dve, s_sct[par], 16 * 2 * GT * (g // 2))
                        for i in range(GT):
                            dst = xa[:, i, :] if n == 0 else xc[:, par, i, :]
                            dve.tensor_scalar(dst, rows[:, i, :], mv[n][:, par, i, 0:1], rstd[n][:, par, i:i + 1],
                                              ALU.subtract, ALU.mult).then_inc(s_xn[n], 1)
                    return run

                def low(n):
                    def run(g, par):
                        for k in range(KD):
                            dve.wait_ge(s_xh[n], KD * g + k + 1)
                            dve.scalar_tensor_tensor(xtl[n][:, par, k, :], psT[:, k, :], SX, xth[n][:, par, k, :],
                                                     ALU.mult, ALU.subtract).then_inc(s_xl[n], 1)
                    return run

                def softmax(g, par):
                    dve.wait_ge(s_sc, g + 1)
                    wait(dve, s_pt, g - 1)
                    sc = psS[:, 0:GT * LK].rearrange("p (i k) -> p i k", i=GT)
                    dve.tensor_reduce(smax[:], sc, AX.X, ALU.max).then_inc(s_smax, 1)
                    dve.wait_ge(s_smax, g + 1)
                    dve.tensor_tensor(pr[:, par, :, :], sc, smax[:].unsqueeze(2).to_broadcast([P, GT, LK]),
                                      ALU.subtract).then_inc(s_sub, 1)

                def denominators(g, par):
                    ch = Chain(dve, s_cf, g, 3)
                    dve.wait_ge(s_exp, g + 1)
                    ch(dve.tensor_reduce(ssum[:], pr[:, par, :, :], AX.X, ALU.add))
                    ch(dve.reciprocal(ssum[:], ssum[:]))
                    ch(dve.tensor_scalar(cf[:, par, :], ssum[:], th[:, 0:1], 1.0 / (SP * SV), ALU.mult, ALU.mult))
                    ch.end()

                def probs_low(g, par):
                    dve.wait_ge(s_pth, g + 1)
                    dve.scalar_tensor_tensor(ptl[:], psP[0:LK, :], SP, pth[:], ALU.mult, ALU.subtract).then_inc(s_ptl, 1)

                def residual(g, par):
                    dve.wait_ge(s_av, g + 1)
                    rows = X[:, bass.ds(GT * g, GT), :]
                    for i in range(GT):
                        dve.scalar_tensor_tensor(rows[:, i, :], psO[:, i, :], cf[:, par, i:i + 1], rows[:, i, :],
                                                 ALU.mult, ALU.add).then_inc(s_res, 1)

                def weights_low(g, par):
                    dve.wait_ge(s_wh, g + 1)
                    dve.tensor_tensor(Wl[:, bass.ds(g * W0E, HW)], stage[:, par, 0:HW], Wh[:, bass.ds(g * W0E, HW)],
                                      ALU.subtract).then_inc(s_wl, 1)

                def choose(g, par):
                    ch = Chain(dve, s_route, g, ROUTE)
                    tiles = bass.ds(GT * g, GT)
                    dve.wait_ge(s_lg, g + 1)
                    ch(dve.tensor_copy(lg[:], psL[:, 0:GT * E].rearrange("p (i e) -> p i e", i=GT)))
                    for i in range(GT):
                        last = dve.max(mx[:, i, :], lg[:, i, :])
                    ch(last)
                    for i in range(GT):
                        last = dve.max_index(ix[:, i, :], mx[:, i, :], lg[:, i, :])
                    ch(last)
                    dve.tensor_copy(top[:, tiles, :], mx[:])
                    ch(dve.tensor_copy(ixf[:], ix[:]))
                    for c in range(2):
                        last = dve.tensor_tensor(pick[:, c, tiles, :], iota8[:].unsqueeze(1).to_broadcast([P, GT, E]),
                                                 ixf[:, :, c:c + 1].to_broadcast([P, GT, E]), ALU.is_equal)
                    ch(last)
                    dve.tensor_tensor(both[:], pick[:, 0, tiles, :], pick[:, 1, tiles, :], ALU.add).then_inc(s_both, 1)

                def place(g, par):
                    ch = Chain(dve, s_route, g, ROUTE)
                    ch.n = 5
                    tiles = bass.ds(GT * g, GT)
                    dve.wait_ge(s_rk, g + 1)
                    ch(dve.tensor_tensor(rank[:, tiles, :], psR[:, 0:GT * E].rearrange("p (i e) -> p i e", i=GT),
                                         base[:].unsqueeze(1).to_broadcast([P, GT, E]), ALU.add))
                    ch(dve.tensor_tensor(base[:], base[:], psR[:, GT * E:GT * E + E], ALU.add))
                    for c in range(2):
                        last = dve.tensor_tensor(prod[:, c, :, :], rank[:, tiles, :], pick[:, c, tiles, :], ALU.mult)
                    ch(last)
                    ch(dve.tensor_reduce(slotf[:], prod[:], AX.X, ALU.add))
                    wait(dve, s_sct[par], 16 * 2 * GT * (g // 2))
                    dve.tensor_copy(slots[:, par, :, :], slotf[:]).then_inc(s_slot, 1)
                    dve.wait_ge(s_slot, g + 1)
                    ch(dve.tensor_copy(slotf[:, 0, 0:1], slotf[:, 1, 0:1]))
                    ch.end()
                steps = dict(stats_in=stats(0), stats_out=stats(1), normalise_in=normalise(0), normalise_out=normalise(1),
                             low_in=low(0), low_out=low(1), softmax=softmax, denominators=denominators,
                             probs_low=probs_low, residual=residual, weights_low=weights_low, choose=choose, place=place)
                in_order(dve, steps, DVE0_ORDER, NG, straight=True)

                ch = Chain(dve, s_blk, 0, 18)
                ch(dve.tensor_copy(padrow[:], base[:]))
                ch(dve.tensor_tensor(cnt[:], base[:], reg8[:], ALU.subtract))
                ch(dve.tensor_tensor(more[:], cnt[:].unsqueeze(2).to_broadcast([P, E, 16]), thr[:], ALU.is_gt))
                ch(dve.tensor_reduce(nblk[:], more[:], AX.X, ALU.add))
                ch(dve.tensor_tensor(tri8n[:], tri8[:], nblk[:].unsqueeze(1).to_broadcast([P, E, E]), ALU.mult))
                ch(dve.tensor_reduce(cum[:], tri8n[:], AX.X, ALU.add))
                ch(dve.tensor_tensor(adj[:], cum[:], nblk[:], ALU.subtract))
                ch(dve.scalar_tensor_tensor(adj[:], adj[:], float(BR), reg8[:], ALU.mult, ALU.subtract))
                jj = iotaj[:].unsqueeze(2).to_broadcast([P, NB0, E])
                ch(dve.tensor_tensor(done[:], cum[:].unsqueeze(1).to_broadcast([P, NB0, E]), jj, ALU.is_le))
                ch(dve.tensor_reduce(ej[:], done[:], AX.X, ALU.add))
                ch(dve.tensor_tensor(done2[:], done[:], nblk[:].unsqueeze(1).to_broadcast([P, NB0, E]), ALU.mult))
                ch(dve.tensor_reduce(mj[:], done2[:], AX.X, ALU.add))
                ch(dve.tensor_tensor(mj[:], iotaj[:], mj[:], ALU.subtract))
                ch(dve.tensor_scalar(lt[:], ej[:], float(E), float(BR), ALU.is_lt, ALU.mult))
                ch(dve.tensor_tensor(mj[:], mj[:], lt[:], ALU.mult))
                ch(dve.scalar_tensor_tensor(lt[:], ej[:], float(REG), mj[:], ALU.mult, ALU.add))
                ch(dve.tensor_scalar(ej[:], ej[:], float(E - 1), float(W0E), ALU.min, ALU.mult))
                dve.tensor_copy(blkrow[:], lt[:])
                ch(dve.tensor_copy(blkw[:], ej[:]))
                ch.end()

                ch = Chain(dve, s_fin2, 0, 8)
                ch(dve.tensor_tensor(wts[:, 0, :], top[:, :, 1], top[:, :, 0], ALU.subtract))
                dve.tensor_copy(smax[:], smax[:]).then_inc(s_fin, 1)
                ch(dve.tensor_tensor(rank[:], rank[:], adj[:].unsqueeze(1).to_broadcast([P, T, E]), ALU.add))
                for c in range(2):
                    last = dve.tensor_tensor(prodT[:, c, :, :], rank[:], pick[:, c, :, :], ALU.mult)
                ch(last)
                ch(dve.tensor_reduce(slotT[:], prodT, AX.X, ALU.add))
                dve.tensor_copy(islot[:], slotT[:])
                dve.wait_ge(s_fin, 2)
                ch(dve.tensor_scalar(wts[:, 0, :], wts[:, 1, :], 1.0, None, ALU.add))
                ch(dve.reciprocal(wts[:, 0, :], wts[:, 0, :]))
                ch(dve.tensor_tensor(wts[:, 1, :], wts[:, 1, :], wts[:, 0, :], ALU.mult))
                ch(dve.tensor_scalar(wts[:], wts[:], th[:, 2:3], None, ALU.mult))
                ch.end()
        a0.close()

        FT = F0 // P
        HF = FT // 2
        UP, DOWN = KD * F0, 2 * KD * F0
        e0 = ExitStack()
        bx = sb("bx", [P, 2, 2, D], F32, e0)
        bxh = sb("bxh", [P, 2, KD, BR], F16, e0)
        bxl = sb("bxl", [P, 2, KD, BR], F16, e0)
        sil = sb("sil", [P, 2, HF, BR], F32, e0)
        hid = sb("hid", [P, 2, HF, BR], F32, e0)
        hh = sb("hh", [P, 2, FT, BR], F16, e0)
        hl = sb("hl", [P, 2, FT, BR], F16, e0)
        yo = sb("yo", [P, 2, 2, D], F32, e0)
        e0.close()
        pe0 = ExitStack()
        psX = [ps(f"psX{n}", [P, KD, BR], F32, pe0) for n in range(2)]
        psG = [ps(f"psG{n}", [P, HF, BR], F32, pe0) for n in range(2)]
        psU = [ps(f"psU{n}", [P, HF, BR], F32, pe0) for n in range(2)]
        psY = [ps(f"psY{n}", [P, 2, D], F32, pe0) for n in range(2)]
        pe0.close()
        b_in = [sem(f"b_in{n}") for n in range(2)]
        b_xt = sem("b_xt")
        b_xh = sem("b_xh")
        b_xl = sem("b_xl")
        b_g = [sem(f"b_g{n}") for n in range(2)]
        b_sil = [sem(f"b_sil{n}") for n in range(2)]
        b_hid = [sem(f"b_hid{n}") for n in range(2)]
        b_hh = [sem(f"b_hh{n}") for n in range(2)]
        b_hl = [sem(f"b_hl{n}") for n in range(2)]
        b_y = sem("b_y")
        b_yo = sem("b_yo")
        b_out = [sem(f"b_out{n}") for n in range(2)]
        BDEPTH = 4

        with nc.Block() as block:
            @block.sync
            def _(sp):
                def load(j, par):
                    wait(sp, b_xt, j - 1)
                    row = sp.value_load(blkrow[0:1, bass.ds(j, 1)], min_val=0, max_val=E * REG)
                    sp.dma_start(bx[:, par, :, :], x_rows[bass.ds(row, BR), :].rearrange("(n p) d -> p n d", p=P))\
                      .then_inc(b_in[par], 16)

                def store(j, par):
                    sp.wait_ge(b_yo, j + 1)
                    sp.dma_start(y_rows[bass.ds(j * BR, BR), :].rearrange("(n p) d -> p n d", p=P), yo[:, par, :, :])\
                      .then_inc(b_out[par], 16)
                pipeline(sp, NB0, BDEPTH, [(0, load), (3, store)])
                sp.wait_ge(b_out[0], 16 * ((NB0 + 1) // 2))
                sp.wait_ge(b_out[1], 16 * (NB0 // 2))

            @block.tensor
            def _(pe):
                def transposes(j, par):
                    pe.wait_ge(b_in[par], 16 * (j // 2) + 16)
                    wait(pe, b_xl, j - 1)
                    for k in range(KD):
                        for n in range(2):
                            last = pe.transpose(psX[par][:, k, n * P:(n + 1) * P], bx[:, par, n, k * P:(k + 1) * P], ident[:])
                    last.then_inc(b_xt, 1)

                def up(j, par):
                    w = pe.value_load(blkw[0:1, bass.ds(j, 1)], min_val=0, max_val=(E - 1) * W0E)
                    pe.wait_ge(b_xl, j + 1)
                    for half in range(2):
                        wait(pe, b_hid[half], j)
                        for psum, off in ((psG, 0), (psU, UP)):
                            for f in range(HF):
                                for k in range(KD):
                                    at = bass.ds(w + (off + k * F0 + (half * HF + f) * P), P)
                                    last = mm3(pe, psum[half][:, f, :], Wh[:, at], Wl[:, at], bxh[:, par, k, :],
                                               bxl[:, par, k, :], k == 0, k == KD - 1)
                        last.then_inc(b_g[half], 1)

                def down(j, par):
                    w = pe.value_load(blkw[0:1, bass.ds(j, 1)], min_val=0, max_val=(E - 1) * W0E)
                    for half in range(2):
                        pe.wait_ge(b_hl[half], j + 1)
                    wait(pe, b_yo, j - 1)
                    for n in range(2):
                        rows = slice(n * P, (n + 1) * P)
                        for f in range(FT):
                            at = bass.ds(w + (DOWN + f * D), D)
                            last = mm3(pe, psY[par][:, n, :], hh[:, par, f, rows], hl[:, par, f, rows], Wh[:, at], Wl[:, at],
                                       f == 0, f == FT - 1)
                    last.then_inc(b_y, 1)
                pipeline(pe, NB0, BDEPTH, [(2, up), (1, transposes), (3, down)])

            @block.scalar
            def _(act):
                def rows_high(j, par):
                    act.wait_ge(b_xt, j + 1)
                    wait(act, b_g[1], j - 1)
                    act.activation(bxh[:, par, :, :], psX[par][:, :, :], ACT.Copy, scale=SX).then_inc(b_xh, 1)

                def silu(j, par):
                    for half in range(2):
                        act.wait_ge(b_g[half], j + 1)
                        act.activation(sil[:, half, :, :], psG[half][:, :, :], ACT.Silu, scale=1.0 / (SX * SW))\
                           .then_inc(b_sil[half], 1)

                def results(j, par):
                    act.wait_ge(b_y, j + 1)
                    if not isinstance(j, int) or j >= 2:
                        act.wait_ge(b_out[par], 16 * (j // 2))
                    act.activation(yo[:, par, :, :], psY[par][:, :, :], ACT.Copy, scale=1.0 / (SH * SW)).then_inc(b_yo, 1)
                pipeline(act, NB0, BDEPTH, [(2, silu), (1, rows_high), (3, results)])

            @block.vector
            def _(dve):
                def rows_low(j, par):
                    dve.wait_ge(b_xh, j + 1)
                    dve.scalar_tensor_tensor(bxl[:, par, :, :], psX[par][:, :, :], SX, bxh[:, par, :, :],
                                             ALU.mult, ALU.subtract).then_inc(b_xl, 1)

                def hidden(j, par):
                    wait(dve, b_y, j - 1)
                    for half in range(2):
                        f = slice(half * HF, (half + 1) * HF)
                        dve.wait_ge(b_sil[half], j + 1)
                        dve.scalar_tensor_tensor(hid[:, half, :, :], psU[half][:, :, :], SH / (SX * SW), sil[:, half, :, :],
                                                 ALU.mult, ALU.mult).then_inc(b_hid[half], 1)
                        dve.wait_ge(b_hid[half], j + 1)
                        dve.tensor_copy(hh[:, par, f, :], hid[:, half, :, :]).then_inc(b_hh[half], 1)
                        dve.wait_ge(b_hh[half], j + 1)
                        dve.tensor_tensor(hl[:, par, f, :], hid[:, half, :, :], hh[:, par, f, :], ALU.subtract)\
                           .then_inc(b_hl[half], 1)
                pipeline(dve, NB0, BDEPTH, [(2, hidden), (1, rows_low)])

        l0.close()

        H, DH = 16, 64
        HP = H // 2
        CK = H * LK
        NC = (CK + P - 1) // P
        QK = CK // 4
        LASTC = CK - (NC - 1) * P
        SM1 = SM * DH ** -0.5
        l1 = ExitStack()
        M1h = sb("M1h", [P, B, KD, CK], F16, l1)
        M1l = sb("M1l", [P, B, KD, CK], F16, l1)
        N1 = sb("N1", [P, B, NC, 2 * D], F16, l1)
        gth1 = sb("gth1", [P, KD, E], F16, l1)
        gtl1 = sb("gtl1", [P, KD, E], F16, l1)
        bo = sb("bo", [P, D], F32, l1)
        gts1 = sb("gts1", [P, KD, E], F32, l1)
        thx1 = sb("thx1", [P, 1], F32, l1)
        u1 = ExitStack()
        ctx1 = sb("ctx1", [P, 2, NKEY], F32, u1)
        wk1 = sb("wk1", [P, 2, H * DH], F32, u1)
        wv1 = sb("wv1", [P, 2, H * DH], F32, u1)
        wq1 = sb("wq1", [P, HP, D], F32, u1)
        wo1 = sb("wo1", [P, HP, D], F32, u1)
        K1 = sb("K1", [P, HP, NKEY], F32, u1)
        V1 = sb("V1", [P, HP, NKEY], F32, u1)
        nst = sb("nst", [LK, H, 2, D], F16, u1)
        u1.close()
        pu = ExitStack()
        psM = [ps(f"psM{n}", [P, 512], F32, pu) for n in range(4)]
        psN = [ps(f"psN{n}", [P, 2, D], F32, pu) for n in range(4)]
        pu.close()
        u_w = sem("u_w")
        u_k = sem("u_k")
        u_v = sem("u_v")
        u_kc = sem("u_kc")
        u_vc = sem("u_vc")
        u_m = sem("u_m")
        u_mh = sem("u_mh")
        u_ml = sem("u_ml")
        u_n = sem("u_n")
        u_nh = sem("u_nh")
        u_nl = sem("u_nl")
        u_nd = sem("u_nd")
        u_g = sem("u_g")
        u_p = sem("u_p")

        def head(bank, i):
            return 2 * ((bank % 2) * 4 + i) + bank // 2

        def place_of(h):
            return (h % 2) * HP + h // 2

        segments = []
        for place_ in range(H):
            r, left = place_ * LK, LK
            while left:
                n_ = min(left, P - r % P)
                segments.append((place_, LK - left, n_, r // P, r % P))
                r, left = r + n_, left - n_

        def over_batches(e, body):
            for b in range(B):
                body(b)

        with nc.Block() as block:
            @block.sync
            def _(sp):
                sp.dma_start(ctx1[:, 0, :], a["ctxT"][0:P, :]).then_inc(u_w, 16)
                sp.dma_start(ctx1[0:DC - P, 1, :], a["ctxT"][P:DC, :]).then_inc(u_w, 16)
                for dst, name in ((wk1, "wk1"), (wv1, "wv1")):
                    sp.dma_start(dst[:, 0, :], a[name][0:P, :]).then_inc(u_w, 16)
                    sp.dma_start(dst[0:DC - P, 1, :], a[name][P:DC, :]).then_inc(u_w, 16)
                sp.dma_start(wq1[:], a["wqT1"].rearrange("(k p) d -> p k d", p=P)).then_inc(u_w, 16)
                sp.dma_start(wo1[:], a["wo1"].rearrange("(k p) d -> p k d", p=P)).then_inc(u_w, 16)
                sp.dma_start(gts1[:], a["gate1"]).then_inc(u_w, 16)
                sp.dma_start(bo[:], a["bo1"].partition_broadcast(P)).then_inc(u_w, 16)

                def move(b):
                    sp.wait_ge(u_nl, 4 * b + 4)
                    for q, k, n, c, p in segments:
                        sp.dma_start(N1[p:p + n, bass.ds(b, 1), c, :], nst[k:k + n, q:q + 1, :, :].rearrange("p q a d -> p q (a d)"))\
                          .then_inc(u_nd, 16)
                    sp.wait_ge(u_nd, 16 * len(segments) * b + 16 * len(segments))
                    sp.sem_inc(u_p, 1)
                over_batches(sp, move)

            @block.tensor
            def _(pe):
                pe.wait_ge(u_w, 16 * 10)
                for m in range(HP):
                    for w_, psum, s_done, s_free in ((wk1, psM, u_k, u_kc), (wv1, psN, u_v, u_vc)):
                        o = psum[m % 4][:, :] if psum is psM else psum[m % 4][:, :, :].rearrange("p a d -> p (a d)")
                        o = o[:, 0:NKEY]
                        wait(pe, s_free, m - 3)
                        pe.matmul(o, w_[:, 0, m * P:(m + 1) * P], ctx1[:, 0, :], start=True, stop=False)
                        pe.matmul(o, w_[0:DC - P, 1, m * P:(m + 1) * P], ctx1[0:DC - P, 1, :], start=False, stop=True)\
                          .then_inc(s_done, 1)
                pe.wait_ge(u_kc, HP)
                pe.wait_ge(u_vc, HP)

                def fold(b):
                    keys = bass.ds(b * LK, LK)
                    for m in range(KD):
                        wait(pe, u_ml, (KD * b + m) * 4)
                        for i in range(4):
                            for bank in (0, 2, 1, 3):
                                h = head(bank, i)
                                p = DH * (h % 2)
                                last = pe.matmul(psM[bank][:, i * LK:(i + 1) * LK], wq1[p:p + DH, h // 2, m * P:(m + 1) * P],
                                                 K1[p:p + DH, h // 2, keys], start=True, stop=True)
                        last.then_inc(u_m, 1)
                    for v in range(4):
                        if isinstance(b, int):
                            wait(pe, u_nl, 4 * b + v - 1)
                        else:
                            pe.wait_ge(u_nl, 4 * b + (v - 1))
                        for i in range(2):
                            for odd in range(2):
                                h = 4 * v + 2 * i + odd
                                p = DH * odd
                                last = pe.matmul(psN[(v % 2) * 2 + odd][0:LK, i, :], V1[p:p + DH, h // 2, keys],
                                                 wo1[p:p + DH, h // 2, :], start=True, stop=True)
                        last.then_inc(u_n, 1)
                over_batches(pe, fold)

            @block.scalar
            def _(act):
                for m in range(HP):
                    act.wait_ge(u_k, m + 1)
                    act.activation(K1[:, m, :], psM[m % 4][:, 0:NKEY], ACT.Copy).then_inc(u_kc, 1)
                act.activation(gth1[:], gts1[:], ACT.Copy, scale=SW).then_inc(u_g, 1)

                def high(b):
                    for m in range(KD):
                        act.wait_ge(u_m, KD * b + (m + 1))
                        for bank in range(4):
                            act.activation(M1h[:, bass.ds(b, 1), m, bank * QK:(bank + 1) * QK], psM[bank][:, 0:QK].unsqueeze(1), ACT.Copy,
                                           scale=SM1).then_inc(u_mh, 1)
                    if isinstance(b, int):
                        wait(act, u_p, b)
                    else:
                        act.wait_ge(u_p, b)
                    for v in range(4):
                        act.wait_ge(u_n, 4 * b + (v + 1))
                        for odd in range(2):
                            q = odd * HP + 2 * v
                            ins = act.activation(nst[:, q:q + 2, 0, :], psN[(v % 2) * 2 + odd][0:LK, :, :], ACT.Copy, scale=SV)
                        ins.then_inc(u_nh, 1)
                over_batches(act, high)

            @block.vector
            def _(dve):
                dve.wait_ge(u_w, 160)
                dve.tensor_scalar(bo[:], bo[:], th[:, 1:2], None, ALU.mult)
                for m in range(HP):
                    dve.wait_ge(u_v, m + 1)
                    dve.tensor_copy(V1[:, m, :], psN[m % 4][:, :, :].rearrange("p a d -> p (a d)")[:, 0:NKEY]).then_inc(u_vc, 1)
                dve.wait_ge(u_g, 1)
                dve.scalar_tensor_tensor(gtl1[:], gts1[:], SW, gth1[:], ALU.mult, ALU.subtract)

                def low(b):
                    for m in range(KD):
                        for bank in range(4):
                            dve.wait_ge(u_mh, (KD * 4) * b + (4 * m + bank + 1))
                            dve.scalar_tensor_tensor(M1l[:, bass.ds(b, 1), m, bank * QK:(bank + 1) * QK], psM[bank][:, 0:QK].unsqueeze(1), SM1,
                                                     M1h[:, bass.ds(b, 1), m, bank * QK:(bank + 1) * QK],
                                                     ALU.mult, ALU.subtract).then_inc(u_ml, 1)
                    for v in range(4):
                        dve.wait_ge(u_nh, 4 * b + (v + 1))
                        for odd in range(2):
                            q = odd * HP + 2 * v
                            ins = dve.scalar_tensor_tensor(nst[:, q:q + 2, 1, :], psN[(v % 2) * 2 + odd][0:LK, :, :], SV,
                                                           nst[:, q:q + 2, 0, :], ALU.mult, ALU.subtract)
                        ins.then_inc(u_nl, 1)
                over_batches(dve, low)


        m1 = ExitStack()
        yg = sb("yg", [P, 2, 2, D], F32, m1)
        st1 = [sb(f"st1{n}", [P, 6], F32, m1) for n in range(2)]
        mv1 = [sb(f"mv1{n}", [P, 2, 2], F32, m1) for n in range(2)]
        rs1 = [sb(f"rs1{n}", [P, 2, 1], F32, m1) for n in range(2)]
        xn1 = [sb(f"xn1{n}", [P, 2, D], F32, m1) for n in range(2)]
        xh1 = [sb(f"xh1{n}", [P, 2, KD, P], F16, m1) for n in range(2)]
        xl1 = [sb(f"xl1{n}", [P, 2, KD, P], F16, m1) for n in range(2)]
        mx1 = sb("mx1", [P, H], F32, m1)
        pr1 = sb("pr1", [P, 2, CK], F32, m1)
        sum1 = sb("sum1", [P, 2, H], F32, m1)
        ph1 = sb("ph1", [P, NC, P], F16, m1)
        pl1 = sb("pl1", [P, NC, P], F16, m1)
        lmx = sb("lmx", [P, 1], F32, m1)
        lex = sb("lex", [P, 2, E], F32, m1)
        lsum = sb("lsum", [P, 2, 1], F32, m1)
        m1.close()
        pm1 = ExitStack()
        psS1 = ps("psS1", [P, 4, 512], F32, pm1)
        psXa = ps("psXa", [P, KD, P], F32, pm1)
        psP1 = [ps(f"psP1{n}", [P, 4, P], F32, pm1) for n in range(2)]
        psOL = ps("psOL", [P, 2, D], F32, pm1)
        psO1, psL1 = psOL[:, 0, :], psOL[:, 1, :]
        pm1.close()
        CH = [(0, 4), (4, 8), (8, NC)]
        c_y = [sem(f"c_y{n}") for n in range(2)]
        c_comb = sem("c_comb")
        c_mv = [sem(f"c_mv{n}") for n in range(2)]
        c_rs = [sem(f"c_rs{n}") for n in range(2)]
        c_xn = [sem(f"c_xn{n}") for n in range(2)]
        c_xt = [sem(f"c_xt{n}") for n in range(2)]
        c_xh = [sem(f"c_xh{n}") for n in range(2)]
        c_xl = [sem(f"c_xl{n}") for n in range(2)]
        c_bo = sem("c_bo")
        c_sc = [sem(f"c_sc{n}") for n in range(2)]
        c_mx = sem("c_mx")
        c_sub = [sem(f"c_sub{n}") for n in range(2)]
        c_exp = [sem(f"c_exp{n}") for n in range(2)]
        c_rcp = sem("c_rcp")
        c_pn = sem("c_pn")
        c_pt = [sem(f"c_pt{n}") for n in range(3)]
        c_ph = [sem(f"c_ph{n}") for n in range(3)]
        c_pl = [sem(f"c_pl{n}") for n in range(3)]
        c_av = [sem(f"c_av{n}") for n in range(3)]
        c_res = sem("c_res")
        c_lg = sem("c_lg")
        c_lm = sem("c_lm")
        c_ls = sem("c_ls")
        c_le = sem("c_le")
        c_aff = sem("c_aff")
        c_one = sem("c_one")
        c_tick = sem("c_tick")
        c_out = [sem(f"c_out{n}") for n in range(2)]

        PE_ORDER = [("turn0", 4), ("transposes_out", 6), ("scores0", 2), ("scores1", 2), ("logits", 6), ("turn2", 4),
                    ("transposes_in", 1), ("outputs0", 4), ("turn1", 3), ("outputs1", 4), ("outputs2", 4)]
        ACT_ORDER = [("probs_high0", 4), ("high_out", 6), ("probs_high1", 4), ("exps0", 2), ("high_in", 1), ("probs_high2", 4),
                     ("exps1", 2), ("router_exp", 7)]
        DVE_ORDER = [("probs_low0", 4), ("maxima0", 2), ("normalise_in", 1), ("low_out", 6), ("router_sub", 6), ("maxima1", 2),
                     ("probs_low1", 4), ("low_in", 1), ("probs_low2", 4), ("combine", 0), ("normalise_out", 5),
                     ("residual", 4), ("reciprocals", 2), ("router_norm", 7)]
        POOL_ORDER = [("gather", 0), ("add_bias", 2), ("rstd_out", 5), ("rstd_in", 1), ("normalise_probs", 3)]

        def apart(e, sem_, value):
            wait(e, sem_, value)
            if not isinstance(value, int):
                e.sem_inc(c_tick, 1)

        with nc.Block() as block:
            @block.sync
            def _(sp):
                def store(t, par):
                    sp.wait_ge(c_xn[1], t + 1)
                    sp.dma_start(out_rows[bass.ds(t * P, P), :], X[:, bass.ds(t, 1), :].rearrange("p t d -> p (t d)"))\
                      .then_inc(c_out[par], 16)
                    sp.dma_start(n_rows[bass.ds(t * P, P), :], xn1[1][:, par, :]).then_inc(c_out[par], 16)
                pipeline(sp, T, 1, [(0, store)])
                for n in range(2):
                    sp.wait_ge(c_out[n], 16 * T)

            @block.gpsimd
            def _(pool):
                def rstd_of(n):
                    def run(t, par):
                        pool.wait_ge(c_mv[n], 2 * t + 2)
                        pool.tensor_scalar(rs1[n][:, par, :], mv1[n][:, par, 1:2], EPS, None, ALU.add).then_inc(c_rs[n], 1)
                        pool.wait_ge(c_rs[n], 2 * t + 1)
                        pool.tensor_tensor(rs1[n][:, par, :], rs1[n][:, par, :], mhalf[:, 0:1], ALU.pow).then_inc(c_rs[n], 1)
                    return run

                def normalise_probs(t, par):
                    pool.wait_ge(c_rcp, t + 1)
                    p = pr1[:, par, :].rearrange("p (h k) -> p h k", h=H)
                    pool.tensor_tensor(p, p, sum1[:, par, :].unsqueeze(2).to_broadcast([P, H, LK]), ALU.mult).then_inc(c_pn, 1)

                def gather(t, par):
                    wait(pool, c_comb, 2 * (t - 1))
                    for c in range(2):
                        pool.indirect_dma_start(yg[:, par, c, :], None, y_rows[:, :],
                                                bass.IndirectOffsetOnAxis(islot[:, c, t:t + 1], 0)).then_inc(c_y[par], 16)

                def add_bias(t, par):
                    pool.wait_ge(c_xn[0], t + 1)
                    pool.tensor_tensor(X[:, t, :], X[:, t, :], bo[:], ALU.add).then_inc(c_bo, 1)
                steps = dict(gather=gather, add_bias=add_bias, rstd_out=rstd_of(1), rstd_in=rstd_of(0),
                             normalise_probs=normalise_probs)
                in_order(pool, steps, POOL_ORDER, T, straight=True)

            @block.scalar
            def _(act):
                def high(n):
                    def run(t, par):
                        if n:
                            wait(act, c_lg, t - 1)
                        else:
                            wait(act, c_sc[0], t - 1)
                            wait(act, c_sc[1], t - 1)
                        act.wait_ge(c_xt[n], t + 1)
                        act.activation(xh1[n][:, par, :, :], psXa[:], ACT.Copy, scale=SX).then_inc(c_xh[n], 1)
                    return run

                def exps(half):
                    def run(t, par):
                        act.wait_ge(c_sub[half], t + 1)
                        for n in range(3):
                            wait(act, c_pt[n], t - 1)
                        for q in (2 * half, 2 * half + 1):
                            for i in range(4):
                                h = 4 * q + i
                                ins = act.activation(pr1[:, par, h * LK:(h + 1) * LK], psS1[:, q, i * LK:(i + 1) * LK], ACT.Exp,
                                                     bias=mx1[:, h:h + 1], scale=1.0 / (SX * SM), accum_out=sum1[:, par, h:h + 1])
                        ins.then_inc(c_exp[half], 1)
                    return run

                def probs_high(n):
                    def run(t, par):
                        a_, b_ = CH[n]
                        act.wait_ge(c_pt[n], t + 1)
                        wait(act, c_av[n], t)
                        if b_ == NC:
                            act.activation(ph1[:, a_:b_ - 1, :], psP1[0][:, 0:b_ - a_ - 1, :], ACT.Copy, scale=SP)
                            ins = act.activation(ph1[0:LASTC, b_ - 1, :], psP1[0][0:LASTC, b_ - a_ - 1, :], ACT.Copy, scale=SP)
                        else:
                            ins = act.activation(ph1[:, a_:b_, :], psP1[n % 2][:, :, :], ACT.Copy, scale=SP)
                        ins.then_inc(c_ph[n], 1)
                    return run

                def router_exp(t, par):
                    act.wait_ge(c_ls, t + 1)
                    act.activation(lex[:, par, :], lex[:, par, :], ACT.Exp, scale=1.0 / (SX * SW),
                                   accum_out=lsum[:, par, :]).then_inc(c_le, 1)
                steps = dict(high_in=high(0), high_out=high(1), exps0=exps(0), exps1=exps(1), router_exp=router_exp,
                             probs_high0=probs_high(0), probs_high1=probs_high(1), probs_high2=probs_high(2))
                in_order(act, steps, ACT_ORDER, T)

            @block.tensor
            def _(pe):
                def transposes(n):
                    def run(t, par):
                        pe.wait_ge(c_xn[n], t + 1)
                        wait(pe, c_xl[n], t)
                        wait(pe, c_xl[1 - n], before(t, *(("transposes_out", "transposes_in") if n else
                                                          ("transposes_in", "transposes_out")), PE_ORDER, T))
                        for k in range(KD):
                            last = pe.transpose(psXa[:, k, :], xn1[n][:, par, k * P:(k + 1) * P], ident[:])
                        last.then_inc(c_xt[n], 1)
                    return run

                def scores(half):
                    def run(t, par):
                        pe.wait_ge(c_xl[0], t + 1)
                        wait(pe, c_exp[half], t)
                        for q in (2 * half, 2 * half + 1):
                            for k in range(KD):
                                at = bass.ds((t // (S // P)) * (KD * CK) + (k * CK + q * QK), QK)
                                last = mm3(pe, psS1[:, q, 0:QK], xh1[0][:, par, k, :], xl1[0][:, par, k, :],
                                           M1hf[:, at], M1lf[:, at], k == 0, k == KD - 1)
                        last.then_inc(c_sc[half], 1)
                    return run

                def logits(t, par):
                    pe.wait_ge(c_xl[1], t + 1)
                    wait(pe, c_ls, t)
                    wait(pe, c_res, before(t, "logits", "outputs0", PE_ORDER, T))
                    for k in range(KD):
                        last = mm3(pe, psL1[:, 0:E], xh1[1][:, par, k, :], xl1[1][:, par, k, :], gth1[:, k, :], gtl1[:, k, :],
                                   k == 0, k == KD - 1)
                    last.then_inc(c_lg, 1)

                def turn(n):
                    def run(t, par):
                        pe.wait_ge(c_pn, t + 1)
                        a_, b_ = CH[n]
                        wait(pe, c_pl[(2, 1, 0)[n]], t + 1 if n == 2 else t)
                        for c in range(a_, b_):
                            cols = min(P, CK - c * P)
                            ins = pe.transpose(psP1[n % 2][0:cols, c - a_, :], pr1[:, par, c * P:c * P + cols], ident[:])
                        ins.then_inc(c_pt[n], 1)
                    return run

                def outputs(n):
                    def run(t, par):
                        a_, b_ = CH[n]
                        pe.wait_ge(c_pl[n], t + 1)
                        if n == 0:
                            wait(pe, c_res, t)
                            wait(pe, c_ls, before(t, "outputs0", "logits", PE_ORDER, T))
                        for c in range(a_, b_):
                            rows = min(P, CK - c * P)
                            at = (t // (S // P)) * (NC * 2 * D) + c * 2 * D
                            ins = mm3(pe, psO1, ph1[0:rows, c, :], pl1[0:rows, c, :], N1f[0:rows, bass.ds(at, D)],
                                      N1f[0:rows, bass.ds(at + D, D)], c == 0, c == NC - 1)
                        ins.then_inc(c_av[n], 1)
                    return run
                M1hf = M1h[:].rearrange("p b k c -> p (b k c)")
                M1lf = M1l[:].rearrange("p b k c -> p (b k c)")
                N1f = N1[:].rearrange("p b c d -> p (b c d)")
                steps = dict(transposes_in=transposes(0), transposes_out=transposes(1), scores0=scores(0), scores1=scores(1),
                             turn0=turn(0), turn1=turn(1), turn2=turn(2), logits=logits,
                             outputs0=outputs(0), outputs1=outputs(1), outputs2=outputs(2))
                in_order(pe, steps, PE_ORDER, T)

            @block.vector
            def _(dve):
                def combine(t, par):
                    row = X[:, bass.ds(t, 1), :].rearrange("p t d -> p (t d)")
                    dve.wait_ge(c_y[par], 32 * (t // 2) + 32)
                    for c in range(2):
                        dve.scalar_tensor_tensor(row, yg[:, par, c, :], wts[:, c, bass.ds(t, 1)], row, ALU.mult, ALU.add)\
                           .then_inc(c_comb, 1)
                        apart(dve, c_comb, 2 * t + (c + 1))
                    stats(0)(t, par)

                def stats(n):
                    def run(t, par):
                        row = X[:, bass.ds(t, 1), :].rearrange("p t d -> p (t d)")
                        dve.bn_stats(st1[n][:], row).then_inc(c_mv[n], 1)
                        apart(dve, c_mv[n], 2 * t + 1)
                        dve.bn_aggr(mv1[n][:, par, :], st1[n][:]).then_inc(c_mv[n], 1)
                    return run

                def normalise(n):
                    def run(t, par):
                        row = X[:, bass.ds(t, 1), :].rearrange("p t d -> p (t d)")
                        dve.wait_ge(c_rs[n], 2 * t + 2)
                        if n == 0:
                            wait(dve, c_xt[0], t - 1)
                        elif not isinstance(t, int) or t >= 2:
                            dve.wait_ge(c_out[par], 32 * (t // 2))
                            dve.wait_ge(c_xt[1], t - 1)
                        dve.tensor_scalar(xn1[n][:, par, :], row, mv1[n][:, par, 0:1], rs1[n][:, par, :],
                                          ALU.subtract, ALU.mult).then_inc(c_xn[n], 1)
                    return run

                def low(n):
                    def run(t, par):
                        dve.wait_ge(c_xh[n], t + 1)
                        dve.scalar_tensor_tensor(xl1[n][:, par, :, :], psXa[:], SX, xh1[n][:, par, :, :],
                                                 ALU.mult, ALU.subtract).then_inc(c_xl[n], 1)
                    return run

                def maxima(half):
                    def run(t, par):
                        dve.wait_ge(c_sc[half], t + 1)
                        wait(dve, c_exp[half], t)
                        m = mx1[:, half * HP:(half + 1) * HP]
                        dve.tensor_reduce(m.rearrange("p (q h) -> p q h", q=2),
                                          psS1[:, 2 * half:2 * half + 2, 0:QK].rearrange("p q (h k) -> p q h k", k=LK),
                                          AX.X, ALU.max).then_inc(c_mx, 1)
                        dve.wait_ge(c_mx, 2 * t + (half + 1))
                        dve.tensor_scalar(m, m, -1.0 / (SX * SM), None, ALU.mult).then_inc(c_sub[half], 1)
                    return run

                def reciprocals(t, par):
                    dve.wait_ge(c_exp[0], t + 1)
                    dve.wait_ge(c_exp[1], t + 1)
                    dve.reciprocal(sum1[:, par, :], sum1[:, par, :]).then_inc(c_rcp, 1)

                def probs_low(n):
                    def run(t, par):
                        a_, b_ = CH[n]
                        dve.wait_ge(c_ph[n], t + 1)
                        if b_ == NC:
                            dve.scalar_tensor_tensor(pl1[:, a_:b_ - 1, :], psP1[0][:, 0:b_ - a_ - 1, :], SP, ph1[:, a_:b_ - 1, :],
                                                     ALU.mult, ALU.subtract)
                            ins = dve.scalar_tensor_tensor(pl1[0:LASTC, b_ - 1, :], psP1[0][0:LASTC, b_ - a_ - 1, :], SP,
                                                           ph1[0:LASTC, b_ - 1, :], ALU.mult, ALU.subtract)
                        else:
                            ins = dve.scalar_tensor_tensor(pl1[:, a_:b_, :], psP1[n % 2][:, :, :], SP, ph1[:, a_:b_, :],
                                                           ALU.mult, ALU.subtract)
                        ins.then_inc(c_pl[n], 1)
                    return run

                def residual(t, par):
                    row = X[:, bass.ds(t, 1), :].rearrange("p t d -> p (t d)")
                    dve.wait_ge(c_av[2], t + 1)
                    dve.wait_ge(c_bo, t + 1)
                    dve.scalar_tensor_tensor(row, psO1, thx1[:, 0:1], row, ALU.mult, ALU.add).then_inc(c_res, 1)
                    apart(dve, c_res, t + 1)
                    stats(1)(t, par)

                def router_sub(t, par):
                    dve.wait_ge(c_lg, t + 1)
                    dve.tensor_reduce(lmx[:], psL1[:, 0:E], AX.X, ALU.max).then_inc(c_lm, 1)
                    dve.wait_ge(c_lm, t + 1)
                    dve.tensor_scalar(lex[:, par, :], psL1[:, 0:E], lmx[:, 0:1], None, ALU.subtract).then_inc(c_ls, 1)

                def router_norm(t, par):
                    dve.wait_ge(c_le, t + 1)
                    dve.reciprocal(lsum[:, par, :], lsum[:, par, :]).then_inc(c_aff, 1)
                    dve.wait_ge(c_aff, 2 * t + 1)
                    at = bass.ds((t % (S // P)) * (B * E) + (t // (S // P)) * E, E)
                    dve.tensor_scalar(afff[:, at], lex[:, par, :], lsum[:, par, :], None, ALU.mult).then_inc(c_aff, 1)
                afff = aff[:].rearrange("p t b e -> p (t b e)")
                dve.tensor_scalar(thx1[:], th[:, 1:2], 1.0 / (SP * SV), None, ALU.mult).then_inc(c_one, 1)
                dve.wait_ge(c_one, 1)
                steps = dict(probs_low0=probs_low(0), probs_low1=probs_low(1), probs_low2=probs_low(2), maxima0=maxima(0),
                             maxima1=maxima(1), normalise_in=normalise(0), normalise_out=normalise(1), low_in=low(0),
                             low_out=low(1), router_sub=router_sub, combine=combine, residual=residual,
                             reciprocals=reciprocals, router_norm=router_norm)
                in_order(dve, steps, DVE_ORDER, T)

        CAP = 2 * (S // E)
        SLT = CAP // P
        GSC = 1.0 / (SH * SW)
        k1 = ExitStack()
        at_ = sb("at_", [B * E, S], F32, k1)
        tv = sb("tv", [B * E, CAP], F32, k1)
        ti = sb("ti", [B * E, CAP], U32, k1)
        tif = sb("tif", [B * E, CAP], F32, k1)
        boff = sb("boff", [P, B * E], F32, k1)
        k1.close()
        pk = ExitStack()
        psA = ps("psA", [B * E, S], F32, pk)
        psV = ps("psV", [P, 2, SLT, B * E], F32, pk)
        pk.close()
        k_at = sem("k_at")
        k_dve = sem("k_dve")
        k_off = sem("k_off")
        k_ps = sem("k_ps")
        with nc.Block() as block:
            @block.gpsimd
            def _(pool):
                pool.iota(boff[:], [[S, B], [0, E]], base=0, channel_multiplier=0,
                          allow_small_or_imprecise_dtypes=True).then_inc(k_off, 1)

            @block.tensor
            def _(pe):
                for t in range(S // P):
                    last = pe.transpose(psA[:, t * P:(t + 1) * P], aff[:, t, :, :].rearrange("p b e -> p (b e)"), ident[:])
                last.then_inc(k_at, 1)
                pe.wait_ge(k_dve, 2 + 3 * (CAP // 8))
                for n in range(SLT):
                    cols = slice(n * P, (n + 1) * P)
                    pe.transpose(psV[:, 0, n, :], tv[:, cols], ident[0:B * E, 0:B * E])
                    last = pe.transpose(psV[:, 1, n, :], tif[:, cols], ident[0:B * E, 0:B * E])
                last.then_inc(k_ps, 1)

            @block.vector
            def _(dve):
                ch = Chain(dve, k_dve, 0, 2 + 3 * (CAP // 8))
                dve.wait_ge(k_at, 1)
                ch(dve.tensor_copy(at_[:], psA[:]))
                for r in range(CAP // 8):
                    cols = slice(8 * r, 8 * r + 8)
                    ch(dve.max(tv[:, cols], at_[:]))
                    ch(dve.max_index(ti[:, cols], tv[:, cols], at_[:]))
                    ch(dve.match_replace(at_[:], tv[:, cols], at_[:], -1.0))
                ch(dve.tensor_copy(tif[:], ti[:]))
                ch.end()
                dve.wait_ge(k_ps, 1)
                dve.wait_ge(k_off, 1)
                for n in range(SLT):
                    dve.tensor_tensor(gidx[:, n, :], psV[:, 1, n, :], boff[:], ALU.add)
                dve.tensor_scalar(gval[:], psV[:, 0, :, :], th[:, 3:4], GSC, ALU.mult, ALU.mult)

        FT1 = F1 // P
        BS = 2 * CAP
        NT = BS // P
        NB1 = E * B // 2
        W1E = 2 * KD * F1 + FT1 * D
        UP1, DOWN1 = KD * F1, 2 * KD * F1
        l1.close()
        f1 = ExitStack()
        W1h = sb("W1h", [P, 2, W1E], F16, f1)
        W1l = sb("W1l", [P, 2, W1E], F16, f1)
        w1s = sb("w1s", [P, 2, W1E // 2], F32, f1)
        gx = sb("gx", [P, 2, NT, D], F32, f1)
        gxh = sb("gxh", [P, 2, KD, BS], F16, f1)
        gxl = sb("gxl", [P, 2, KD, BS], F16, f1)
        sil1 = sb("sil1", [P, 2, BS], F32, f1)
        hid1 = sb("hid1", [P, 2, BS], F32, f1)
        hh1 = sb("hh1", [P, 2, FT1, BS], F16, f1)
        hl1 = sb("hl1", [P, 2, FT1, BS], F16, f1)
        yo1 = sb("yo1", [P, 2, NT, D], F32, f1)
        f1.close()
        pf = ExitStack()
        psXb = ps("psXb", [P, KD, BS], F32, pf)
        psG1 = [ps(f"psG1{n}", [P, BS], F32, pf) for n in range(2)]
        psU1 = [ps(f"psU1{n}", [P, BS], F32, pf) for n in range(2)]
        psYb = ps("psYb", [P, NT, D], F32, pf)
        pf.close()
        d_w = [sem(f"d_w{n}") for n in range(2)]
        d_wh = sem("d_wh")
        d_wl = sem("d_wl")
        d_in = [sem(f"d_in{n}") for n in range(2)]
        d_xt = sem("d_xt")
        d_xh = sem("d_xh")
        d_xl = sem("d_xl")
        d_g = sem("d_g")
        d_sil = sem("d_sil")
        d_hid = sem("d_hid")
        d_hh = sem("d_hh")
        d_hl = sem("d_hl")
        d_y = sem("d_y")
        d_yo = sem("d_yo")
        d_out = [sem(f"d_out{n}") for n in range(2)]
        DD = 4

        with nc.Block() as block:
            @block.sync
            def _(sp):
                def load(j, ph):
                    half = ph % 2
                    wait(sp, d_wl, j - 1)
                    src = a["w1"][bass.ds(j // 2, 1)].rearrange("e p w -> p (e w)") if not isinstance(j, int) else a["w1"][j // 2]
                    sp.dma_start(w1s[:, half, :], src[:, half * (W1E // 2):(half + 1) * (W1E // 2)]).then_inc(d_w[half], 16)
                pipeline(sp, NB1, 1, [(0, load)], unroll=2)

            @block.gpsimd
            def _(pool):
                def column(j, n):
                    e, q = j // 2, j % 2
                    return n % SLT, (2 * q + n // SLT) * E + e

                def gather(j, ph):
                    wait(pool, d_xt, j - 1)
                    for n in range(NT):
                        half, col = column(j, n)
                        pool.indirect_dma_start(gx[:, j % 2, n, :], None, n_rows[:, :],
                                                bass.IndirectOffsetOnAxis(gidx[:, half, col:col + 1], 0)).then_inc(d_in[j % 2], 16)

                def add(j, ph):
                    pool.wait_ge(d_yo, NT * j + NT)
                    wait(pool, d_out[j % 2], 16 * NT * (j // 2))
                    for n in range(NT):
                        half, col = column(j, n)
                        pool.indirect_dma_start(out_rows[:, :], bass.IndirectOffsetOnAxis(gidx[:, half, col:col + 1], 0),
                                                yo1[:, j % 2, n, :], None, compute_op=ALU.add).then_inc(d_out[j % 2], 16)
                pipeline(pool, NB1, DD, [(0, gather), (3, add)], straight=True)
                for n in range(2):
                    pool.wait_ge(d_out[n], 16 * NT * NB1 // 2)

            @block.tensor
            def _(pe):
                def transposes(j, ph):
                    par = ph % 2
                    pe.wait_ge(d_in[par], 16 * NT * (j // 2) + 16 * NT)
                    wait(pe, d_xl, KD * j)
                    for k in range(KD):
                        for n in range(NT):
                            last = pe.transpose(psXb[:, k, n * P:(n + 1) * P], gx[:, par, n, k * P:(k + 1) * P], ident[:])
                    last.then_inc(d_xt, 1)

                def up(j, ph):
                    par, wp = ph % 2, ph // 2
                    pe.wait_ge(d_xl, KD * j + KD)
                    pe.wait_ge(d_wl, 2 * (j // 2) + 2)
                    for f in range(FT1):
                        wait(pe, d_hid, FT1 * j + (f - 1))
                        for psum, off in ((psG1, 0), (psU1, UP1)):
                            for k in range(KD):
                                at = off + k * F1 + f * P
                                last = mm3(pe, psum[f % 2][:], W1h[:, wp, at:at + P], W1l[:, wp, at:at + P], gxh[:, par, k, :],
                                           gxl[:, par, k, :], k == 0, k == KD - 1)
                        last.then_inc(d_g, 1)

                def down(j, ph):
                    par, wp = ph % 2, ph // 2
                    pe.wait_ge(d_hl, FT1 * j + FT1)
                    wait(pe, d_yo, NT * j)
                    for n in range(NT):
                        rows = slice(n * P, (n + 1) * P)
                        for f in range(FT1):
                            at = DOWN1 + f * D
                            last = mm3(pe, psYb[:, n, :], hh1[:, par, f, rows], hl1[:, par, f, rows], W1h[:, wp, at:at + D],
                                       W1l[:, wp, at:at + D], f == 0, f == FT1 - 1)
                    last.then_inc(d_y, 1)
                pipeline(pe, NB1, DD, [(2, up), (1, transposes), (3, down)], unroll=4)

            @block.scalar
            def _(act):
                def weights_high(j, ph):
                    half, wp = ph % 2, ph // 2
                    act.wait_ge(d_w[half], 16 * (j // 2) + 16)
                    wait(act, d_y, j - 3)
                    act.activation(W1h[:, wp, half * (W1E // 2):(half + 1) * (W1E // 2)], w1s[:, half, :], ACT.Copy, scale=SW)\
                       .then_inc(d_wh, 1)

                def rows_high(j, ph):
                    par = ph % 2
                    act.wait_ge(d_xt, j + 1)
                    wait(act, d_g, FT1 * (j - 1))
                    for k in range(KD):
                        act.activation(gxh[:, par, k, :], psXb[:, k, :], ACT.Copy, scale=SX).then_inc(d_xh, 1)

                def silu(j, ph):
                    for f in range(FT1):
                        act.wait_ge(d_g, FT1 * j + (f + 1))
                        wait(act, d_hid, FT1 * j + (f - 1))
                        act.activation(sil1[:, f % 2, :], psG1[f % 2][:], ACT.Silu, scale=1.0 / (SX * SW)).then_inc(d_sil, 1)

                def results(j, ph):
                    par = ph % 2
                    act.wait_ge(d_y, j + 1)
                    if not isinstance(j, int) or j >= 2:
                        act.wait_ge(d_out[par], 16 * NT * (j // 2))
                    for n in range(NT):
                        col = bass.ds((n % SLT) * (B * E) + ((2 * par + n // SLT) * E) + j // 2, 1)
                        act.activation(yo1[:, par, n, :], psYb[:, n, :], ACT.Copy, scale=gvalf[:, col]).then_inc(d_yo, 1)
                gvalf = gval[:].rearrange("p n c -> p (n c)")
                pipeline(act, NB1, DD, [(0, weights_high), (2, silu), (1, rows_high), (3, results)], unroll=4)

            @block.vector
            def _(dve):
                def weights_low(j, ph):
                    half, wp = ph % 2, ph // 2
                    cols = slice(half * (W1E // 2), (half + 1) * (W1E // 2))
                    dve.wait_ge(d_wh, j + 1)
                    dve.scalar_tensor_tensor(W1l[:, wp, cols], w1s[:, half, :], SW, W1h[:, wp, cols], ALU.mult, ALU.subtract)\
                       .then_inc(d_wl, 1)

                def rows_low(j, ph):
                    par = ph % 2
                    for k in range(KD):
                        dve.wait_ge(d_xh, KD * j + (k + 1))
                        dve.scalar_tensor_tensor(gxl[:, par, k, :], psXb[:, k, :], SX, gxh[:, par, k, :],
                                                 ALU.mult, ALU.subtract).then_inc(d_xl, 1)

                def hidden(j, ph):
                    par = ph % 2
                    wait(dve, d_y, j - 1)
                    for f in range(FT1):
                        dve.wait_ge(d_sil, FT1 * j + (f + 1))
                        dve.scalar_tensor_tensor(hid1[:, f % 2, :], psU1[f % 2][:], SH / (SX * SW), sil1[:, f % 2, :],
                                                 ALU.mult, ALU.mult).then_inc(d_hid, 1)
                        dve.wait_ge(d_hid, FT1 * j + (f + 1))
                        dve.tensor_copy(hh1[:, par, f, :], hid1[:, f % 2, :]).then_inc(d_hh, 1)
                        dve.wait_ge(d_hh, FT1 * j + (f + 1))
                        dve.tensor_tensor(hl1[:, par, f, :], hid1[:, f % 2, :], hh1[:, par, f, :], ALU.subtract)\
                           .then_inc(d_hl, 1)
                pipeline(dve, NB1, DD, [(0, weights_low), (2, hidden), (1, rows_low)], unroll=4)


_SINGLE = {}


def kernel(**inputs):
    import numpy as np
    import concourse.bacc as bacc
    from concourse.bass_utils import run_bass_kernel_spmd

    def tiles(w, n):
        return w.reshape(n, P, -1).transpose(1, 0, 2)

    def experts(wa, wb, wd, f):
        e = wa.shape[0]
        up = [w.transpose(0, 2, 1).reshape(e, KD, P, f).transpose(0, 2, 1, 3).reshape(e, P, KD * f) for w in (wa, wb)]
        down = wd.transpose(0, 2, 1).reshape(e, f // P, P, D).transpose(0, 2, 1, 3).reshape(e, P, (f // P) * D)
        return np.concatenate(up + [down], axis=2)

    i = {k: np.asarray(v) for k, v in inputs.items()}
    arrays = {
        "x": i["x"],
        "ctxT": i["ctx_768"].reshape(NKEY, DC).T,
        "g_xattn": i["g_xattn"].reshape(1, 2),
        "g_ffn": i["g_ffn"].reshape(1, 2),
        "wk0": i["L0_xattn_Wk"],
        "wv0": i["L0_xattn_Wv"],
        "wqT0": i["L0_xattn_Wq"].T,
        "bq0": i["L0_xattn_bq"].reshape(KD, P).T,
        "bk0": i["L0_xattn_bk"].reshape(KD, P).T,
        "bv0": i["L0_xattn_bv"].reshape(1, D),
        "gate0": tiles(i["L0_ffn_gate_w"].T, KD),
        "wk1": i["L1_xattn_Wk"],
        "wv1": i["L1_xattn_Wv"],
        "wqT1": i["L1_xattn_Wq"].T,
        "wo1": i["L1_xattn_Wo"],
        "bo1": i["L1_xattn_bo"].reshape(1, D),
        "gate1": tiles(i["L1_ffn_gate_w"].T, KD),
        "w1": experts(i["L1_ffn_w_gate"], i["L1_ffn_w_up"], i["L1_ffn_w_down"], F1),
        "w0": experts(i["L0_ffn_w1"], i["L0_ffn_w3"], i["L0_ffn_w2"], F0),
    }
    arrays = {k: np.ascontiguousarray(v) for k, v in arrays.items()}
    nc = bacc.Bacc("TRN2", target_bir_lowering=False, num_devices=1)
    aps = {k: nc.dram_tensor("in_" + k, v.shape, F32, kind="ExternalInput").ap() for k, v in arrays.items()}
    out = nc.dram_tensor("out_x", (B, S, D), F32, kind="ExternalOutput").ap()
    x_rows = nc.dram_tensor("x_rows", ((E + 1) * REG, D), F32, kind="Internal").ap()
    y_rows = nc.dram_tensor("y_rows", (NB0 * BR, D), F32, kind="Internal").ap()
    n_rows = nc.dram_tensor("n_rows", (B * S, D), F32, kind="Internal").ap()
    program(nc, aps, out, x_rows, y_rows, n_rows)
    r = run_bass_kernel_spmd(nc, [{"in_" + k: v for k, v in arrays.items()}], core_ids=[0])
    return r.results[0]["out_x"]
```

```python
from contextlib import ExitStack

import concourse.bass as bass
from concourse import mybir

F32 = mybir.dt.float32
F16 = mybir.dt.float16
BF16 = mybir.dt.bfloat16
I32 = mybir.dt.int32
U32 = mybir.dt.uint32
ALU = mybir.AluOpType
ACT = mybir.ActivationFunctionType
AX = mybir.AxisListType

P = 128
B, S, D = 4, 1024, 256
LK, DC = 77, 192
NKEY = B * LK
T = B * S // P
KD = D // P
E = 8
F0 = 512
F1 = 1024
GT = 4
NG = T // GT
EPS = 1e-5

SX = 256.0
SW = 256.0
SM = 64.0
SV = 64.0
SP = 256.0
SH = 16.0

BR = 256
REG = B * S + BR
NB0 = (2 * B * S + E * (BR - 1)) // BR
W0E = 2 * KD * F0 + (F0 // P) * D


def wait(e, sem, value):
    if not isinstance(value, int) or value > 0:
        e.wait_ge(sem, value)


class Chain:

    def __init__(self, engine, sem, turn, steps):
        self.engine, self.sem, self.base, self.steps, self.n = engine, sem, turn * steps, steps, 0

    def __call__(self, ins):
        self.n += 1
        ins.then_inc(self.sem, 1)
        self.engine.wait_ge(self.sem, self.base + self.n)

    def end(self):
        assert self.n == self.steps, (self.n, self.steps)


def pipeline(e, n, depth, work, unroll=2, straight=False):
    def step(j, phase):
        for lag, fn in work:
            item = j - lag
            if isinstance(item, int) and not 0 <= item < n:
                continue
            fn(item, (phase - lag) % unroll)

    first = depth + 1
    turns = (n - first) // unroll
    if turns < 2 or straight:
        turns = 0
    for j in range(min(first, n + depth - 1)):
        step(j, j % unroll)
    if turns:
        with e.Fori(0, turns) as u:
            for c in range(unroll):
                step(u * unroll + (first + c), (first + c) % unroll)
    for j in range(first + turns * unroll, n + depth - 1):
        step(j, j % unroll)


def mm3(pe, o, lh, ll, rh, rl, first, stop):
    pe.matmul(o, lh, rh, start=first, stop=False)
    pe.matmul(o, lh, rl, start=False, stop=False)
    return pe.matmul(o, ll, rh, start=False, stop=stop)


def least(a, limit):
    return min(a, limit) if isinstance(a, int) else a


def in_order(e, steps, order, n, straight=False):
    pipeline(e, n, max(lag for _, lag in order) + 1, [(lag, steps[name]) for name, lag in order], straight=straight)


def before(item, mine, other, order, n):
    names = [name for name, _ in order]
    ahead = dict(order)[mine] - dict(order)[other] + (names.index(other) < names.index(mine))
    return least(item + ahead, n)


def program(nc, a, out, x_rows, y_rows, n_rows):
    ctx = ExitStack()
    with ctx:
        def sb(name, shape, dt=F32, on=ctx, side=None):
            return on.enter_context(nc.sbuf_tensor(name, shape, dt, side=side))

        def ps(name, shape, dt=F32, on=ctx):
            return on.enter_context(nc.psum_tensor(name, shape, dt))

        def sem(name):
            return ctx.enter_context(nc.semaphore(name))

        X = sb("X", [P, T, D])
        ident = sb("ident", [P, P])
        th = sb("th", [P, 4])
        wts = sb("wts", [P, 2, T])
        islot = sb("islot", [P, 2, T], I32)
        aff = sb("aff", [P, S // P // 2, 2, B, E])
        gval = sb("gval", [P, 2 * S // E // P, B * E])
        gidx = sb("gidx", [P, 2 * S // E // P, B * E], I32)
        mhalf = sb("mhalf", [P, GT])

        l0 = ExitStack()
        Wh = sb("Wh", [P, E * W0E], F16, l0)
        Wl = sb("Wl", [P, E * W0E], F16, l0)
        blkrow = sb("blkrow", [P, NB0], I32, l0)
        blkw = sb("blkw", [P, NB0], I32, l0)
        padrow = sb("padrow", [P, E], I32, l0)
        a0 = ExitStack()
        stage = sb("stage", [P, 2, W0E], F32, a0)
        ctxT = stage[:, 0, 0:2 * NKEY].rearrange("p (k n) -> p k n", k=2)
        wk = stage[:, 0, 1024:1536].rearrange("p (k n) -> p k n", k=2)
        wv = stage[:, 0, 1536:2048].rearrange("p (k n) -> p k n", k=2)
        wqT = stage[:, 0, 2048:2560].rearrange("p (k n) -> p k n", k=2)
        KT = stage[:, 1, 0:2 * NKEY].rearrange("p (k n) -> p k n", k=2)
        bqs = sb("bqs", [P, KD], F32, a0)
        bks = sb("bks", [P, KD], F32, a0)
        bvs = sb("bvs", [1, D], F32, a0)
        gts = sb("gts", [P, KD, E], F32, a0)
        gth = sb("gth", [P, KD, E], F16, a0)
        gtl = sb("gtl", [P, KD, E], F16, a0)
        Mh = sb("Mh", [P, KD, NKEY], F16, a0)
        Ml = sb("Ml", [P, KD, NKEY], F16, a0)
        c0 = sb("c0", [1, NKEY], F32, a0)
        Vh = sb("Vh", [LK, B, D], F16, a0)
        Vl = sb("Vl", [LK, B, D], F16, a0)
        ones1 = sb("ones1", [1, P], F32, a0)
        trib = sb("trib", [P, P], BF16, a0)
        onesb = sb("onesb", [P, P], BF16, a0)
        iota8 = sb("iota8", [P, E], F32, a0)
        reg8 = sb("reg8", [P, E], F32, a0)
        thr = sb("thr", [P, E, 16], F32, a0)
        tri8 = sb("tri8", [P, E, E], F32, a0)
        iotaj = sb("iotaj", [P, NB0], F32, a0)
        base = sb("base", [P, E], F32, a0)
        st = [sb(f"st{n}", [P, GT, 6], F32, a0) for n in range(2)]
        mv = [sb(f"mv{n}", [P, 2, GT, 2], F32, a0) for n in range(2)]
        rstd = [sb(f"rstd{n}", [P, 2, GT], F32, a0) for n in range(2)]
        xa = sb("xa", [P, GT, D], F32, a0)
        xc = sb("xc", [P, 2, GT, D], F32, a0)
        xth = [sb(f"xth{n}", [P, 2, KD, GT * P], F16, a0) for n in range(2)]
        xtl = [sb(f"xtl{n}", [P, 2, KD, GT * P], F16, a0) for n in range(2)]
        smax = sb("smax", [P, GT], F32, a0)
        pr = sb("pr", [P, 2, GT, LK], F32, a0)
        ssum = sb("ssum", [P, GT], F32, a0)
        cf = sb("cf", [P, 2, GT], F32, a0)
        pth = sb("pth", [LK, GT * P], F16, a0)
        ptl = sb("ptl", [LK, GT * P], F16, a0)
        lg = sb("lg", [P, GT, E], F32, a0)
        top = sb("top", [P, T, E], F32, a0)
        ix = sb("ix", [P, GT, E], U32, a0)
        ixf = sb("ixf", [P, GT, E], F32, a0)
        pick = sb("pick", [P, 2, T, E], F32, a0)
        mx = sb("mx", [P, GT, E], F32, a0)
        both = sb("both", [P, GT, E], BF16, a0)
        rank = sb("rank", [P, T, E], F32, a0)
        prod = sb("prod", [P, 2, GT, E], F32, a0)
        slotf = sb("slotf", [P, 2, GT], F32, a0)
        slots = sb("slots", [P, 2, 2, GT], I32, a0)
        cnt = sb("cnt", [P, E], F32, a0)
        more = sb("more", [P, E, 16], F32, a0)
        nblk = sb("nblk", [P, E], F32, a0)
        tri8n = sb("tri8n", [P, E, E], F32, a0)
        cum = sb("cum", [P, E], F32, a0)
        adj = sb("adj", [P, E], F32, a0)
        done = sb("done", [P, NB0, E], F32, a0)
        done2 = sb("done2", [P, NB0, E], F32, a0)
        ej = sb("ej", [P, NB0], F32, a0)
        mj = sb("mj", [P, NB0], F32, a0)
        lt = sb("lt", [P, NB0], F32, a0)
        slotT = sb("slotT", [P, 2, T], F32, a0)

        pa = ExitStack()
        psT = ps("psT", [P, KD, GT * P], F32, pa)
        psS = ps("psS", [P, 512], F32, pa)
        psP = ps("psP", [P, GT * P], F32, pa)
        psO = ps("psO", [P, GT, D], F32, pa)
        psL = ps("psL", [P, 512], F32, pa)
        psR = ps("psR", [P, 512], F32, pa)
        pa.close()

        s_x = [sem(f"s_x{g}") for g in range(NG)]
        s_w = sem("s_w")
        s_setpe = sem("s_setpe")
        s_setact = sem("s_setact")
        s_pc = sem("s_pc")
        out_rows = out.rearrange("b s d -> (b s) d")
        xv = a["x"].rearrange("b (t p) d -> p (b t) d", p=P)
        with nc.Block() as block:
            @block.sync
            def _(sp):
                sp.dma_start(ctxT[:, 0, :], a["ctxT"][0:P, :]).then_inc(s_w, 16)
                sp.dma_start(ctxT[0:DC - P, 1, :], a["ctxT"][P:DC, :]).then_inc(s_w, 16)
                for dst, name in ((wk, "wk0"), (wv, "wv0")):
                    sp.dma_start(dst[:, 0, :], a[name][0:P, :]).then_inc(s_w, 16)
                    sp.dma_start(dst[0:DC - P, 1, :], a[name][P:DC, :]).then_inc(s_w, 16)
                sp.dma_start(wqT, a["wqT0"].rearrange("(k p) d -> p k d", p=P)).then_inc(s_w, 16)
                sp.dma_start(bqs[:], a["bq0"]).then_inc(s_w, 16)
                sp.dma_start(bks[:], a["bk0"]).then_inc(s_w, 16)
                sp.dma_start(bvs[:], a["bv0"]).then_inc(s_w, 16)
                sp.dma_start(gts[:], a["gate0"]).then_inc(s_w, 16)
                sp.dma_start(th[:, 0:2], a["g_xattn"].partition_broadcast(P)).then_inc(s_w, 16)
                sp.dma_start(th[:, 2:4], a["g_ffn"].partition_broadcast(P)).then_inc(s_w, 16)
                for g in range(NG):
                    sp.dma_start(X[:, GT * g:GT * g + GT, :], xv[:, GT * g:GT * g + GT, :]).then_inc(s_x[g], 16)

            W_ALL = 13 * 16

            @block.gpsimd
            def _(pool):
                ch = Chain(pool, s_pc, 0, 9)
                ch(pool.memset(ident[:], 0.0))
                ch(pool.affine_select(out=ident[:], in_=ident[:], compare_op=ALU.not_equal, fill=1.0,
                                      base=0, pattern=[[-1, P]], channel_multiplier=1))
                pool.memset(ones1[:], 1.0)
                pool.memset(mhalf[:], -0.5)
                ch(pool.memset(onesb[:], 1.0))
                ch(pool.affine_select(out=trib[:], in_=onesb[:], compare_op=ALU.is_gt, fill=0.0,
                                      base=0, pattern=[[1, P]], channel_multiplier=-1))
                ch(pool.memset(tri8[:], 1.0))
                ch(pool.affine_select(out=tri8[:], in_=tri8[:], compare_op=ALU.is_ge, fill=0.0,
                                      base=0, pattern=[[1, E], [-1, E]], channel_multiplier=0))
                pool.iota(iota8[:], [[1, E]], base=0, channel_multiplier=0, allow_small_or_imprecise_dtypes=True)
                pool.iota(reg8[:], [[REG, E]], base=0, channel_multiplier=0, allow_small_or_imprecise_dtypes=True)
                ch(pool.iota(base[:], [[REG, E]], base=0, channel_multiplier=0, allow_small_or_imprecise_dtypes=True))
                ch(pool.iota(thr[:], [[0, E], [BR, 16]], base=0, channel_multiplier=0,
                             allow_small_or_imprecise_dtypes=True))
                ch(pool.iota(iotaj[:], [[1, NB0]], base=0, channel_multiplier=0, allow_small_or_imprecise_dtypes=True))
                ch.end()

            @block.tensor
            def _(pe):
                pe.wait_ge(s_w, W_ALL)
                pe.wait_ge(s_pc, 9)
                for m in range(KD):
                    pe.matmul(psT[:, m, 0:NKEY], wk[:, 0, m * P:(m + 1) * P], ctxT[:, 0, :], start=True, stop=False)
                    pe.matmul(psT[:, m, 0:NKEY], wk[0:DC - P, 1, m * P:(m + 1) * P], ctxT[0:DC - P, 1, :],
                              start=False, stop=True).then_inc(s_setpe, 1)
                for b in range(B):
                    o = psO[0:LK, b, :]
                    pe.matmul(o, ctxT[:, 0, b * LK:(b + 1) * LK], wv[:, 0, :], start=True, stop=False)
                    pe.matmul(o, ctxT[0:DC - P, 1, b * LK:(b + 1) * LK], wv[0:DC - P, 1, :], start=False, stop=False)
                    pe.matmul(o, ones1[0:1, 0:LK], bvs[:], start=False, stop=True).then_inc(s_setpe, 1)
                pe.wait_ge(s_setact, 2)
                for m in range(KD):
                    o = (psS, psP)[m][:, 0:NKEY]
                    for k in range(KD):
                        last = pe.matmul(o, wqT[:, k, m * P:(m + 1) * P], KT[:, k, :], start=(k == 0), stop=(k == KD - 1))
                    last.then_inc(s_setpe, 1)
                for k in range(KD):
                    last = pe.matmul(psL[0:1, 0:NKEY], bqs[:, k:k + 1], KT[:, k, :], start=(k == 0), stop=(k == KD - 1))
                last.then_inc(s_setpe, 1)

            @block.scalar
            def _(act):
                for m in range(KD):
                    act.wait_ge(s_setpe, m + 1)
                    act.activation(KT[:, m, :], psT[:, m, 0:NKEY], ACT.Identity, bias=bks[:, m:m + 1]).then_inc(s_setact, 1)
                for b in range(B):
                    act.wait_ge(s_setpe, 4 + b // 2 * 2)
                    act.activation(Vh[:, b, :], psO[0:LK, b, :], ACT.Copy, scale=SV).then_inc(s_setact, 1)
                for m in range(KD):
                    act.wait_ge(s_setpe, 7 + m)
                    act.activation(Mh[:, m, :], (psS, psP)[m][:, 0:NKEY], ACT.Copy, scale=SM).then_inc(s_setact, 1)
                act.wait_ge(s_setpe, 9)
                act.activation(c0[:], psL[0:1, 0:NKEY], ACT.Copy, scale=SX * SM).then_inc(s_setact, 1)
                act.activation(gth[:], gts[:], ACT.Copy, scale=SW).then_inc(s_setact, 1)
                act.activation(th[:], th[:], ACT.Tanh).then_inc(s_setact, 1)

            @block.vector
            def _(dve):
                for b in range(B):
                    dve.wait_ge(s_setact, 4 + b // 2 * 2)
                    dve.scalar_tensor_tensor(Vl[:, b, :], psO[0:LK, b, :], SV, Vh[:, b, :], ALU.mult, ALU.subtract)
                for m in range(KD):
                    dve.wait_ge(s_setact, 7 + m)
                    dve.scalar_tensor_tensor(Ml[:, m, :], (psS, psP)[m][:, 0:NKEY], SM, Mh[:, m, :],
                                             ALU.mult, ALU.subtract)
                dve.wait_ge(s_setact, 10)
                dve.scalar_tensor_tensor(gtl[:], gts[:], SW, gth[:], ALU.mult, ALU.subtract)

        s_ws = [sem(f"s_ws{n}") for n in range(2)]
        s_we = sem("s_we")
        s_wh = sem("s_wh")
        s_wl = sem("s_wl")
        s_wp = sem("s_wp")
        s_st = [sem(f"s_st{n}") for n in range(2)]
        s_mv = [sem(f"s_mv{n}") for n in range(2)]
        s_rstd = [sem(f"s_rstd{n}") for n in range(2)]
        s_xn = [sem(f"s_xn{n}") for n in range(2)]
        s_xt = [sem(f"s_xt{n}") for n in range(2)]
        s_xh = [sem(f"s_xh{n}") for n in range(2)]
        s_xl = [sem(f"s_xl{n}") for n in range(2)]
        s_sc = sem("s_sc")
        s_smax = sem("s_smax")
        s_sub = sem("s_sub")
        s_exp = sem("s_exp")
        s_cf = sem("s_cf")
        s_pt = sem("s_pt")
        s_pth = sem("s_pth")
        s_ptl = sem("s_ptl")
        s_av = sem("s_av")
        s_res = sem("s_res")
        s_lg = sem("s_lg")
        s_route = sem("s_route")
        s_both = sem("s_both")
        s_rk = sem("s_rk")
        s_slot = sem("s_slot")
        s_sct = [sem(f"s_sct{n}") for n in range(2)]
        s_zero = sem("s_zero")
        s_fin = sem("s_fin")
        s_blk = sem("s_blk")
        s_fin2 = sem("s_fin2")
        s_pad = sem("s_pad")
        ROUTE = 10
        HW = W0E // 2
        PE0_ORDER = [("transpose_probs", 2), ("logits", 4), ("ranks", 4), ("transposes_out", 3), ("scores", 1), ("attend", 2),
                     ("transposes_in", 0)]
        ACT0_ORDER = [("high_out", 3), ("exps", 1), ("high_in", 0), ("probs_high", 1), ("weights_high", 3)]
        DVE0_ORDER = [("softmax", 2), ("residual", 3), ("stats_in", 0), ("stats_out", 3), ("choose", 4), ("low_in", 1),
                      ("place", 4), ("normalise_out", 3), ("weights_low", 5), ("probs_low", 2), ("denominators", 2),
                      ("normalise_in", 0), ("low_out", 3)]
        POOL0_ORDER = [("rstd_out", 4), ("rstd_in", 1), ("scatter", 5), ("weights_low", 5)]
        prodT = xa[:, 2:4, :].rearrange("p a (t e) -> p a t e", e=E)

        with nc.Block() as block:
            @block.sync
            def _(sp):
                def load_weights(g, par):
                    wait(sp, s_wl, g - 1)
                    wait(sp, s_wp, g - 1)
                    sp.dma_start(stage[:, par, :], a["w0"][g]).then_inc(s_ws[par], 16)
                for g in range(E):
                    load_weights(g, g % 2)
                sp.wait_ge(s_zero, 1)
                sp.wait_ge(s_blk, 1)
                zeros = xa[:, 0:2, :]
                for e in range(E):
                    row = sp.value_load(padrow[0:1, e:e + 1], min_val=0, max_val=E * REG - BR)
                    sp.dma_start(x_rows[bass.ds(row, BR), :].rearrange("(n p) d -> p n d", p=P), zeros).then_inc(s_pad, 16)
                sp.dma_start(x_rows[E * REG:E * REG + BR, :].rearrange("(n p) d -> p n d", p=P), zeros).then_inc(s_pad, 16)
                sp.wait_ge(s_pad, 16 * (E + 1))

            @block.gpsimd
            def _(pool):
                def rstd_of(n):
                    def run(g, par):
                        pool.wait_ge(s_mv[n], GT * g + GT)
                        pool.tensor_scalar(rstd[n][:, par, :], mv[n][:, par, :, 1], EPS, None, ALU.add).then_inc(s_rstd[n], 1)
                        pool.wait_ge(s_rstd[n], 2 * g + 1)
                        pool.tensor_tensor(rstd[n][:, par, :], rstd[n][:, par, :], mhalf[:], ALU.pow).then_inc(s_rstd[n], 1)
                    return run

                def weights_low(g, par):
                    pool.wait_ge(s_wh, g + 1)
                    pool.tensor_tensor(Wl[:, bass.ds(g * W0E + HW, HW)], stage[:, par, HW:], Wh[:, bass.ds(g * W0E + HW, HW)],
                                       ALU.subtract).then_inc(s_wp, 1)

                def scatter(g, par):
                    pool.wait_ge(s_slot, g + 1)
                    for k in range(GT):
                        for c in range(2):
                            pool.indirect_dma_start(x_rows[:, :], bass.IndirectOffsetOnAxis(slots[:, par, c, k:k + 1], 0),
                                                    xc[:, par, k, :], None, bounds_check=E * REG - 1,
                                                    oob_is_err=True).then_inc(s_sct[par], 16)
                steps = dict(rstd_out=rstd_of(1), rstd_in=rstd_of(0), weights_low=weights_low, scatter=scatter)
                in_order(pool, steps, POOL0_ORDER, NG, straight=True)
                for n in range(2):
                    pool.wait_ge(s_sct[n], 16 * T)
                pool.memset(xa[:, 0:2, :], 0.0).then_inc(s_zero, 1)

            @block.scalar
            def _(act):
                def high(n):
                    def run(g, par):
                        wait(act, s_lg if n else s_sc, g - 1)
                        for k in range(KD):
                            act.wait_ge(s_xt[n], KD * g + k + 1)
                            act.activation(xth[n][:, par, k, :], psT[:, k, :], ACT.Copy, scale=SX).then_inc(s_xh[n], 1)
                    return run

                def weights_high(g, par):
                    act.wait_ge(s_ws[par], 16 * (g // 2) + 16)
                    act.activation(stage[:, par, :], stage[:, par, :], ACT.Copy, scale=SW).then_inc(s_we, 1)
                    act.wait_ge(s_we, g + 1)
                    act.activation(Wh[:, bass.ds(g * W0E, W0E)], stage[:, par, :], ACT.Copy).then_inc(s_wh, 1)

                def exps(g, par):
                    act.wait_ge(s_sub, g + 1)
                    act.activation(pr[:, par, :, :], pr[:, par, :, :], ACT.Exp, scale=1.0 / (SX * SM)).then_inc(s_exp, 1)

                def probs_high(g, par):
                    wait(act, s_av, g)
                    act.wait_ge(s_pt, g + 1)
                    act.activation(pth[:], psP[0:LK, :], ACT.Copy, scale=SP).then_inc(s_pth, 1)

                steps = dict(high_in=high(0), high_out=high(1), exps=exps, probs_high=probs_high, weights_high=weights_high)
                in_order(act, steps, ACT0_ORDER, NG, straight=True)
                act.wait_ge(s_fin, 1)
                act.activation(wts[:, 1, :], wts[:, 0, :], ACT.Exp, scale=1.0 / (SX * SW)).then_inc(s_fin, 1)

            @block.tensor
            def _(pe):
                def transposes(n):
                    def run(g, par):
                        pe.wait_ge(s_xn[n], GT * g + GT)
                        src = xa[:, :, :] if n == 0 else xc[:, par, :, :]
                        for k in range(KD):
                            mine, other = (("transposes_in", "transposes_out"), ("transposes_out", "transposes_in"))[n]
                            if g > 0:
                                pe.wait_ge(s_xl[n], KD * (g - 1) + k + 1)
                            begun = before(g, mine, other, PE0_ORDER, NG)
                            if begun > 0:
                                pe.wait_ge(s_xl[1 - n], KD * (begun - 1) + k + 1)
                            for i in range(GT):
                                last = pe.transpose(psT[:, k, i * P:(i + 1) * P], src[:, i, k * P:(k + 1) * P], ident[:])
                            last.then_inc(s_xt[n], 1)
                    return run

                def scores(g, par):
                    pe.wait_ge(s_xl[0], KD * g + KD)
                    wait(pe, s_sub, g)
                    b = g // 2
                    for i in range(GT):
                        o = psS[:, i * LK:(i + 1) * LK]
                        t = slice(i * P, (i + 1) * P)
                        keys = bass.ds(b * LK, LK)
                        pe.matmul(o, ones1[:], c0[:, keys], start=True, stop=False)
                        for k in range(KD):
                            last = mm3(pe, o, xth[0][:, par, k, t], xtl[0][:, par, k, t], Mh[:, k, keys], Ml[:, k, keys],
                                       False, k == KD - 1)
                    last.then_inc(s_sc, 1)

                def transpose_probs(g, par):
                    pe.wait_ge(s_exp, g + 1)
                    wait(pe, s_ptl, g)
                    for i in range(GT):
                        last = pe.transpose(psP[0:LK, i * P:(i + 1) * P], pr[:, par, i, :], ident[:])
                    last.then_inc(s_pt, 1)

                def attend(g, par):
                    pe.wait_ge(s_ptl, g + 1)
                    wait(pe, s_res, GT * g)
                    vb = bass.ds((g // 2) * D, D)
                    for i in range(GT):
                        t = slice(i * P, (i + 1) * P)
                        last = mm3(pe, psO[:, i, :], pth[:, t], ptl[:, t], Vh2[:, vb], Vl2[:, vb], True, True)
                    last.then_inc(s_av, 1)

                def logits(g, par):
                    pe.wait_ge(s_xl[1], KD * g + KD)
                    wait(pe, s_route, ROUTE * g)
                    for i in range(GT):
                        t = slice(i * P, (i + 1) * P)
                        for k in range(KD):
                            last = mm3(pe, psL[:, i * E:(i + 1) * E], xth[1][:, par, k, t], xtl[1][:, par, k, t],
                                       gth[:, k, :], gtl[:, k, :], k == 0, k == KD - 1)
                    last.then_inc(s_lg, 1)

                def ranks(g, par):
                    pe.wait_ge(s_both, g + 1)
                    for i in range(GT + 1):
                        o = psR[:, i * E:(i + 1) * E]
                        for j in range(min(i, GT)):
                            last = pe.matmul(o, onesb[:], both[:, j, :], start=(j == 0), stop=(i == GT and j == GT - 1))
                        if i < GT:
                            last = pe.matmul(o, trib[:], both[:, i, :], start=(i == 0), stop=True)
                    last.then_inc(s_rk, 1)
                Vh2 = Vh[:, :, :].rearrange("p b d -> p (b d)")
                Vl2 = Vl[:, :, :].rearrange("p b d -> p (b d)")
                steps = dict(transposes_in=transposes(0), transposes_out=transposes(1), scores=scores,
                             transpose_probs=transpose_probs, attend=attend, logits=logits, ranks=ranks)
                in_order(pe, steps, PE0_ORDER, NG, straight=True)

            @block.vector
            def _(dve):
                def stats(n):
                    def run(g, par):
                        if n == 0:
                            dve.wait_ge(s_x[g], 16)
                        else:
                            dve.wait_ge(s_res, GT * g + GT)
                        rows = X[:, bass.ds(GT * g, GT), :]
                        for i in range(GT):
                            dve.bn_stats(st[n][:, i, :], rows[:, i, :]).then_inc(s_st[n], 1)
                        for i in range(GT):
                            dve.wait_ge(s_st[n], GT * g + i + 1)
                            dve.bn_aggr(mv[n][:, par, i, :], st[n][:, i, :]).then_inc(s_mv[n], 1)
                    return run

                def normalise(n):
                    def run(g, par):
                        rows = X[:, bass.ds(GT * g, GT), :]
                        dve.wait_ge(s_rstd[n], 2 * g + 2)
                        if n == 0:
                            wait(dve, s_xt[0], KD * g)
                        else:
                            wait(dve, s_sct[par], 16 * 2 * GT * (g // 2))
                        for i in range(GT):
                            dst = xa[:, i, :] if n == 0 else xc[:, par, i, :]
                            dve.tensor_scalar(dst, rows[:, i, :], mv[n][:, par, i, 0:1], rstd[n][:, par, i:i + 1],
                                              ALU.subtract, ALU.mult).then_inc(s_xn[n], 1)
                    return run

                def low(n):
                    def run(g, par):
                        for k in range(KD):
                            dve.wait_ge(s_xh[n], KD * g + k + 1)
                            dve.scalar_tensor_tensor(xtl[n][:, par, k, :], psT[:, k, :], SX, xth[n][:, par, k, :],
                                                     ALU.mult, ALU.subtract).then_inc(s_xl[n], 1)
                    return run

                def softmax(g, par):
                    dve.wait_ge(s_sc, g + 1)
                    wait(dve, s_pt, g - 1)
                    sc = psS[:, 0:GT * LK].rearrange("p (i k) -> p i k", i=GT)
                    dve.tensor_reduce(smax[:], sc, AX.X, ALU.max).then_inc(s_smax, 1)
                    dve.wait_ge(s_smax, g + 1)
                    dve.tensor_tensor(pr[:, par, :, :], sc, smax[:].unsqueeze(2).to_broadcast([P, GT, LK]),
                                      ALU.subtract).then_inc(s_sub, 1)

                def denominators(g, par):
                    ch = Chain(dve, s_cf, g, 3)
                    dve.wait_ge(s_exp, g + 1)
                    ch(dve.tensor_reduce(ssum[:], pr[:, par, :, :], AX.X, ALU.add))
                    ch(dve.reciprocal(ssum[:], ssum[:]))
                    ch(dve.tensor_scalar(cf[:, par, :], ssum[:], th[:, 0:1], 1.0 / (SP * SV), ALU.mult, ALU.mult))
                    ch.end()

                def probs_low(g, par):
                    dve.wait_ge(s_pth, g + 1)
                    dve.scalar_tensor_tensor(ptl[:], psP[0:LK, :], SP, pth[:], ALU.mult, ALU.subtract).then_inc(s_ptl, 1)

                def residual(g, par):
                    dve.wait_ge(s_av, g + 1)
                    rows = X[:, bass.ds(GT * g, GT), :]
                    for i in range(GT):
                        dve.scalar_tensor_tensor(rows[:, i, :], psO[:, i, :], cf[:, par, i:i + 1], rows[:, i, :],
                                                 ALU.mult, ALU.add).then_inc(s_res, 1)

                def weights_low(g, par):
                    dve.wait_ge(s_wh, g + 1)
                    dve.tensor_tensor(Wl[:, bass.ds(g * W0E, HW)], stage[:, par, 0:HW], Wh[:, bass.ds(g * W0E, HW)],
                                      ALU.subtract).then_inc(s_wl, 1)

                def choose(g, par):
                    ch = Chain(dve, s_route, g, ROUTE)
                    tiles = bass.ds(GT * g, GT)
                    dve.wait_ge(s_lg, g + 1)
                    ch(dve.tensor_copy(lg[:], psL[:, 0:GT * E].rearrange("p (i e) -> p i e", i=GT)))
                    for i in range(GT):
                        last = dve.max(mx[:, i, :], lg[:, i, :])
                    ch(last)
                    for i in range(GT):
                        last = dve.max_index(ix[:, i, :], mx[:, i, :], lg[:, i, :])
                    ch(last)
                    dve.tensor_copy(top[:, tiles, :], mx[:])
                    ch(dve.tensor_copy(ixf[:], ix[:]))
                    for c in range(2):
                        last = dve.tensor_tensor(pick[:, c, tiles, :], iota8[:].unsqueeze(1).to_broadcast([P, GT, E]),
                                                 ixf[:, :, c:c + 1].to_broadcast([P, GT, E]), ALU.is_equal)
                    ch(last)
                    dve.tensor_tensor(both[:], pick[:, 0, tiles, :], pick[:, 1, tiles, :], ALU.add).then_inc(s_both, 1)

                def place(g, par):
                    ch = Chain(dve, s_route, g, ROUTE)
                    ch.n = 5
                    tiles = bass.ds(GT * g, GT)
                    dve.wait_ge(s_rk, g + 1)
                    ch(dve.tensor_tensor(rank[:, tiles, :], psR[:, 0:GT * E].rearrange("p (i e) -> p i e", i=GT),
                                         base[:].unsqueeze(1).to_broadcast([P, GT, E]), ALU.add))
                    ch(dve.tensor_tensor(base[:], base[:], psR[:, GT * E:GT * E + E], ALU.add))
                    for c in range(2):
                        last = dve.tensor_tensor(prod[:, c, :, :], rank[:, tiles, :], pick[:, c, tiles, :], ALU.mult)
                    ch(last)
                    ch(dve.tensor_reduce(slotf[:], prod[:], AX.X, ALU.add))
                    wait(dve, s_sct[par], 16 * 2 * GT * (g // 2))
                    dve.tensor_copy(slots[:, par, :, :], slotf[:]).then_inc(s_slot, 1)
                    dve.wait_ge(s_slot, g + 1)
                    ch(dve.tensor_copy(slotf[:, 0, 0:1], slotf[:, 1, 0:1]))
                    ch.end()
                steps = dict(stats_in=stats(0), stats_out=stats(1), normalise_in=normalise(0), normalise_out=normalise(1),
                             low_in=low(0), low_out=low(1), softmax=softmax, denominators=denominators,
                             probs_low=probs_low, residual=residual, weights_low=weights_low, choose=choose, place=place)
                in_order(dve, steps, DVE0_ORDER, NG, straight=True)

                ch = Chain(dve, s_blk, 0, 18)
                ch(dve.tensor_copy(padrow[:], base[:]))
                ch(dve.tensor_tensor(cnt[:], base[:], reg8[:], ALU.subtract))
                ch(dve.tensor_tensor(more[:], cnt[:].unsqueeze(2).to_broadcast([P, E, 16]), thr[:], ALU.is_gt))
                ch(dve.tensor_reduce(nblk[:], more[:], AX.X, ALU.add))
                ch(dve.tensor_tensor(tri8n[:], tri8[:], nblk[:].unsqueeze(1).to_broadcast([P, E, E]), ALU.mult))
                ch(dve.tensor_reduce(cum[:], tri8n[:], AX.X, ALU.add))
                ch(dve.tensor_tensor(adj[:], cum[:], nblk[:], ALU.subtract))
                ch(dve.scalar_tensor_tensor(adj[:], adj[:], float(BR), reg8[:], ALU.mult, ALU.subtract))
                jj = iotaj[:].unsqueeze(2).to_broadcast([P, NB0, E])
                ch(dve.tensor_tensor(done[:], cum[:].unsqueeze(1).to_broadcast([P, NB0, E]), jj, ALU.is_le))
                ch(dve.tensor_reduce(ej[:], done[:], AX.X, ALU.add))
                ch(dve.tensor_tensor(done2[:], done[:], nblk[:].unsqueeze(1).to_broadcast([P, NB0, E]), ALU.mult))
                ch(dve.tensor_reduce(mj[:], done2[:], AX.X, ALU.add))
                ch(dve.tensor_tensor(mj[:], iotaj[:], mj[:], ALU.subtract))
                ch(dve.tensor_scalar(lt[:], ej[:], float(E), float(BR), ALU.is_lt, ALU.mult))
                ch(dve.tensor_tensor(mj[:], mj[:], lt[:], ALU.mult))
                ch(dve.scalar_tensor_tensor(lt[:], ej[:], float(REG), mj[:], ALU.mult, ALU.add))
                ch(dve.tensor_scalar(ej[:], ej[:], float(E - 1), float(W0E), ALU.min, ALU.mult))
                dve.tensor_copy(blkrow[:], lt[:])
                ch(dve.tensor_copy(blkw[:], ej[:]))
                ch.end()

                ch = Chain(dve, s_fin2, 0, 8)
                ch(dve.tensor_tensor(wts[:, 0, :], top[:, :, 1], top[:, :, 0], ALU.subtract))
                dve.tensor_copy(smax[:], smax[:]).then_inc(s_fin, 1)
                ch(dve.tensor_tensor(rank[:], rank[:], adj[:].unsqueeze(1).to_broadcast([P, T, E]), ALU.add))
                for c in range(2):
                    last = dve.tensor_tensor(prodT[:, c, :, :], rank[:], pick[:, c, :, :], ALU.mult)
                ch(last)
                ch(dve.tensor_reduce(slotT[:], prodT, AX.X, ALU.add))
                dve.tensor_copy(islot[:], slotT[:])
                dve.wait_ge(s_fin, 2)
                ch(dve.tensor_scalar(wts[:, 0, :], wts[:, 1, :], 1.0, None, ALU.add))
                ch(dve.reciprocal(wts[:, 0, :], wts[:, 0, :]))
                ch(dve.tensor_tensor(wts[:, 1, :], wts[:, 1, :], wts[:, 0, :], ALU.mult))
                ch(dve.tensor_scalar(wts[:], wts[:], th[:, 2:3], None, ALU.mult))
                ch.end()
        a0.close()

        FT = F0 // P
        HF = FT // 2
        UP, DOWN = KD * F0, 2 * KD * F0
        e0 = ExitStack()
        bx = sb("bx", [P, 2, 2, D], F32, e0)
        bxh = sb("bxh", [P, 2, KD, BR], F16, e0)
        bxl = sb("bxl", [P, 2, KD, BR], F16, e0)
        sil = sb("sil", [P, 2, HF, BR], F32, e0)
        hid = sb("hid", [P, 2, HF, BR], F32, e0)
        hh = sb("hh", [P, 2, FT, BR], F16, e0)
        hl = sb("hl", [P, 2, FT, BR], F16, e0)
        yo = sb("yo", [P, 2, 2, D], F32, e0)
        H, DH = 16, 64
        HP = H // 2
        SK = 64.0
        r1 = ExitStack()
        gth1 = sb("gth1", [P, KD, E], F16, r1, "right")
        gtl1 = sb("gtl1", [P, KD, E], F16, r1, "right")
        bo = sb("bo", [P, D], F32, r1, "right")
        gts1 = sb("gts1", [P, KD, E], F32, r1, "right")
        thx1 = sb("thx1", [P, 1], F32, r1, "right")
        r2 = ExitStack()
        PIECES = [("ctx1", "ctxT", NKEY, SK), ("wk1", "wk1", H * DH, SW), ("wv1", "wv1", H * DH, SW),
                  ("wq1", "wqT1", D, SW), ("wo1", "wo1", D, SW)]
        tiles_of = {"ctx1": 2, "wk1": 2, "wv1": 2, "wq1": HP, "wo1": HP}
        split1 = {name: [sb(f"{name}{part}", [P, tiles_of[name] * cols], F16, r2, "right") for part in "hl"]
                  for name, _, cols, _ in PIECES}
        r3 = ExitStack()
        raw1 = sb("raw1", [P, HP * D], F32, r3, "right")
        r3.close()
        e0.close()

        def regions(i):
            name, _, cols, _ = PIECES[i]
            n = tiles_of[name]
            return [(P, 0, n * cols)] if n == HP else [(P, 0, cols), (DC - P, cols, 2 * cols)]

        pe0 = ExitStack()
        psX = [ps(f"psX{n}", [P, KD, BR], F32, pe0) for n in range(2)]
        psG = [ps(f"psG{n}", [P, HF, BR], F32, pe0) for n in range(2)]
        psU = [ps(f"psU{n}", [P, HF, BR], F32, pe0) for n in range(2)]
        psY = [ps(f"psY{n}", [P, 2, D], F32, pe0) for n in range(2)]
        pe0.close()
        b_in = [sem(f"b_in{n}") for n in range(2)]
        b_xt = sem("b_xt")
        b_xh = sem("b_xh")
        b_xl = sem("b_xl")
        b_g = [sem(f"b_g{n}") for n in range(2)]
        b_sil = [sem(f"b_sil{n}") for n in range(2)]
        b_hid = [sem(f"b_hid{n}") for n in range(2)]
        b_hl = [sem(f"b_hl{n}") for n in range(2)]
        b_y = sem("b_y")
        b_yo = sem("b_yo")
        b_out = [sem(f"b_out{n}") for n in range(2)]
        BDEPTH = 4
        b_w1 = sem("b_w1")
        b_w1h = sem("b_w1h")
        b_w1l = sem("b_w1l")
        FIRST_PIECE = 4
        PEEL = FIRST_PIECE + len(PIECES)

        def piece_of(j):
            i = j - FIRST_PIECE if isinstance(j, int) else -1
            return i if 0 <= i < len(PIECES) else None

        with nc.Block() as block:
            @block.sync
            def _(sp):
                def load(j, par):
                    wait(sp, b_xt, j - 1)
                    row = sp.value_load(blkrow[0:1, bass.ds(j, 1)], min_val=0, max_val=E * REG)
                    sp.dma_start(bx[:, par, :, :], x_rows[bass.ds(row, BR), :].rearrange("(n p) d -> p n d", p=P))\
                      .then_inc(b_in[par], 16)

                def store(j, par):
                    sp.wait_ge(b_yo, j + 1)
                    sp.dma_start(y_rows[bass.ds(j * BR, BR), :].rearrange("(n p) d -> p n d", p=P), yo[:, par, :, :])\
                      .then_inc(b_out[par], 16)

                def load_piece(j, par):
                    i = piece_of(j)
                    if i is None:
                        return
                    name, src, cols, _ = PIECES[i]
                    wait(sp, b_w1l, i)
                    for rows, c0_, c1_ in regions(i):
                        if tiles_of[name] == HP:
                            sp.dma_start(raw1[:].rearrange("p (k d) -> p k d", d=D), a[src].rearrange("(k p) d -> p k d", p=P))\
                              .then_inc(b_w1, 16)
                        else:
                            sp.dma_start(raw1[0:rows, c0_:c1_], a[src][(c0_ // cols) * P:(c0_ // cols) * P + rows, :])\
                              .then_inc(b_w1, 16)
                sp.dma_start(gts1[:], a["gate1"]).then_inc(b_w1, 16)
                sp.dma_start(bo[:], a["bo1"].partition_broadcast(P)).then_inc(b_w1, 16)
                pipeline(sp, NB0, PEEL, [(0, load), (3, store), (0, load_piece)])
                sp.wait_ge(b_out[0], 16 * ((NB0 + 1) // 2))
                sp.wait_ge(b_out[1], 16 * (NB0 // 2))

            @block.tensor
            def _(pe):
                def transposes(j, par):
                    pe.wait_ge(b_in[par], 16 * (j // 2) + 16)
                    wait(pe, b_xl, j - 1)
                    for k in range(KD):
                        for n in range(2):
                            last = pe.transpose(psX[par][:, k, n * P:(n + 1) * P], bx[:, par, n, k * P:(k + 1) * P], ident[:])
                    last.then_inc(b_xt, 1)

                def up(j, par):
                    w = pe.value_load(blkw[0:1, bass.ds(j, 1)], min_val=0, max_val=(E - 1) * W0E)
                    pe.wait_ge(b_xl, j + 1)
                    for half in range(2):
                        wait(pe, b_hid[half], 2 * j)
                        for psum, off in ((psG, 0), (psU, UP)):
                            for f in range(HF):
                                for k in range(KD):
                                    at = bass.ds(w + (off + k * F0 + (half * HF + f) * P), P)
                                    last = mm3(pe, psum[half][:, f, :], Wh[:, at], Wl[:, at], bxh[:, par, k, :],
                                               bxl[:, par, k, :], k == 0, k == KD - 1)
                        last.then_inc(b_g[half], 1)

                def down(j, par):
                    w = pe.value_load(blkw[0:1, bass.ds(j, 1)], min_val=0, max_val=(E - 1) * W0E)
                    for half in range(2):
                        pe.wait_ge(b_hl[half], j + 1)
                    wait(pe, b_yo, j - 1)
                    for n in range(2):
                        rows = slice(n * P, (n + 1) * P)
                        for f in range(FT):
                            at = bass.ds(w + (DOWN + f * D), D)
                            last = mm3(pe, psY[par][:, n, :], hh[:, par, f, rows], hl[:, par, f, rows], Wh[:, at], Wl[:, at],
                                       f == 0, f == FT - 1)
                    last.then_inc(b_y, 1)
                pipeline(pe, NB0, BDEPTH, [(2, up), (1, transposes), (3, down)])

            @block.scalar
            def _(act):
                def rows_high(j, par):
                    act.wait_ge(b_xt, j + 1)
                    wait(act, b_g[1], j - 1)
                    act.activation(bxh[:, par, :, :], psX[par][:, :, :], ACT.Copy, scale=SX).then_inc(b_xh, 1)

                def silu(j, par):
                    for half in range(2):
                        act.wait_ge(b_g[half], j + 1)
                        act.activation(sil[:, half, :, :], psG[half][:, :, :], ACT.Silu, scale=1.0 / (SX * SW))\
                           .then_inc(b_sil[half], 1)

                def results(j, par):
                    act.wait_ge(b_y, j + 1)
                    if not isinstance(j, int) or j >= 2:
                        act.wait_ge(b_out[par], 16 * (j // 2))
                    act.activation(yo[:, par, :, :], psY[par][:, :, :], ACT.Copy, scale=1.0 / (SH * SW)).then_inc(b_yo, 1)

                def high_piece(j, par):
                    i = piece_of(j)
                    if i is None:
                        return
                    name, _, _, scale = PIECES[i]
                    act.wait_ge(b_w1, 32 + 16 * sum(len(regions(n)) for n in range(i + 1)))
                    for rows, c0_, c1_ in regions(i):
                        ins = act.activation(split1[name][0][0:rows, c0_:c1_], raw1[0:rows, c0_:c1_], ACT.Copy, scale=scale)
                    ins.then_inc(b_w1h, 1)
                pipeline(act, NB0, PEEL, [(2, silu), (1, rows_high), (3, results), (1, high_piece)])

            @block.vector
            def _(dve):
                def rows_low(j, par):
                    dve.wait_ge(b_xh, j + 1)
                    dve.scalar_tensor_tensor(bxl[:, par, :, :], psX[par][:, :, :], SX, bxh[:, par, :, :],
                                             ALU.mult, ALU.subtract).then_inc(b_xl, 1)

                def hidden(j, par):
                    wait(dve, b_y, j - 1)
                    for half in range(2):
                        f = slice(half * HF, (half + 1) * HF)
                        dve.wait_ge(b_sil[half], j + 1)
                        dve.scalar_tensor_tensor(hid[:, half, :, :], psU[half][:, :, :], SH / (SX * SW), sil[:, half, :, :],
                                                 ALU.mult, ALU.mult).then_inc(b_hid[half], 1)
                        dve.wait_ge(b_hid[half], 2 * j + 1)
                        dve.tensor_copy(hh[:, par, f, :], hid[:, half, :, :]).then_inc(b_hid[half], 1)
                        dve.wait_ge(b_hid[half], 2 * j + 2)
                        dve.tensor_tensor(hl[:, par, f, :], hid[:, half, :, :], hh[:, par, f, :], ALU.subtract)\
                           .then_inc(b_hl[half], 1)

                def low_piece(j, par):
                    i = piece_of(j)
                    if i is None:
                        return
                    name, _, _, scale = PIECES[i]
                    dve.wait_ge(b_w1h, i + 1)
                    for rows, c0_, c1_ in regions(i):
                        ins = dve.scalar_tensor_tensor(split1[name][1][0:rows, c0_:c1_], raw1[0:rows, c0_:c1_], scale,
                                                       split1[name][0][0:rows, c0_:c1_], ALU.mult, ALU.subtract)
                    ins.then_inc(b_w1l, 1)
                pipeline(dve, NB0, PEEL, [(2, hidden), (1, rows_low), (1, low_piece)])

        l0.close()

        CK = H * LK
        KM, KR = P // 2, LK - P // 2
        RR = HP * KR
        NC = HP + 2
        QK = CK // 4
        SM1 = SM * DH ** -0.5
        l1 = ExitStack()
        M1h = sb("M1h", [P, B, KD, CK], F16, l1)
        M1l = sb("M1l", [P, B, KD, CK], F16, l1)
        N1 = sb("N1", [P, B, NC, 2 * D], F16, l1)
        u1 = ExitStack()
        K1 = [sb(f"K1{part}", [P, HP, 2, NKEY], F16, u1) for part in "hl"]
        V1 = [sb(f"V1{part}", [P, HP, B, P], F16, u1) for part in "hl"]
        V2 = [sb(f"V2{part}", [P, HP, B, RR], F16, u1) for part in "hl"]
        u1.close()
        r2.close()
        pu = ExitStack()
        psM = [ps(f"psM{n}", [P, 512], F32, pu) for n in range(4)]
        psN = [ps(f"psN{n}", [P, 2, D], F32, pu) for n in range(4)]
        pu.close()
        u_p = sem("u_p")
        u_ph = sem("u_ph")
        u_pl = sem("u_pl")
        u_m = sem("u_m")
        u_mh = sem("u_mh")
        u_ml = sem("u_ml")
        u_n = sem("u_n")
        u_nh = sem("u_nh")
        u_nl = sem("u_nl")
        u_z = sem("u_z")
        u_z2 = sem("u_z2")
        u_g = sem("u_g")

        halves = (slice(0, DH), slice(DH, P))
        psNf = [p[:, :, :].rearrange("p a d -> p (a d)") for p in psN]

        def keys_of(psum, rows, first, n):
            return psum[rows, 0:NKEY].rearrange("p (b k) -> p b k", b=B)[:, :, first:first + n]

        N_TURNS = ((0, 1), (2, 3, 4))

        def in_v2(m, odd):
            at = ((m % (HP // 2)) * 2 + odd) * KR
            return slice(at, at + KR)

        with nc.Block() as block:
            @block.gpsimd
            def _(pool):
                for i in range(2):
                    pool.memset(K1[i][DH:P, :, 0, :], 0.0)
                    pool.memset(K1[i][0:DH, :, 1, :], 0.0)
                    pool.memset(V1[i][DH:P, :, :, 0:KM], 0.0)
                    pool.memset(V1[i][0:DH, :, :, KM:P], 0.0).then_inc(u_z, 1)

            @block.tensor
            def _(pe):
                cth, ctl = split1["ctx1"]
                for m in range(HP):
                    for turn, (name, psum) in enumerate((("wk1", psM), ("wv1", psN))):
                        wh, wl = split1[name]
                        o = psum[m % 4][:, :] if psum is psM else psum[m % 4][:, :, :].rearrange("p a d -> p (a d)")
                        wait(pe, u_pl, 2 * (m - 4) + turn + 1)
                        for rows, k in ((P, 0), (DC - P, 1)):
                            at = k * H * DH + m * P
                            last = mm3(pe, o[:, 0:NKEY], wh[0:rows, at:at + P], wl[0:rows, at:at + P],
                                       cth[0:rows, k * NKEY:(k + 1) * NKEY], ctl[0:rows, k * NKEY:(k + 1) * NKEY], k == 0, k == 1)
                        last.then_inc(u_p, 1)
                pe.wait_ge(u_pl, 2 * HP)
                wqh, wql = split1["wq1"]
                woh, wol = split1["wo1"]
                pe.wait_ge(u_z, 2)
                for b in range(B):
                    keys = slice(b * LK, (b + 1) * LK)
                    for m in range(KD):
                        for bank in range(4):
                            wait(pe, u_ml, (KD * b + m - 1) * 4 + bank + 1)
                            for i in range(2):
                                pair = 2 * bank + i
                                at = pair * D + m * P
                                last = mm3(pe, psM[bank][:, i * 2 * LK:(i + 1) * 2 * LK].rearrange("p (h k) -> p h k", h=2),
                                           wqh[:, at:at + P], wql[:, at:at + P], K1[0][:, pair, :, keys], K1[1][:, pair, :, keys],
                                           True, True)
                            last.then_inc(u_m, 1)
                        for v in N_TURNS[m]:
                            wait(pe, u_nl, 5 * b + v - 3)
                            o = psN[(5 * b + v) % 4]
                            for i in range(2):
                                if v < 4:
                                    pair = 2 * v + i
                                    last = mm3(pe, o[:, i, :], V1[0][:, pair, b, :], V1[1][:, pair, b, :],
                                               woh[:, pair * D:(pair + 1) * D], wol[:, pair * D:(pair + 1) * D], True, True)
                                    continue
                                first = i * (HP // 2)
                                for pair in range(first, first + HP // 2):
                                    last = mm3(pe, o[0:RR, i, :], V2[0][:, pair, b, :], V2[1][:, pair, b, :],
                                               woh[:, pair * D:(pair + 1) * D], wol[:, pair * D:(pair + 1) * D],
                                               pair == first, pair == first + HP // 2 - 1)
                            last.then_inc(u_n, 1)

            @block.scalar
            def _(act):
                for m in range(HP):
                    act.wait_ge(u_p, 2 * m + 1)
                    for odd, rows in enumerate(halves):
                        ins = act.activation(K1[0][rows, m, odd, :], psM[m % 4][rows, 0:NKEY], ACT.Copy, scale=1.0 / SW)
                    ins.then_inc(u_ph, 1)
                    act.wait_ge(u_p, 2 * m + 2)
                    wait(act, u_z2, 1 if m == 0 else 0)
                    for odd, rows in enumerate(halves):
                        act.activation(V1[0][rows, m, :, odd * KM:(odd + 1) * KM], keys_of(psNf[m % 4], rows, 0, KM), ACT.Copy,
                                       scale=1.0 / SW)
                        ins = act.activation(V2[0][rows, m, :, in_v2(m, odd)], keys_of(psNf[m % 4], rows, KM, KR), ACT.Copy,
                                             scale=1.0 / SW)
                    ins.then_inc(u_ph, 1)
                act.activation(gth1[:], gts1[:], ACT.Copy, scale=SW).then_inc(u_g, 1)

                for b in range(B):
                    for m in range(KD):
                        for bank in range(4):
                            act.wait_ge(u_m, 4 * (KD * b + m) + bank + 1)
                            act.activation(M1h[:, b, m, bank * QK:(bank + 1) * QK], psM[bank][:, 0:QK], ACT.Copy,
                                           scale=SM1 / (SK * SW)).then_inc(u_mh, 1)
                        for v in N_TURNS[m]:
                            act.wait_ge(u_n, 5 * b + (v + 1))
                            rows = P if v < 4 else RR
                            act.activation(N1[0:rows, b, 2 * v:2 * v + 2, 0:D], psN[(5 * b + v) % 4][0:rows, :, :], ACT.Copy,
                                           scale=SV / (SK * SW)).then_inc(u_nh, 1)

            @block.vector
            def _(dve):
                for v2 in V2:
                    ins = dve.memset(v2[:], 0.0)
                ins.then_inc(u_z2, 1)
                dve.tensor_scalar(bo[:], bo[:], th[:, 1:2], None, ALU.mult)
                dve.wait_ge(u_z2, 1)
                for m in range(HP):
                    dve.wait_ge(u_ph, 2 * m + 1)
                    for odd, rows in enumerate(halves):
                        ins = dve.scalar_tensor_tensor(K1[1][rows, m, odd, :], psM[m % 4][rows, 0:NKEY], 1.0 / SW,
                                                       K1[0][rows, m, odd, :], ALU.mult, ALU.subtract)
                    ins.then_inc(u_pl, 1)
                    dve.wait_ge(u_ph, 2 * m + 2)
                    for odd, rows in enumerate(halves):
                        part = slice(odd * KM, (odd + 1) * KM)
                        dve.scalar_tensor_tensor(V1[1][rows, m, :, part], keys_of(psNf[m % 4], rows, 0, KM), 1.0 / SW,
                                                 V1[0][rows, m, :, part], ALU.mult, ALU.subtract)
                        part = in_v2(m, odd)
                        ins = dve.scalar_tensor_tensor(V2[1][rows, m, :, part], keys_of(psNf[m % 4], rows, KM, KR), 1.0 / SW,
                                                       V2[0][rows, m, :, part], ALU.mult, ALU.subtract)
                    ins.then_inc(u_pl, 1)
                dve.wait_ge(u_g, 1)
                dve.scalar_tensor_tensor(gtl1[:], gts1[:], SW, gth1[:], ALU.mult, ALU.subtract)

                for b in range(B):
                    for m in range(KD):
                        for bank in range(4):
                            dve.wait_ge(u_mh, (KD * 4) * b + (4 * m + bank + 1))
                            dve.scalar_tensor_tensor(M1l[:, b, m, bank * QK:(bank + 1) * QK], psM[bank][:, 0:QK], SM1 / (SK * SW),
                                                     M1h[:, b, m, bank * QK:(bank + 1) * QK],
                                                     ALU.mult, ALU.subtract).then_inc(u_ml, 1)
                        for v in N_TURNS[m]:
                            dve.wait_ge(u_nh, 5 * b + (v + 1))
                            rows = P if v < 4 else RR
                            dve.scalar_tensor_tensor(N1[0:rows, b, 2 * v:2 * v + 2, D:2 * D], psN[(5 * b + v) % 4][0:rows, :, :],
                                                     SV / (SK * SW), N1[0:rows, b, 2 * v:2 * v + 2, 0:D],
                                                     ALU.mult, ALU.subtract).then_inc(u_nl, 1)

        m1 = ExitStack()
        yg = sb("yg", [P, 2, 2, D], F32, m1)
        st1 = [sb(f"st1{n}", [P, 6], F32, m1) for n in range(2)]
        mv1 = [sb(f"mv1{n}", [P, 2, 2], F32, m1) for n in range(2)]
        rs1 = [sb(f"rs1{n}", [P, 2, 1], F32, m1) for n in range(2)]
        xn1 = [sb(f"xn1{n}", [P, 2, D], F32, m1) for n in range(2)]
        xh1 = [sb(f"xh1{n}", [P, 2, KD, P], F16, m1) for n in range(2)]
        xl1 = [sb(f"xl1{n}", [P, 2, KD, P], F16, m1) for n in range(2)]
        mx1 = sb("mx1", [P, H], F32, m1)
        pr1 = sb("pr1", [P, 2, CK], F32, m1)
        pn1 = sb("pn1", [P, 2, CK], F32, m1)
        sum1 = sb("sum1", [P, 2, H], F32, m1)
        ph1 = sb("ph1", [P, NC, P], F16, m1)
        pl1 = sb("pl1", [P, NC, P], F16, m1)
        lmx = sb("lmx", [P, 1], F32, m1)
        lex = sb("lex", [P, 2, E], F32, m1)
        lsum = sb("lsum", [P, 2, 1], F32, m1)
        m1.close()
        pm1 = ExitStack()
        psS1 = ps("psS1", [P, 4, 512], F32, pm1)
        psXa = ps("psXa", [P, KD, P], F32, pm1)
        psP1 = [ps(f"psP1{n}", [P, 4, P], F32, pm1) for n in range(2)]
        psOL = ps("psOL", [P, 2, D], F32, pm1)
        psO1, psL1 = psOL[:, 0, :], psOL[:, 1, :]
        pm1.close()
        CH = [(0, 4), (4, 8), (8, NC)]
        c_y = [sem(f"c_y{n}") for n in range(2)]
        c_comb = sem("c_comb")
        c_mv = [sem(f"c_mv{n}") for n in range(2)]
        c_rs = [sem(f"c_rs{n}") for n in range(2)]
        c_xn = [sem(f"c_xn{n}") for n in range(2)]
        c_xt = [sem(f"c_xt{n}") for n in range(2)]
        c_xh = [sem(f"c_xh{n}") for n in range(2)]
        c_xl = [sem(f"c_xl{n}") for n in range(2)]
        c_bo = sem("c_bo")
        c_sc = [sem(f"c_sc{n}") for n in range(2)]
        c_mx = sem("c_mx")
        c_sub = [sem(f"c_sub{n}") for n in range(2)]
        c_exp = [sem(f"c_exp{n}") for n in range(2)]
        c_rcp = sem("c_rcp")
        c_pn = sem("c_pn")
        c_pt = [sem(f"c_pt{n}") for n in range(3)]
        c_ph = [sem(f"c_ph{n}") for n in range(3)]
        c_pl = [sem(f"c_pl{n}") for n in range(3)]
        c_av = [sem(f"c_av{n}") for n in range(3)]
        c_res = sem("c_res")
        c_lg = sem("c_lg")
        c_lm = sem("c_lm")
        c_ls = sem("c_ls")
        c_le = sem("c_le")
        c_aff = sem("c_aff")
        c_one = sem("c_one")
        c_tick = sem("c_tick")
        c_out = [sem(f"c_out{n}") for n in range(2)]

        PE_ORDER = [("turn0", 4), ("transposes_out", 6), ("scores0", 2), ("scores1", 2), ("logits", 6), ("turn2", 4),
                    ("transposes_in", 1), ("outputs0", 4), ("turn1", 3), ("outputs1", 4), ("outputs2", 4)]
        ACT_ORDER = [("probs_high0", 4), ("high_out", 6), ("probs_high1", 4), ("exps0", 2), ("high_in", 1), ("probs_high2", 4),
                     ("exps1", 2), ("router_exp", 7)]
        DVE_ORDER = [("probs_low0", 4), ("maxima0", 2), ("normalise_in", 1), ("low_out", 6), ("router_sub", 6), ("maxima1", 2),
                     ("probs_low1", 4), ("low_in", 1), ("probs_low2", 4), ("combine", 0), ("normalise_out", 5),
                     ("residual", 4), ("reciprocals", 2), ("router_norm", 7)]
        POOL_ORDER = [("gather", 0), ("add_bias", 2), ("rstd_out", 5), ("rstd_in", 1), ("normalise_probs", 3)]

        def apart(e, sem_, value):
            wait(e, sem_, value)
            if not isinstance(value, int):
                e.sem_inc(c_tick, 1)

        with nc.Block() as block:
            @block.sync
            def _(sp):
                def store(t, par):
                    sp.wait_ge(c_xn[1], t + 1)
                    sp.dma_start(out_rows[bass.ds(t * P, P), :], X[:, bass.ds(t, 1), :].rearrange("p t d -> p (t d)"))\
                      .then_inc(c_out[par], 16)
                    sp.dma_start(n_rows[bass.ds(t * P, P), :], xn1[1][:, par, :]).then_inc(c_out[par], 16)
                pipeline(sp, T, 1, [(0, store)])
                for n in range(2):
                    sp.wait_ge(c_out[n], 16 * T)

            @block.gpsimd
            def _(pool):
                def rstd_of(n):
                    def run(t, par):
                        pool.wait_ge(c_mv[n], 2 * t + 2)
                        pool.tensor_scalar(rs1[n][:, par, :], mv1[n][:, par, 1:2], EPS, None, ALU.add).then_inc(c_rs[n], 1)
                        pool.wait_ge(c_rs[n], 2 * t + 1)
                        pool.tensor_tensor(rs1[n][:, par, :], rs1[n][:, par, :], mhalf[:, 0:1], ALU.pow).then_inc(c_rs[n], 1)
                    return run

                def normalise_probs(t, par):
                    pool.wait_ge(c_rcp, t + 1)
                    for n in range(3):
                        wait(pool, c_pt[n], t - 1)
                    p = pr1[:, par, :].rearrange("p (h k) -> p h k", h=H)
                    for at, first, n in ((0, 0, KM), (H * KM, KM, KR)):
                        o = pn1[:, par, at:at + H * n].rearrange("p (h k) -> p h k", h=H)
                        ins = pool.tensor_tensor(o, p[:, :, first:first + n], sum1[:, par, :].unsqueeze(2).to_broadcast([P, H, n]),
                                                 ALU.mult)
                    ins.then_inc(c_pn, 1)

                def gather(t, par):
                    wait(pool, c_comb, 2 * (t - 1))
                    for c in range(2):
                        pool.indirect_dma_start(yg[:, par, c, :], None, y_rows[:, :],
                                                bass.IndirectOffsetOnAxis(islot[:, c, t:t + 1], 0)).then_inc(c_y[par], 16)

                def add_bias(t, par):
                    pool.wait_ge(c_xn[0], t + 1)
                    pool.tensor_tensor(X[:, t, :], X[:, t, :], bo[:], ALU.add).then_inc(c_bo, 1)
                steps = dict(gather=gather, add_bias=add_bias, rstd_out=rstd_of(1), rstd_in=rstd_of(0),
                             normalise_probs=normalise_probs)
                in_order(pool, steps, POOL_ORDER, T, straight=True)

            @block.scalar
            def _(act):
                def high(n):
                    def run(t, par):
                        if n:
                            wait(act, c_lg, t - 1)
                        else:
                            wait(act, c_sc[0], t - 1)
                            wait(act, c_sc[1], t - 1)
                        act.wait_ge(c_xt[n], t + 1)
                        act.activation(xh1[n][:, par, :, :], psXa[:], ACT.Copy, scale=SX).then_inc(c_xh[n], 1)
                    return run

                def exps(half):
                    def run(t, par):
                        act.wait_ge(c_sub[half], t + 1)
                        wait(act, c_pn, t - 1)
                        for q in (2 * half, 2 * half + 1):
                            for i in range(4):
                                h = 4 * q + i
                                ins = act.activation(pr1[:, par, h * LK:(h + 1) * LK], psS1[:, q, i * LK:(i + 1) * LK], ACT.Exp,
                                                     bias=mx1[:, h:h + 1], scale=1.0 / (SX * SM), accum_out=sum1[:, par, h:h + 1])
                        ins.then_inc(c_exp[half], 1)
                    return run

                def probs_high(n):
                    def run(t, par):
                        a_, b_ = CH[n]
                        act.wait_ge(c_pt[n], t + 1)
                        wait(act, c_av[n], t)
                        rows = P if n < 2 else RR
                        ins = act.activation(ph1[0:rows, a_:b_, :], psP1[n % 2][0:rows, 0:b_ - a_, :], ACT.Copy, scale=SP)
                        ins.then_inc(c_ph[n], 1)
                    return run

                def router_exp(t, par):
                    act.wait_ge(c_ls, t + 1)
                    act.activation(lex[:, par, :], lex[:, par, :], ACT.Exp, scale=1.0 / (SX * SW),
                                   accum_out=lsum[:, par, :]).then_inc(c_le, 1)
                steps = dict(high_in=high(0), high_out=high(1), exps0=exps(0), exps1=exps(1), router_exp=router_exp,
                             probs_high0=probs_high(0), probs_high1=probs_high(1), probs_high2=probs_high(2))
                in_order(act, steps, ACT_ORDER, T)

            @block.tensor
            def _(pe):
                def transposes(n):
                    def run(t, par):
                        pe.wait_ge(c_xn[n], t + 1)
                        wait(pe, c_xl[n], t)
                        wait(pe, c_xl[1 - n], before(t, *(("transposes_out", "transposes_in") if n else
                                                          ("transposes_in", "transposes_out")), PE_ORDER, T))
                        for k in range(KD):
                            last = pe.transpose(psXa[:, k, :], xn1[n][:, par, k * P:(k + 1) * P], ident[:])
                        last.then_inc(c_xt[n], 1)
                    return run

                def scores(half):
                    def run(t, par):
                        pe.wait_ge(c_xl[0], t + 1)
                        wait(pe, c_exp[half], t)
                        for q in (2 * half, 2 * half + 1):
                            for k in range(KD):
                                at = bass.ds((t // (S // P)) * (KD * CK) + (k * CK + q * QK), QK)
                                last = mm3(pe, psS1[:, q, 0:QK], xh1[0][:, par, k, :], xl1[0][:, par, k, :],
                                           M1hf[:, at], M1lf[:, at], k == 0, k == KD - 1)
                        last.then_inc(c_sc[half], 1)
                    return run

                def logits(t, par):
                    pe.wait_ge(c_xl[1], t + 1)
                    wait(pe, c_ls, t)
                    wait(pe, c_res, before(t, "logits", "outputs0", PE_ORDER, T))
                    for k in range(KD):
                        last = mm3(pe, psL1[:, 0:E], xh1[1][:, par, k, :], xl1[1][:, par, k, :], gth1[:, k, :], gtl1[:, k, :],
                                   k == 0, k == KD - 1)
                    last.then_inc(c_lg, 1)

                def turn(n):
                    def run(t, par):
                        pe.wait_ge(c_pn, t + 1)
                        a_, b_ = CH[n]
                        wait(pe, c_pl[(2, 1, 0)[n]], t + 1 if n == 2 else t)
                        for c in range(a_, b_):
                            rows = P if c < HP else RR
                            at = c * P if c < HP else HP * P + (c - HP) * RR
                            ins = pe.transpose(psP1[n % 2][0:rows, c - a_, :], pn1[:, par, at:at + rows], ident[:])
                        ins.then_inc(c_pt[n], 1)
                    return run

                def outputs(n):
                    def run(t, par):
                        a_, b_ = CH[n]
                        pe.wait_ge(c_pl[n], t + 1)
                        if n == 0:
                            wait(pe, c_res, t)
                            wait(pe, c_ls, before(t, "outputs0", "logits", PE_ORDER, T))
                        for c in range(a_, b_):
                            rows = P if c < HP else RR
                            at = (t // (S // P)) * (NC * 2 * D) + c * 2 * D
                            ins = mm3(pe, psO1, ph1[0:rows, c, :], pl1[0:rows, c, :], N1f[0:rows, bass.ds(at, D)],
                                      N1f[0:rows, bass.ds(at + D, D)], c == 0, c == NC - 1)
                        ins.then_inc(c_av[n], 1)
                    return run
                M1hf = M1h[:].rearrange("p b k c -> p (b k c)")
                M1lf = M1l[:].rearrange("p b k c -> p (b k c)")
                N1f = N1[:].rearrange("p b c d -> p (b c d)")
                steps = dict(transposes_in=transposes(0), transposes_out=transposes(1), scores0=scores(0), scores1=scores(1),
                             turn0=turn(0), turn1=turn(1), turn2=turn(2), logits=logits,
                             outputs0=outputs(0), outputs1=outputs(1), outputs2=outputs(2))
                in_order(pe, steps, PE_ORDER, T)

            @block.vector
            def _(dve):
                def combine(t, par):
                    row = X[:, bass.ds(t, 1), :].rearrange("p t d -> p (t d)")
                    dve.wait_ge(c_y[par], 32 * (t // 2) + 32)
                    for c in range(2):
                        dve.scalar_tensor_tensor(row, yg[:, par, c, :], wts[:, c, bass.ds(t, 1)], row, ALU.mult, ALU.add)\
                           .then_inc(c_comb, 1)
                        apart(dve, c_comb, 2 * t + (c + 1))
                    stats(0)(t, par)

                def stats(n):
                    def run(t, par):
                        row = X[:, bass.ds(t, 1), :].rearrange("p t d -> p (t d)")
                        dve.bn_stats(st1[n][:], row).then_inc(c_mv[n], 1)
                        apart(dve, c_mv[n], 2 * t + 1)
                        dve.bn_aggr(mv1[n][:, par, :], st1[n][:]).then_inc(c_mv[n], 1)
                    return run

                def normalise(n):
                    def run(t, par):
                        row = X[:, bass.ds(t, 1), :].rearrange("p t d -> p (t d)")
                        dve.wait_ge(c_rs[n], 2 * t + 2)
                        if n == 0:
                            wait(dve, c_xt[0], t - 1)
                        elif not isinstance(t, int) or t >= 2:
                            dve.wait_ge(c_out[par], 32 * (t // 2))
                            dve.wait_ge(c_xt[1], t - 1)
                        dve.tensor_scalar(xn1[n][:, par, :], row, mv1[n][:, par, 0:1], rs1[n][:, par, :],
                                          ALU.subtract, ALU.mult).then_inc(c_xn[n], 1)
                    return run

                def low(n):
                    def run(t, par):
                        dve.wait_ge(c_xh[n], t + 1)
                        dve.scalar_tensor_tensor(xl1[n][:, par, :, :], psXa[:], SX, xh1[n][:, par, :, :],
                                                 ALU.mult, ALU.subtract).then_inc(c_xl[n], 1)
                    return run

                def maxima(half):
                    def run(t, par):
                        dve.wait_ge(c_sc[half], t + 1)
                        wait(dve, c_exp[half], t)
                        m = mx1[:, half * HP:(half + 1) * HP]
                        dve.tensor_reduce(m.rearrange("p (q h) -> p q h", q=2),
                                          psS1[:, 2 * half:2 * half + 2, 0:QK].rearrange("p q (h k) -> p q h k", k=LK),
                                          AX.X, ALU.max).then_inc(c_mx, 1)
                        dve.wait_ge(c_mx, 2 * t + (half + 1))
                        dve.tensor_scalar(m, m, -1.0 / (SX * SM), None, ALU.mult).then_inc(c_sub[half], 1)
                    return run

                def reciprocals(t, par):
                    dve.wait_ge(c_exp[0], t + 1)
                    dve.wait_ge(c_exp[1], t + 1)
                    dve.reciprocal(sum1[:, par, :], sum1[:, par, :]).then_inc(c_rcp, 1)

                def probs_low(n):
                    def run(t, par):
                        a_, b_ = CH[n]
                        dve.wait_ge(c_ph[n], t + 1)
                        rows = P if n < 2 else RR
                        ins = dve.scalar_tensor_tensor(pl1[0:rows, a_:b_, :], psP1[n % 2][0:rows, 0:b_ - a_, :], SP,
                                                       ph1[0:rows, a_:b_, :], ALU.mult, ALU.subtract)
                        ins.then_inc(c_pl[n], 1)
                    return run

                def residual(t, par):
                    row = X[:, bass.ds(t, 1), :].rearrange("p t d -> p (t d)")
                    dve.wait_ge(c_av[2], t + 1)
                    dve.wait_ge(c_bo, t + 1)
                    dve.scalar_tensor_tensor(row, psO1, thx1[:, 0:1], row, ALU.mult, ALU.add).then_inc(c_res, 1)
                    apart(dve, c_res, t + 1)
                    stats(1)(t, par)

                def router_sub(t, par):
                    dve.wait_ge(c_lg, t + 1)
                    dve.tensor_reduce(lmx[:], psL1[:, 0:E], AX.X, ALU.max).then_inc(c_lm, 1)
                    dve.wait_ge(c_lm, t + 1)
                    dve.tensor_scalar(lex[:, par, :], psL1[:, 0:E], lmx[:, 0:1], None, ALU.subtract).then_inc(c_ls, 1)

                def router_norm(t, par):
                    dve.wait_ge(c_le, t + 1)
                    dve.reciprocal(lsum[:, par, :], lsum[:, par, :]).then_inc(c_aff, 1)
                    dve.wait_ge(c_aff, 2 * t + 1)
                    tile = t % (S // P)
                    at = bass.ds(((tile % HT) * 2 + tile // HT) * (B * E) + (t // (S // P)) * E, E)
                    dve.tensor_scalar(afff[:, at], lex[:, par, :], lsum[:, par, :], None, ALU.mult).then_inc(c_aff, 1)
                HT = S // P // 2
                afff = aff[:].rearrange("p t h b e -> p (t h b e)")
                dve.tensor_scalar(thx1[:], th[:, 1:2], 1.0 / (SP * SV), None, ALU.mult).then_inc(c_one, 1)
                dve.wait_ge(c_one, 1)
                steps = dict(probs_low0=probs_low(0), probs_low1=probs_low(1), probs_low2=probs_low(2), maxima0=maxima(0),
                             maxima1=maxima(1), normalise_in=normalise(0), normalise_out=normalise(1), low_in=low(0),
                             low_out=low(1), router_sub=router_sub, combine=combine, residual=residual,
                             reciprocals=reciprocals, router_norm=router_norm)
                in_order(dve, steps, DVE_ORDER, T)

        CAP = 2 * (S // E)
        SLT = CAP // P
        GSC = 1.0 / (SH * SW)
        l1.close()
        r1.close()
        FT1 = F1 // P
        BS = 2 * CAP
        NT = BS // P
        NB1 = E * B // 2
        W1E = 2 * KD * F1 + FT1 * D
        UP1, DOWN1 = KD * F1, 2 * KD * F1
        f1 = ExitStack()
        W1h = sb("W1h", [P, 2, W1E], F16, f1)
        W1l = sb("W1l", [P, 2, W1E], F16, f1)
        w1s = sb("w1s", [P, 2, W1E // 2], F32, f1)
        gx = sb("gx", [P, 2, NT, D], F32, f1)
        gxh = sb("gxh", [P, 2, KD, BS], F16, f1)
        gxl = sb("gxl", [P, 2, KD, BS], F16, f1)
        sil1 = sb("sil1", [P, 2, BS], F32, f1)
        hid1 = sb("hid1", [P, 2, BS], F32, f1)
        hh1 = sb("hh1", [P, 2, FT1, BS], F16, f1)
        hl1 = sb("hl1", [P, 2, FT1, BS], F16, f1)
        yo1 = sb("yo1", [P, 2, NT, D], F32, f1)
        HB = 2 * B * E
        at_ = sb("at_", [HB, S // 2], F32, f1)
        tv = sb("tv", [HB, CAP], F32, f1)
        ti = sb("ti", [HB, CAP], U32, f1)
        tif = sb("tif", [HB, CAP], F32, f1)
        tvr = sb("tvr", [HB, CAP], F32, f1)
        tir = sb("tir", [HB, CAP], F32, f1)
        boff = sb("boff", [P, B * E], F32, f1)
        better = sb("better", [P, SLT, B * E], F32, f1)
        tok = sb("tok", [P, SLT, B * E], F32, f1)
        diff = sb("diff", [P, SLT, B * E], F32, f1)
        f1.close()
        pk = ExitStack()
        psA = ps("psA", [HB, S // 2], F32, pk)
        psV = ps("psV", [P, 4, SLT, HB], F32, pk)
        pk.close()
        pf = ExitStack()
        psXb = ps("psXb", [P, KD, BS], F32, pf)
        psG1 = [ps(f"psG1{n}", [P, BS], F32, pf) for n in range(2)]
        psU1 = [ps(f"psU1{n}", [P, BS], F32, pf) for n in range(2)]
        psYb = ps("psYb", [P, NT, D], F32, pf)
        pf.close()
        d_w = [sem(f"d_w{n}") for n in range(2)]
        d_first = sem("d_first")
        d_wh = sem("d_wh")
        d_wl = sem("d_wl")
        d_in = [sem(f"d_in{n}") for n in range(2)]
        d_xt = sem("d_xt")
        d_xh = sem("d_xh")
        d_xl = sem("d_xl")
        d_g = sem("d_g")
        d_sil = sem("d_sil")
        d_hid = sem("d_hid")
        d_hl = sem("d_hl")
        d_y = sem("d_y")
        d_yo = sem("d_yo")
        d_out = [sem(f"d_out{n}") for n in range(2)]
        DD = 4
        WC = W1E // 2 // FT1

        k_dve = sem("k_dve")
        k_off = sem("k_off")
        k_pe = sem("k_pe")
        ROUNDS = CAP // 8
        KSTEPS = 10 + 3 * ROUNDS

        def load_weights1(sp, j, half):
            src = a["w1"][bass.ds(j // 2, 1)].rearrange("e p w -> p (e w)") if not isinstance(j, int) else a["w1"][j // 2]
            sp.dma_start(w1s[:, half, :], src[:, half * (W1E // 2):(half + 1) * (W1E // 2)]).then_inc(d_w[half], 16)

        with nc.Block() as block:
            @block.sync
            def _(sp):
                for j in range(2):
                    load_weights1(sp, j, j)

            @block.scalar
            def _(act):
                for j in range(2):
                    act.wait_ge(d_w[j], 16)
                    act.activation(w1s[:, j, :], w1s[:, j, :], ACT.Copy, scale=SW).then_inc(d_first, 1)
                    act.wait_ge(d_first, 2 * j + 1)
                    act.activation(W1h[:, 0, j * (W1E // 2):(j + 1) * (W1E // 2)], w1s[:, j, :], ACT.Copy).then_inc(d_first, 1)

            @block.gpsimd
            def _(pool):
                pool.iota(boff[:], [[S, B], [0, E]], base=0, channel_multiplier=0,
                          allow_small_or_imprecise_dtypes=True).then_inc(k_off, 1)
                for j in range(2):
                    cols = slice(j * (W1E // 2), (j + 1) * (W1E // 2))
                    pool.wait_ge(d_first, 2 * j + 2)
                    pool.tensor_tensor(W1l[:, 0, cols], w1s[:, j, :], W1h[:, 0, cols], ALU.subtract)

            @block.tensor
            def _(pe):
                for t in range(S // P // 2):
                    last = pe.transpose(psA[:, t * P:(t + 1) * P], aff[:, t, :, :, :].rearrange("p h b e -> p (h b e)"), ident[:])
                last.then_inc(k_pe, 1)
                pe.wait_ge(k_dve, 3 + 3 * ROUNDS)
                for m, lists in enumerate((tv, tif, tvr, tir)):
                    for n in range(SLT):
                        last = pe.transpose(psV[:, m, n, :], lists[:, n * P:(n + 1) * P], ident[0:HB, 0:HB])
                last.then_inc(k_pe, 1)

            @block.vector
            def _(dve):
                ch = Chain(dve, k_dve, 0, KSTEPS)
                dve.wait_ge(k_pe, 1)
                ch(dve.tensor_copy(at_[:], psA[:]))
                for r in range(ROUNDS):
                    cols = slice(8 * r, 8 * r + 8)
                    ch(dve.max(tv[:, cols], at_[:]))
                    ch(dve.max_index(ti[:, cols], tv[:, cols], at_[:]))
                    ch(dve.match_replace(at_[:], tv[:, cols], at_[:], -1.0))
                ch(dve.tensor_copy(tif[:], ti[:]))
                dve.tensor_copy(tvr[:], tv[:, ::-1])
                ch(dve.tensor_copy(tir[:], tif[:, ::-1]))
                first, second = slice(0, B * E), slice(B * E, HB)
                dve.wait_ge(k_pe, 2)
                dve.wait_ge(k_off, 1)
                ch(dve.tensor_copy(gval[:], psV[:, 0, :, first]))
                ch(dve.tensor_tensor(better[:], gval[:], psV[:, 2, :, second], ALU.is_ge))
                dve.tensor_tensor(gval[:], gval[:], psV[:, 2, :, second], ALU.max)
                ch(dve.tensor_scalar(tok[:], psV[:, 3, :, second], float(S // 2), None, ALU.add))
                dve.tensor_scalar(gval[:], gval[:], th[:, 3:4], GSC, ALU.mult, ALU.mult)
                ch(dve.tensor_tensor(diff[:], psV[:, 1, :, first], tok[:], ALU.subtract))
                ch(dve.tensor_tensor(diff[:], diff[:], better[:], ALU.mult))
                ch(dve.tensor_tensor(tok[:], tok[:], diff[:], ALU.add))
                ch(dve.tensor_tensor(gidx[:], tok[:], boff[:].unsqueeze(1).to_broadcast([P, SLT, B * E]), ALU.add))
                ch.end()

        with nc.Block() as block:
            @block.sync
            def _(sp):
                def load(j, ph):
                    if isinstance(j, int) and j < 2:
                        return
                    wait(sp, d_wl, FT1 * (j - 3))
                    load_weights1(sp, j, ph % 2)
                pipeline(sp, NB1, 3, [(0, load)], unroll=2)

            @block.gpsimd
            def _(pool):
                def column(j, n):
                    e, q = j // 2, j % 2
                    return n % SLT, (2 * q + n // SLT) * E + e

                def gather(j, ph):
                    wait(pool, d_xt, j - 1)
                    for n in range(NT):
                        half, col = column(j, n)
                        pool.indirect_dma_start(gx[:, j % 2, n, :], None, n_rows[:, :],
                                                bass.IndirectOffsetOnAxis(gidx[:, half, col:col + 1], 0)).then_inc(d_in[j % 2], 16)

                def add(j, ph):
                    pool.wait_ge(d_yo, NT * j + NT)
                    wait(pool, d_out[j % 2], 16 * NT * (j // 2))
                    for n in range(NT):
                        half, col = column(j, n)
                        pool.indirect_dma_start(out_rows[:, :], bass.IndirectOffsetOnAxis(gidx[:, half, col:col + 1], 0),
                                                yo1[:, j % 2, n, :], None, compute_op=ALU.add).then_inc(d_out[j % 2], 16)
                pipeline(pool, NB1, DD, [(0, gather), (3, add)], straight=True)
                for n in range(2):
                    pool.wait_ge(d_out[n], 16 * NT * NB1 // 2)

            @block.tensor
            def _(pe):
                def transposes(j, ph):
                    par = ph % 2
                    pe.wait_ge(d_in[par], 16 * NT * (j // 2) + 16 * NT)
                    wait(pe, d_xl, KD * j)
                    for k in range(KD):
                        for n in range(NT):
                            last = pe.transpose(psXb[:, k, n * P:(n + 1) * P], gx[:, par, n, k * P:(k + 1) * P], ident[:])
                    last.then_inc(d_xt, 1)

                def up(j, ph):
                    par, wp = ph % 2, ph // 2
                    pe.wait_ge(d_xl, KD * j + KD)
                    wait(pe, d_wl, 2 * FT1 * (j // 2))
                    for f in range(FT1):
                        wait(pe, d_hid, 2 * FT1 * j + (2 * f - 3))
                        for psum, off in ((psG1, 0), (psU1, UP1)):
                            for k in range(KD):
                                at = off + k * F1 + f * P
                                last = mm3(pe, psum[f % 2][:], W1h[:, wp, at:at + P], W1l[:, wp, at:at + P], gxh[:, par, k, :],
                                           gxl[:, par, k, :], k == 0, k == KD - 1)
                        last.then_inc(d_g, 1)

                def down(j, ph):
                    par, wp = ph % 2, ph // 2
                    pe.wait_ge(d_hl, FT1 * j + FT1)
                    wait(pe, d_yo, NT * j)
                    for n in range(NT):
                        rows = slice(n * P, (n + 1) * P)
                        for f in range(FT1):
                            at = DOWN1 + f * D
                            last = mm3(pe, psYb[:, n, :], hh1[:, par, f, rows], hl1[:, par, f, rows], W1h[:, wp, at:at + D],
                                       W1l[:, wp, at:at + D], f == 0, f == FT1 - 1)
                    last.then_inc(d_y, 1)
                pipeline(pe, NB1, DD, [(2, up), (1, transposes), (3, down)], unroll=4)

            @block.scalar
            def _(act):
                def weights_high(f):
                    def run(j, ph):
                        half, wp = ph % 2, ph // 2
                        if isinstance(j, int) and j < 2:
                            return
                        if f == 0:
                            act.wait_ge(d_w[half], 16 * (j // 2) + 16)
                            wait(act, d_y, j - 3)
                        at = half * (W1E // 2) + f * WC
                        act.activation(W1h[:, wp, at:at + WC], w1s[:, half, f * WC:(f + 1) * WC], ACT.Copy, scale=SW)\
                           .then_inc(d_wh, 1)
                    return run

                def rows_high(j, ph):
                    par = ph % 2
                    act.wait_ge(d_xt, j + 1)
                    wait(act, d_g, FT1 * (j - 1))
                    for k in range(KD):
                        act.activation(gxh[:, par, k, :], psXb[:, k, :], ACT.Copy, scale=SX).then_inc(d_xh, 1)

                def silu(f):
                    def run(j, ph):
                        act.wait_ge(d_g, FT1 * j + (f + 1))
                        wait(act, d_hid, 2 * FT1 * j + (2 * f - 3))
                        act.activation(sil1[:, f % 2, :], psG1[f % 2][:], ACT.Silu, scale=1.0 / (SX * SW)).then_inc(d_sil, 1)
                    return run

                def results(j, ph):
                    par = ph % 2
                    act.wait_ge(d_y, j + 1)
                    if not isinstance(j, int) or j >= 2:
                        act.wait_ge(d_out[par], 16 * NT * (j // 2))
                    for n in range(NT):
                        col = bass.ds((n % SLT) * (B * E) + ((2 * par + n // SLT) * E) + j // 2, 1)
                        act.activation(yo1[:, par, n, :], psYb[:, n, :], ACT.Copy, scale=gvalf[:, col]).then_inc(d_yo, 1)
                gvalf = gval[:].rearrange("p n c -> p (n c)")
                work = [step for f in range(FT1) for step in ((2, silu(f)), (0, weights_high(f)))]
                pipeline(act, NB1, DD, work + [(1, rows_high), (3, results)], unroll=4)

            @block.vector
            def _(dve):
                def weights_low(f):
                    def run(j, ph):
                        half, wp = ph % 2, ph // 2
                        if isinstance(j, int) and j < 2:
                            return
                        at = half * (W1E // 2) + f * WC
                        dve.wait_ge(d_wh, FT1 * (j - 2) + (f + 1))
                        dve.scalar_tensor_tensor(W1l[:, wp, at:at + WC], w1s[:, half, f * WC:(f + 1) * WC], SW,
                                                 W1h[:, wp, at:at + WC], ALU.mult, ALU.subtract).then_inc(d_wl, 1)
                    return run

                def rows_low(j, ph):
                    par = ph % 2
                    for k in range(KD):
                        dve.wait_ge(d_xh, KD * j + (k + 1))
                        dve.scalar_tensor_tensor(gxl[:, par, k, :], psXb[:, k, :], SX, gxh[:, par, k, :],
                                                 ALU.mult, ALU.subtract).then_inc(d_xl, 1)

                def hidden(f):
                    def run(j, ph):
                        par = ph % 2
                        if f == 0:
                            wait(dve, d_y, j - 1)
                        dve.wait_ge(d_sil, FT1 * j + (f + 1))
                        dve.scalar_tensor_tensor(hid1[:, f % 2, :], psU1[f % 2][:], SH / (SX * SW), sil1[:, f % 2, :],
                                                 ALU.mult, ALU.mult).then_inc(d_hid, 1)
                        dve.wait_ge(d_hid, 2 * FT1 * j + (2 * f + 1))
                        dve.tensor_copy(hh1[:, par, f, :], hid1[:, f % 2, :]).then_inc(d_hid, 1)
                        dve.wait_ge(d_hid, 2 * FT1 * j + (2 * f + 2))
                        dve.tensor_tensor(hl1[:, par, f, :], hid1[:, f % 2, :], hh1[:, par, f, :], ALU.subtract)\
                           .then_inc(d_hl, 1)
                    return run
                work = [step for f in range(FT1) for step in ((2, hidden(f)), (0, weights_low(f)))]
                pipeline(dve, NB1, DD, work + [(1, rows_low)], unroll=4)


_SINGLE = {}


def kernel(**inputs):
    import numpy as np
    import concourse.bacc as bacc
    from concourse.bass_utils import run_bass_kernel_spmd

    def tiles(w, n):
        return w.reshape(n, P, -1).transpose(1, 0, 2)

    def experts(wa, wb, wd, f):
        e = wa.shape[0]
        up = [w.transpose(0, 2, 1).reshape(e, KD, P, f).transpose(0, 2, 1, 3).reshape(e, P, KD * f) for w in (wa, wb)]
        down = wd.transpose(0, 2, 1).reshape(e, f // P, P, D).transpose(0, 2, 1, 3).reshape(e, P, (f // P) * D)
        return np.concatenate(up + [down], axis=2)

    i = {k: np.asarray(v) for k, v in inputs.items()}
    arrays = {
        "x": i["x"],
        "ctxT": i["ctx_768"].reshape(NKEY, DC).T,
        "g_xattn": i["g_xattn"].reshape(1, 2),
        "g_ffn": i["g_ffn"].reshape(1, 2),
        "wk0": i["L0_xattn_Wk"],
        "wv0": i["L0_xattn_Wv"],
        "wqT0": i["L0_xattn_Wq"].T,
        "bq0": i["L0_xattn_bq"].reshape(KD, P).T,
        "bk0": i["L0_xattn_bk"].reshape(KD, P).T,
        "bv0": i["L0_xattn_bv"].reshape(1, D),
        "gate0": tiles(i["L0_ffn_gate_w"].T, KD),
        "wk1": i["L1_xattn_Wk"],
        "wv1": i["L1_xattn_Wv"],
        "wqT1": i["L1_xattn_Wq"].T,
        "wo1": i["L1_xattn_Wo"],
        "bo1": i["L1_xattn_bo"].reshape(1, D),
        "gate1": tiles(i["L1_ffn_gate_w"].T, KD),
        "w1": experts(i["L1_ffn_w_gate"], i["L1_ffn_w_up"], i["L1_ffn_w_down"], F1),
        "w0": experts(i["L0_ffn_w1"], i["L0_ffn_w3"], i["L0_ffn_w2"], F0),
    }
    arrays = {k: np.ascontiguousarray(v) for k, v in arrays.items()}
    nc = bacc.Bacc("TRN2", target_bir_lowering=False, num_devices=1)
    aps = {k: nc.dram_tensor("in_" + k, v.shape, F32, kind="ExternalInput").ap() for k, v in arrays.items()}
    out = nc.dram_tensor("out_x", (B, S, D), F32, kind="ExternalOutput").ap()
    x_rows = nc.dram_tensor("x_rows", ((E + 1) * REG, D), F32, kind="Internal").ap()
    y_rows = nc.dram_tensor("y_rows", (NB0 * BR, D), F32, kind="Internal").ap()
    n_rows = nc.dram_tensor("n_rows", (B * S, D), F32, kind="Internal").ap()
    program(nc, aps, out, x_rows, y_rows, n_rows)
    r = run_bass_kernel_spmd(nc, [{"in_" + k: v for k, v in arrays.items()}], core_ids=[0])
    return r.results[0]["out_x"]
```

```python
from contextlib import ExitStack

import concourse.bass as bass
from concourse import mybir

F32 = mybir.dt.float32
F16 = mybir.dt.float16
BF16 = mybir.dt.bfloat16
I32 = mybir.dt.int32
U32 = mybir.dt.uint32
ALU = mybir.AluOpType
ACT = mybir.ActivationFunctionType
AX = mybir.AxisListType

P = 128
B, S, D = 4, 1024, 256
LK, DC = 77, 192
NKEY = B * LK
T = B * S // P
KD = D // P
E = 8
F0 = 512
F1 = 1024
GT = 4
NG = T // GT
EPS = 1e-5

SX = 256.0
SW = 256.0
SM = 64.0
SV = 64.0
SP = 256.0
SH = 16.0

BR = 256
REG = B * S + BR
NB0 = (2 * B * S + E * (BR - 1)) // BR
W0E = 2 * KD * F0 + (F0 // P) * D


def wait(e, sem, value):
    if not isinstance(value, int) or value > 0:
        e.wait_ge(sem, value)


class Chain:

    def __init__(self, engine, sem, turn, steps):
        self.engine, self.sem, self.base, self.steps, self.n = engine, sem, turn * steps, steps, 0

    def __call__(self, ins):
        self.n += 1
        ins.then_inc(self.sem, 1)
        self.engine.wait_ge(self.sem, self.base + self.n)

    def end(self):
        assert self.n == self.steps, (self.n, self.steps)


def pipeline(e, n, depth, work, unroll=2, straight=False):
    def step(j, phase):
        for lag, fn in work:
            item = j - lag
            if isinstance(item, int) and not 0 <= item < n:
                continue
            fn(item, (phase - lag) % unroll)

    first = depth + 1
    turns = (n - first) // unroll
    if turns < 2 or straight:
        turns = 0
    for j in range(min(first, n + depth - 1)):
        step(j, j % unroll)
    if turns:
        with e.Fori(0, turns) as u:
            for c in range(unroll):
                step(u * unroll + (first + c), (first + c) % unroll)
    for j in range(first + turns * unroll, n + depth - 1):
        step(j, j % unroll)


def mm3(pe, o, lh, ll, rh, rl, first, stop):
    pe.matmul(o, lh, rh, start=first, stop=False)
    pe.matmul(o, lh, rl, start=False, stop=False)
    return pe.matmul(o, ll, rh, start=False, stop=stop)


def least(a, limit):
    return min(a, limit) if isinstance(a, int) else a


def in_order(e, steps, order, n, straight=False):
    pipeline(e, n, max(lag for _, lag in order) + 1, [(lag, steps[name]) for name, lag in order], straight=straight)


def before(item, mine, other, order, n):
    names = [name for name, _ in order]
    ahead = dict(order)[mine] - dict(order)[other] + (names.index(other) < names.index(mine))
    return least(item + ahead, n)


def program(nc, a, out, x_rows, y_rows, n_rows):
    ctx = ExitStack()
    with ctx:
        def sb(name, shape, dt=F32, on=ctx, side=None):
            return on.enter_context(nc.sbuf_tensor(name, shape, dt, side=side))

        def ps(name, shape, dt=F32, on=ctx):
            return on.enter_context(nc.psum_tensor(name, shape, dt))

        def sem(name):
            return ctx.enter_context(nc.semaphore(name))

        X = sb("X", [P, T, D])
        ident = sb("ident", [P, P])
        identh = sb("identh", [P, P], F16)
        th = sb("th", [P, 4])
        wts = sb("wts", [P, 2, T])
        islot = sb("islot", [P, 2, T], I32)
        aff = sb("aff", [P, S // P // 2, 2, B, E])
        gval = sb("gval", [P, 2 * S // E // P, B * E])
        gidx = sb("gidx", [P, 2 * S // E // P, B * E], I32)
        mhalf = sb("mhalf", [P, GT])

        l0 = ExitStack()
        Wh = sb("Wh", [P, E * W0E], F16, l0)
        Wl = sb("Wl", [P, E * W0E], F16, l0)
        blkrow = sb("blkrow", [P, NB0], I32, l0)
        blkw = sb("blkw", [P, NB0], I32, l0)
        padrow = sb("padrow", [P, E], I32, l0)
        a0 = ExitStack()
        stage = sb("stage", [P, 2, W0E], F32, a0)
        ctxT = stage[:, 0, 0:2 * NKEY].rearrange("p (k n) -> p k n", k=2)
        wk = stage[:, 0, 1024:1536].rearrange("p (k n) -> p k n", k=2)
        wv = stage[:, 0, 1536:2048].rearrange("p (k n) -> p k n", k=2)
        wqT = stage[:, 0, 2048:2560].rearrange("p (k n) -> p k n", k=2)
        KT = stage[:, 1, 0:2 * NKEY].rearrange("p (k n) -> p k n", k=2)
        bqs = sb("bqs", [P, KD], F32, a0)
        bks = sb("bks", [P, KD], F32, a0)
        bvs = sb("bvs", [1, D], F32, a0)
        gts = sb("gts", [P, KD, E], F32, a0)
        gth = sb("gth", [P, KD, E], F16, a0)
        gtl = sb("gtl", [P, KD, E], F16, a0)
        Mh = sb("Mh", [P, KD, NKEY], F16, a0)
        Ml = sb("Ml", [P, KD, NKEY], F16, a0)
        c0 = sb("c0", [1, NKEY], F32, a0)
        Vh = sb("Vh", [LK, B, D], F16, a0)
        Vl = sb("Vl", [LK, B, D], F16, a0)
        ones1 = sb("ones1", [1, P], F32, a0)
        trib = sb("trib", [P, P], BF16, a0)
        onesb = sb("onesb", [P, P], BF16, a0)
        iota8 = sb("iota8", [P, E], F32, a0)
        reg8 = sb("reg8", [P, E], F32, a0)
        thr = sb("thr", [P, E, 16], F32, a0)
        tri8 = sb("tri8", [P, E, E], F32, a0)
        iotaj = sb("iotaj", [P, NB0], F32, a0)
        base = sb("base", [P, E], F32, a0)
        st = [sb(f"st{n}", [P, GT, 6], F32, a0) for n in range(2)]
        mv = [sb(f"mv{n}", [P, 2, GT, 2], F32, a0) for n in range(2)]
        rstd = [sb(f"rstd{n}", [P, 2, GT], F32, a0) for n in range(2)]
        xa = sb("xa", [P, GT, D], F32, a0)
        xc = sb("xc", [P, 2, GT, D], F32, a0)
        xth = [sb(f"xth{n}", [P, 2, KD, GT * P], F16, a0) for n in range(2)]
        xtl = [sb(f"xtl{n}", [P, 2, KD, GT * P], F16, a0) for n in range(2)]
        smax = sb("smax", [P, GT], F32, a0)
        pr = sb("pr", [P, 2, GT, LK], F32, a0)
        ssum = sb("ssum", [P, GT], F32, a0)
        cf = sb("cf", [P, 2, GT], F32, a0)
        pth = sb("pth", [LK, GT * P], F16, a0)
        ptl = sb("ptl", [LK, GT * P], F16, a0)
        top = sb("top", [P, T, E], F32, a0)
        ix = sb("ix", [P, GT, E], U32, a0)
        ixf = sb("ixf", [P, GT, E], F32, a0)
        pick = sb("pick", [P, 2, T, E], F32, a0)
        both = sb("both", [P, GT, E], BF16, a0)
        rank = sb("rank", [P, T, E], F32, a0)
        prod = sb("prod", [P, 2, GT, E], F32, a0)
        slotf = sb("slotf", [P, 2, GT], F32, a0)
        slots = sb("slots", [P, 2, 2, GT], I32, a0)
        cnt = sb("cnt", [P, E], F32, a0)
        more = sb("more", [P, E, 16], F32, a0)
        nblk = sb("nblk", [P, E], F32, a0)
        tri8n = sb("tri8n", [P, E, E], F32, a0)
        cum = sb("cum", [P, E], F32, a0)
        adj = sb("adj", [P, E], F32, a0)
        done = sb("done", [P, NB0, E], F32, a0)
        done2 = sb("done2", [P, NB0, E], F32, a0)
        ej = sb("ej", [P, NB0], F32, a0)
        mj = sb("mj", [P, NB0], F32, a0)
        lt = sb("lt", [P, NB0], F32, a0)
        slotT = sb("slotT", [P, 2, T], F32, a0)

        pa = ExitStack()
        psT = ps("psT", [P, KD, GT * P], F32, pa)
        psS = ps("psS", [P, 512], F32, pa)
        psP = ps("psP", [P, GT * P], F32, pa)
        psO = ps("psO", [P, GT, D], F32, pa)
        psL = ps("psL", [P, 512], F32, pa)
        psR = ps("psR", [P, 512], F32, pa)
        pa.close()

        s_x = [sem(f"s_x{g}") for g in range(NG)]
        s_w = sem("s_w")
        s_setpe = sem("s_setpe")
        s_setact = sem("s_setact")
        s_vl = sem("s_vl")
        s_pc = sem("s_pc")
        out_rows = out.rearrange("b s d -> (b s) d")
        xv = a["x"].rearrange("b (t p) d -> p (b t) d", p=P)
        with nc.Block() as block:
            @block.sync
            def _(sp):
                sp.dma_start(ctxT[:, 0, :], a["ctxT"][0:P, :]).then_inc(s_w, 16)
                sp.dma_start(ctxT[0:DC - P, 1, :], a["ctxT"][P:DC, :]).then_inc(s_w, 16)
                for dst, name in ((wk, "wk0"), (wv, "wv0")):
                    sp.dma_start(dst[:, 0, :], a[name][0:P, :]).then_inc(s_w, 16)
                    sp.dma_start(dst[0:DC - P, 1, :], a[name][P:DC, :]).then_inc(s_w, 16)
                sp.dma_start(wqT, a["wqT0"].rearrange("(k p) d -> p k d", p=P)).then_inc(s_w, 16)
                sp.dma_start(bqs[:], a["bq0"]).then_inc(s_w, 16)
                sp.dma_start(bks[:], a["bk0"]).then_inc(s_w, 16)
                sp.dma_start(bvs[:], a["bv0"]).then_inc(s_w, 16)
                sp.dma_start(gts[:], a["gate0"]).then_inc(s_w, 16)
                sp.dma_start(th[:, 0:2], a["g_xattn"].partition_broadcast(P)).then_inc(s_w, 16)
                sp.dma_start(th[:, 2:4], a["g_ffn"].partition_broadcast(P)).then_inc(s_w, 16)
                for g in range(NG):
                    sp.dma_start(X[:, GT * g:GT * g + GT, :], xv[:, GT * g:GT * g + GT, :]).then_inc(s_x[g], 16)

            W_ALL = 13 * 16

            @block.gpsimd
            def _(pool):
                ch = Chain(pool, s_pc, 0, 9)
                ch(pool.memset(ident[:], 0.0))
                ch(pool.affine_select(out=ident[:], in_=ident[:], compare_op=ALU.not_equal, fill=1.0,
                                      base=0, pattern=[[-1, P]], channel_multiplier=1))
                pool.memset(ones1[:], 1.0)
                pool.memset(mhalf[:], -0.5)
                ch(pool.memset(onesb[:], 1.0))
                ch(pool.affine_select(out=trib[:], in_=onesb[:], compare_op=ALU.is_gt, fill=0.0,
                                      base=0, pattern=[[1, P]], channel_multiplier=-1))
                ch(pool.memset(tri8[:], 1.0))
                ch(pool.affine_select(out=tri8[:], in_=tri8[:], compare_op=ALU.is_ge, fill=0.0,
                                      base=0, pattern=[[1, E], [-1, E]], channel_multiplier=0))
                pool.iota(iota8[:], [[1, E]], base=0, channel_multiplier=0, allow_small_or_imprecise_dtypes=True)
                pool.iota(reg8[:], [[REG, E]], base=0, channel_multiplier=0, allow_small_or_imprecise_dtypes=True)
                ch(pool.iota(base[:], [[REG, E]], base=0, channel_multiplier=0, allow_small_or_imprecise_dtypes=True))
                ch(pool.iota(thr[:], [[0, E], [BR, 16]], base=0, channel_multiplier=0,
                             allow_small_or_imprecise_dtypes=True))
                ch(pool.iota(iotaj[:], [[1, NB0]], base=0, channel_multiplier=0, allow_small_or_imprecise_dtypes=True))
                ch.end()

            @block.tensor
            def _(pe):
                pe.wait_ge(s_w, W_ALL)
                pe.wait_ge(s_pc, 9)
                for m in range(KD):
                    pe.matmul(psT[:, m, 0:NKEY], wk[:, 0, m * P:(m + 1) * P], ctxT[:, 0, :], start=True, stop=False)
                    pe.matmul(psT[:, m, 0:NKEY], wk[0:DC - P, 1, m * P:(m + 1) * P], ctxT[0:DC - P, 1, :],
                              start=False, stop=True).then_inc(s_setpe, 1)
                pe.wait_ge(s_setact, 2)
                for m in range(KD):
                    o = (psS, psP)[m][:, 0:NKEY]
                    for k in range(KD):
                        last = pe.matmul(o, wqT[:, k, m * P:(m + 1) * P], KT[:, k, :], start=(k == 0), stop=(k == KD - 1))
                    last.then_inc(s_setpe, 1)
                for k in range(KD):
                    last = pe.matmul(psL[0:1, 0:NKEY], bqs[:, k:k + 1], KT[:, k, :], start=(k == 0), stop=(k == KD - 1))
                last.then_inc(s_setpe, 1)

            @block.scalar
            def _(act):
                for m in range(KD):
                    act.wait_ge(s_setpe, m + 1)
                    act.activation(KT[:, m, :], psT[:, m, 0:NKEY], ACT.Identity, bias=bks[:, m:m + 1]).then_inc(s_setact, 1)
                for m in range(KD):
                    act.wait_ge(s_setpe, 3 + m)
                    act.activation(Mh[:, m, :], (psS, psP)[m][:, 0:NKEY], ACT.Copy, scale=SM).then_inc(s_setact, 1)
                act.wait_ge(s_setpe, 5)
                act.activation(c0[:], psL[0:1, 0:NKEY], ACT.Copy, scale=SX * SM).then_inc(s_setact, 1)
                act.activation(gth[:], gts[:], ACT.Copy, scale=SW).then_inc(s_setact, 1)
                act.activation(th[:], th[:], ACT.Tanh).then_inc(s_setact, 1)

            @block.vector
            def _(dve):
                dve.wait_ge(s_pc, 2)
                dve.tensor_copy(identh[:], ident[:])
                for m in range(KD):
                    dve.wait_ge(s_setact, 3 + m)
                    dve.scalar_tensor_tensor(Ml[:, m, :], (psS, psP)[m][:, 0:NKEY], SM, Mh[:, m, :],
                                             ALU.mult, ALU.subtract)
                dve.wait_ge(s_setact, 6)
                dve.scalar_tensor_tensor(gtl[:], gts[:], SW, gth[:], ALU.mult, ALU.subtract)

        s_ws = [sem(f"s_ws{n}") for n in range(2)]
        s_we = sem("s_we")
        s_wh = sem("s_wh")
        s_wl = sem("s_wl")
        s_wp = sem("s_wp")
        s_st = [sem(f"s_st{n}") for n in range(2)]
        s_mv = [sem(f"s_mv{n}") for n in range(2)]
        s_rstd = [sem(f"s_rstd{n}") for n in range(2)]
        s_xn = [sem(f"s_xn{n}") for n in range(2)]
        s_xt = [sem(f"s_xt{n}") for n in range(2)]
        s_xh = [sem(f"s_xh{n}") for n in range(2)]
        s_xl = [sem(f"s_xl{n}") for n in range(2)]
        s_sc = sem("s_sc")
        s_smax = sem("s_smax")
        s_sub = sem("s_sub")
        s_exp = sem("s_exp")
        s_cf = sem("s_cf")
        s_pt = sem("s_pt")
        s_pth = sem("s_pth")
        s_ptl = sem("s_ptl")
        s_av = sem("s_av")
        s_res = sem("s_res")
        s_lg = sem("s_lg")
        s_cho = sem("s_cho")
        s_row = sem("s_row")
        s_both = sem("s_both")
        s_rk = sem("s_rk")
        s_slot = sem("s_slot")
        s_sct = [sem(f"s_sct{n}") for n in range(2)]
        s_zero = sem("s_zero")
        s_fin = sem("s_fin")
        s_blk = sem("s_blk")
        s_fin2 = sem("s_fin2")
        s_pad = sem("s_pad")
        HW = W0E // 2
        PE0_ORDER = [("attend", 2), ("scores", 1), ("logits", 3), ("transposes_in", 0), ("transpose_probs", 1), ("ranks",
                     3), ("transposes_out", 2)]
        ACT0_ORDER = [("high_out", 3), ("weights_high", 2), ("exps", 1), ("high_in", 0), ("probs_high", 1),
                      ("values_high", 0)]
        DVE0_ORDER = [("residual", 3), ("top_logits", 4), ("largest", 2), ("top_experts", 4), ("subtract", 2),
                      ("stats_out", 3), ("top_floats", 4), ("stats_in", 0), ("one_hot", 4), ("sums", 2), ("chosen", 4),
                      ("low_in", 1), ("add_base", 4), ("normalise_out", 3), ("own_ranks", 4), ("reciprocals", 2),
                      ("own_rows", 4), ("factors", 2), ("place", 4), ("probs_low", 2), ("weights_low", 3),
                      ("normalise_in", 0), ("low_out", 3), ("values_low", 0)]
        POOL0_ORDER = [("rstd_out", 3), ("weights_low", 3), ("rstd_in", 0), ("scatter", 4)]
        prodT = xa[:, 2:4, :].rearrange("p a (t e) -> p a t e", e=E)

        with nc.Block() as block:
            @block.sync
            def _(sp):
                def load_weights(g, par):
                    if g == 0:
                        sp.wait_ge(s_setpe, 5 + B)
                    wait(sp, s_wl, g - 1)
                    wait(sp, s_wp, g - 1)
                    sp.dma_start(stage[:, par, :], a["w0"][g]).then_inc(s_ws[par], 16)
                for g in range(E):
                    load_weights(g, g % 2)
                sp.wait_ge(s_zero, 1)
                sp.wait_ge(s_blk, 1)
                zeros = xa[:, 0:2, :]
                for e in range(E):
                    row = sp.value_load(padrow[0:1, e:e + 1], min_val=0, max_val=E * REG - BR)
                    sp.dma_start(x_rows[bass.ds(row, BR), :].rearrange("(n p) d -> p n d", p=P), zeros).then_inc(s_pad, 16)
                sp.dma_start(x_rows[E * REG:E * REG + BR, :].rearrange("(n p) d -> p n d", p=P), zeros).then_inc(s_pad, 16)
                sp.wait_ge(s_pad, 16 * (E + 1))

            @block.gpsimd
            def _(pool):
                def rstd_of(n):
                    def run(g, par):
                        pool.wait_ge(s_mv[n], GT * g + GT)
                        pool.tensor_scalar(rstd[n][:, par, :], mv[n][:, par, :, 1], EPS, None, ALU.add).then_inc(s_rstd[n], 1)
                        pool.wait_ge(s_rstd[n], 2 * g + 1)
                        pool.tensor_tensor(rstd[n][:, par, :], rstd[n][:, par, :], mhalf[:], ALU.pow).then_inc(s_rstd[n], 1)
                    return run

                def weights_low(g, par):
                    pool.wait_ge(s_wh, g + 1)
                    pool.tensor_tensor(Wl[:, bass.ds(g * W0E + HW, HW)], stage[:, par, HW:], Wh[:, bass.ds(g * W0E + HW, HW)],
                                       ALU.subtract).then_inc(s_wp, 1)

                def scatter(g, par):
                    pool.wait_ge(s_slot, g + 1)
                    for k in range(GT):
                        for c in range(2):
                            pool.indirect_dma_start(x_rows[:, :], bass.IndirectOffsetOnAxis(slots[:, par, c, k:k + 1], 0),
                                                    xc[:, par, k, :], None, bounds_check=E * REG - 1,
                                                    oob_is_err=True).then_inc(s_sct[par], 16)
                steps = dict(rstd_out=rstd_of(1), rstd_in=rstd_of(0), weights_low=weights_low, scatter=scatter)
                in_order(pool, steps, POOL0_ORDER, NG, straight=True)
                for n in range(2):
                    pool.wait_ge(s_sct[n], 16 * T)

            @block.scalar
            def _(act):
                def high(n):
                    def run(g, par):
                        wait(act, s_lg if n else s_sc, g - 1)
                        for k in range(KD):
                            act.wait_ge(s_xt[n], KD * g + k + 1)
                            act.activation(xth[n][:, par, k, :], psT[:, k, :], ACT.Copy, scale=SX).then_inc(s_xh[n], 1)
                    return run

                def weights_high(g, par):
                    act.wait_ge(s_ws[par], 16 * (g // 2) + 16)
                    act.activation(stage[:, par, :], stage[:, par, :], ACT.Copy, scale=SW).then_inc(s_we, 1)
                    act.wait_ge(s_we, g + 1)
                    act.activation(Wh[:, bass.ds(g * W0E, W0E)], stage[:, par, :], ACT.Copy).then_inc(s_wh, 1)

                def exps(g, par):
                    act.wait_ge(s_sub, g + 1)
                    act.activation(pr[:, par, :, :], pr[:, par, :, :], ACT.Exp, scale=1.0 / (SX * SM)).then_inc(s_exp, 1)

                def probs_high(g, par):
                    wait(act, s_av, g)
                    act.wait_ge(s_pt, g + 1)
                    act.activation(pth[:], psP[0:LK, :], ACT.Copy, scale=SP).then_inc(s_pth, 1)

                def values_high(g, par):
                    for b in range(B if g == 0 else 0):
                        act.wait_ge(s_setpe, 5 + b // 2 * 2 + 2)
                        act.activation(Vh[:, b, :], psO[0:LK, b, :], ACT.Copy, scale=SV).then_inc(s_setact, 1)

                steps = dict(high_in=high(0), high_out=high(1), exps=exps, probs_high=probs_high, weights_high=weights_high,
                             values_high=values_high)
                in_order(act, steps, ACT0_ORDER, NG, straight=True)
                act.wait_ge(s_fin, 1)
                act.activation(wts[:, 1, :], wts[:, 0, :], ACT.Exp, scale=1.0 / (SX * SW)).then_inc(s_fin, 1)

            @block.tensor
            def _(pe):
                def transposes(n):
                    def run(g, par):
                        pe.wait_ge(s_xn[n], GT * g + GT)
                        src = xa[:, :, :] if n == 0 else xc[:, par, :, :]
                        for k in range(KD):
                            mine, other = (("transposes_in", "transposes_out"), ("transposes_out", "transposes_in"))[n]
                            if g > 0:
                                pe.wait_ge(s_xl[n], KD * (g - 1) + k + 1)
                            begun = before(g, mine, other, PE0_ORDER, NG)
                            if begun > 0:
                                pe.wait_ge(s_xl[1 - n], KD * (begun - 1) + k + 1)
                            for i in range(GT):
                                last = pe.transpose(psT[:, k, i * P:(i + 1) * P], src[:, i, k * P:(k + 1) * P], ident[:])
                            last.then_inc(s_xt[n], 1)
                    return run

                def scores(g, par):
                    pe.wait_ge(s_xl[0], KD * g + KD)
                    wait(pe, s_sub, g)
                    b = g // 2
                    for i in range(GT):
                        o = psS[:, i * LK:(i + 1) * LK]
                        t = slice(i * P, (i + 1) * P)
                        keys = bass.ds(b * LK, LK)
                        pe.matmul(o, ones1[:], c0[:, keys], start=True, stop=False)
                        for k in range(KD):
                            last = mm3(pe, o, xth[0][:, par, k, t], xtl[0][:, par, k, t], Mh[:, k, keys], Ml[:, k, keys],
                                       False, k == KD - 1)
                    last.then_inc(s_sc, 1)

                def transpose_probs(g, par):
                    pe.wait_ge(s_exp, g + 1)
                    wait(pe, s_ptl, g)
                    for i in range(GT):
                        last = pe.transpose(psP[0:LK, i * P:(i + 1) * P], pr[:, par, i, :], ident[:])
                    last.then_inc(s_pt, 1)

                def attend(g, par):
                    pe.wait_ge(s_ptl, g + 1)
                    wait(pe, s_res, GT * g)
                    if g == 0:
                        pe.wait_ge(s_vl, B)
                    vb = bass.ds((g // 2) * D, D)
                    for i in range(GT):
                        t = slice(i * P, (i + 1) * P)
                        last = mm3(pe, psO[:, i, :], pth[:, t], ptl[:, t], Vh2[:, vb], Vl2[:, vb], True, True)
                    last.then_inc(s_av, 1)

                def logits(g, par):
                    pe.wait_ge(s_xl[1], KD * g + KD)
                    wait(pe, s_cho, 4 * g - 2)
                    for i in range(GT):
                        t = slice(i * P, (i + 1) * P)
                        for k in range(KD):
                            last = mm3(pe, psL[:, i * E:(i + 1) * E], xth[1][:, par, k, t], xtl[1][:, par, k, t],
                                       gth[:, k, :], gtl[:, k, :], k == 0, k == KD - 1)
                    last.then_inc(s_lg, 1)

                def ranks(g, par):
                    pe.wait_ge(s_both, g + 1)
                    wait(pe, s_row, 4 * g - 2)
                    for i in range(GT + 1):
                        o = psR[:, i * E:(i + 1) * E]
                        for j in range(min(i, GT)):
                            last = pe.matmul(o, onesb[:], both[:, j, :], start=(j == 0), stop=(i == GT and j == GT - 1))
                        if i < GT:
                            last = pe.matmul(o, trib[:], both[:, i, :], start=(i == 0), stop=True)
                    last.then_inc(s_rk, 1)
                Vh2 = Vh[:, :, :].rearrange("p b d -> p (b d)")
                Vl2 = Vl[:, :, :].rearrange("p b d -> p (b d)")
                for b in range(B):
                    o = psO[0:LK, b, :]
                    pe.matmul(o, ctxT[:, 0, b * LK:(b + 1) * LK], wv[:, 0, :], start=True, stop=False)
                    pe.matmul(o, ctxT[0:DC - P, 1, b * LK:(b + 1) * LK], wv[0:DC - P, 1, :], start=False, stop=False)
                    pe.matmul(o, ones1[0:1, 0:LK], bvs[:], start=False, stop=True).then_inc(s_setpe, 1)
                steps = dict(transposes_in=transposes(0), transposes_out=transposes(1), scores=scores,
                             transpose_probs=transpose_probs, attend=attend, logits=logits, ranks=ranks)
                in_order(pe, steps, PE0_ORDER, NG, straight=True)

            @block.vector
            def _(dve):
                def stats(n):
                    def run(g, par):
                        if n == 0:
                            dve.wait_ge(s_x[g], 16)
                        else:
                            dve.wait_ge(s_res, GT * g + GT)
                        rows = X[:, bass.ds(GT * g, GT), :]
                        for i in range(GT):
                            dve.bn_stats(st[n][:, i, :], rows[:, i, :]).then_inc(s_st[n], 1)
                        for i in range(GT):
                            dve.wait_ge(s_st[n], GT * g + i + 1)
                            dve.bn_aggr(mv[n][:, par, i, :], st[n][:, i, :]).then_inc(s_mv[n], 1)
                    return run

                def normalise(n):
                    def run(g, par):
                        rows = X[:, bass.ds(GT * g, GT), :]
                        dve.wait_ge(s_rstd[n], 2 * g + 2)
                        if n == 0:
                            wait(dve, s_xt[0], KD * g)
                        else:
                            wait(dve, s_sct[par], 16 * 2 * GT * (g // 2))
                        for i in range(GT):
                            dst = xa[:, i, :] if n == 0 else xc[:, par, i, :]
                            dve.tensor_scalar(dst, rows[:, i, :], mv[n][:, par, i, 0:1], rstd[n][:, par, i:i + 1],
                                              ALU.subtract, ALU.mult).then_inc(s_xn[n], 1)
                    return run

                def low(n):
                    def run(g, par):
                        for k in range(KD):
                            dve.wait_ge(s_xh[n], KD * g + k + 1)
                            dve.scalar_tensor_tensor(xtl[n][:, par, k, :], psT[:, k, :], SX, xth[n][:, par, k, :],
                                                     ALU.mult, ALU.subtract).then_inc(s_xl[n], 1)
                    return run

                scores4 = psS[:, 0:GT * LK].rearrange("p (i k) -> p i k", i=GT)

                def largest(g, par):
                    dve.wait_ge(s_sc, g + 1)
                    dve.tensor_reduce(smax[:], scores4, AX.X, ALU.max).then_inc(s_smax, 1)

                def subtract(g, par):
                    dve.wait_ge(s_smax, g + 1)
                    wait(dve, s_pt, g - 1)
                    dve.tensor_tensor(pr[:, par, :, :], scores4, smax[:].unsqueeze(2).to_broadcast([P, GT, LK]),
                                      ALU.subtract).then_inc(s_sub, 1)

                def sums(g, par):
                    dve.wait_ge(s_exp, g + 1)
                    dve.tensor_reduce(ssum[:], pr[:, par, :, :], AX.X, ALU.add).then_inc(s_cf, 1)

                def reciprocals(g, par):
                    dve.wait_ge(s_cf, 3 * g + 1)
                    dve.reciprocal(ssum[:], ssum[:]).then_inc(s_cf, 1)

                def factors(g, par):
                    dve.wait_ge(s_cf, 3 * g + 2)
                    dve.tensor_scalar(cf[:, par, :], ssum[:], th[:, 0:1], 1.0 / (SP * SV), ALU.mult, ALU.mult).then_inc(s_cf, 1)

                def probs_low(g, par):
                    dve.wait_ge(s_pth, g + 1)
                    dve.scalar_tensor_tensor(ptl[:], psP[0:LK, :], SP, pth[:], ALU.mult, ALU.subtract).then_inc(s_ptl, 1)

                def residual(g, par):
                    dve.wait_ge(s_av, g + 1)
                    dve.wait_ge(s_cf, 3 * g + 3)
                    rows = X[:, bass.ds(GT * g, GT), :]
                    for i in range(GT):
                        dve.scalar_tensor_tensor(rows[:, i, :], psO[:, i, :], cf[:, par, i:i + 1], rows[:, i, :],
                                                 ALU.mult, ALU.add).then_inc(s_res, 1)

                def weights_low(g, par):
                    dve.wait_ge(s_wh, g + 1)
                    dve.tensor_tensor(Wl[:, bass.ds(g * W0E, HW)], stage[:, par, 0:HW], Wh[:, bass.ds(g * W0E, HW)],
                                      ALU.subtract).then_inc(s_wl, 1)

                def top_logits(g, par):
                    dve.wait_ge(s_lg, g + 1)
                    for i in range(GT):
                        last = dve.max(top[:, GT * g + i, :], psL[:, i * E:(i + 1) * E])
                    last.then_inc(s_cho, 1)

                def top_experts(g, par):
                    dve.wait_ge(s_cho, 4 * g + 1)
                    for i in range(GT):
                        last = dve.max_index(ix[:, i, :], top[:, GT * g + i, :], psL[:, i * E:(i + 1) * E])
                    last.then_inc(s_cho, 1)

                def top_floats(g, par):
                    dve.wait_ge(s_cho, 4 * g + 2)
                    dve.tensor_copy(ixf[:], ix[:]).then_inc(s_cho, 1)

                def one_hot(g, par):
                    dve.wait_ge(s_cho, 4 * g + 3)
                    for c in range(2):
                        last = dve.tensor_tensor(pick[:, c, GT * g:GT * g + GT, :], iota8[:].unsqueeze(1).to_broadcast([P, GT, E]),
                                                 ixf[:, :, c:c + 1].to_broadcast([P, GT, E]), ALU.is_equal)
                    last.then_inc(s_cho, 1)

                def chosen(g, par):
                    dve.wait_ge(s_cho, 4 * g + 4)
                    wait(dve, s_rk, g)
                    tiles = slice(GT * g, GT * g + GT)
                    dve.tensor_tensor(both[:], pick[:, 0, tiles, :], pick[:, 1, tiles, :], ALU.add).then_inc(s_both, 1)

                def add_base(g, par):
                    tiles = slice(GT * g, GT * g + GT)
                    dve.wait_ge(s_rk, g + 1)
                    dve.tensor_tensor(rank[:, tiles, :], psR[:, 0:GT * E].rearrange("p (i e) -> p i e", i=GT),
                                      base[:].unsqueeze(1).to_broadcast([P, GT, E]), ALU.add).then_inc(s_row, 1)
                    dve.wait_ge(s_row, 4 * g + 1)
                    dve.tensor_tensor(base[:], base[:], psR[:, GT * E:GT * E + E], ALU.add).then_inc(s_row, 1)

                def own_ranks(g, par):
                    dve.wait_ge(s_row, 4 * g + 2)
                    for c in range(2):
                        last = dve.tensor_tensor(prod[:, c, :, :], rank[:, GT * g:GT * g + GT, :], pick[:, c, GT * g:GT * g + GT, :],
                                                 ALU.mult)
                    last.then_inc(s_row, 1)

                def own_rows(g, par):
                    dve.wait_ge(s_row, 4 * g + 3)
                    wait(dve, s_slot, g)
                    dve.tensor_reduce(slotf[:], prod[:], AX.X, ALU.add).then_inc(s_row, 1)

                def place(g, par):
                    dve.wait_ge(s_row, 4 * g + 4)
                    wait(dve, s_sct[par], 16 * 2 * GT * (g // 2))
                    dve.tensor_copy(slots[:, par, :, :], slotf[:]).then_inc(s_slot, 1)

                def values_low(g, par):
                    for b in range(B if g == 0 else 0):
                        dve.wait_ge(s_setact, 7 + b // 2 * 2 + 2)
                        dve.scalar_tensor_tensor(Vl[:, b, :], psO[0:LK, b, :], SV, Vh[:, b, :], ALU.mult, ALU.subtract)\
                           .then_inc(s_vl, 1)

                steps = dict(values_low=values_low, stats_in=stats(0), stats_out=stats(1), normalise_in=normalise(0), normalise_out=normalise(1),
                             low_in=low(0), low_out=low(1), largest=largest, subtract=subtract, sums=sums,
                             reciprocals=reciprocals, factors=factors, top_logits=top_logits, top_experts=top_experts,
                             top_floats=top_floats, one_hot=one_hot, chosen=chosen, add_base=add_base, own_ranks=own_ranks,
                             own_rows=own_rows, place=place,
                             probs_low=probs_low, residual=residual, weights_low=weights_low)
                in_order(dve, steps, DVE0_ORDER, NG, straight=True)

                dve.wait_ge(s_xt[0], KD * NG)
                dve.memset(xa[:, 0:2, :], 0.0).then_inc(s_zero, 1)

                ch = Chain(dve, s_blk, 0, 18)
                ch(dve.tensor_copy(padrow[:], base[:]))
                ch(dve.tensor_tensor(cnt[:], base[:], reg8[:], ALU.subtract))
                ch(dve.tensor_tensor(more[:], cnt[:].unsqueeze(2).to_broadcast([P, E, 16]), thr[:], ALU.is_gt))
                ch(dve.tensor_reduce(nblk[:], more[:], AX.X, ALU.add))
                ch(dve.tensor_tensor(tri8n[:], tri8[:], nblk[:].unsqueeze(1).to_broadcast([P, E, E]), ALU.mult))
                ch(dve.tensor_reduce(cum[:], tri8n[:], AX.X, ALU.add))
                ch(dve.tensor_tensor(adj[:], cum[:], nblk[:], ALU.subtract))
                ch(dve.scalar_tensor_tensor(adj[:], adj[:], float(BR), reg8[:], ALU.mult, ALU.subtract))
                jj = iotaj[:].unsqueeze(2).to_broadcast([P, NB0, E])
                ch(dve.tensor_tensor(done[:], cum[:].unsqueeze(1).to_broadcast([P, NB0, E]), jj, ALU.is_le))
                ch(dve.tensor_reduce(ej[:], done[:], AX.X, ALU.add))
                ch(dve.tensor_tensor(done2[:], done[:], nblk[:].unsqueeze(1).to_broadcast([P, NB0, E]), ALU.mult))
                ch(dve.tensor_reduce(mj[:], done2[:], AX.X, ALU.add))
                ch(dve.tensor_tensor(mj[:], iotaj[:], mj[:], ALU.subtract))
                ch(dve.tensor_scalar(lt[:], ej[:], float(E), float(BR), ALU.is_lt, ALU.mult))
                ch(dve.tensor_tensor(mj[:], mj[:], lt[:], ALU.mult))
                ch(dve.scalar_tensor_tensor(lt[:], ej[:], float(REG), mj[:], ALU.mult, ALU.add))
                ch(dve.tensor_scalar(ej[:], ej[:], float(E - 1), float(W0E), ALU.min, ALU.mult))
                dve.tensor_copy(blkrow[:], lt[:])
                ch(dve.tensor_copy(blkw[:], ej[:]))
                ch.end()

                ch = Chain(dve, s_fin2, 0, 8)
                ch(dve.tensor_tensor(wts[:, 0, :], top[:, :, 1], top[:, :, 0], ALU.subtract))
                dve.tensor_copy(smax[:], smax[:]).then_inc(s_fin, 1)
                ch(dve.tensor_tensor(rank[:], rank[:], adj[:].unsqueeze(1).to_broadcast([P, T, E]), ALU.add))
                for c in range(2):
                    last = dve.tensor_tensor(prodT[:, c, :, :], rank[:], pick[:, c, :, :], ALU.mult)
                ch(last)
                ch(dve.tensor_reduce(slotT[:], prodT, AX.X, ALU.add))
                dve.tensor_copy(islot[:], slotT[:])
                dve.wait_ge(s_fin, 2)
                ch(dve.tensor_scalar(wts[:, 0, :], wts[:, 1, :], 1.0, None, ALU.add))
                ch(dve.reciprocal(wts[:, 0, :], wts[:, 0, :]))
                ch(dve.tensor_tensor(wts[:, 1, :], wts[:, 1, :], wts[:, 0, :], ALU.mult))
                ch(dve.tensor_scalar(wts[:], wts[:], th[:, 2:3], None, ALU.mult))
                ch.end()
        a0.close()

        FT = F0 // P
        HF = FT // 2
        UP, DOWN = KD * F0, 2 * KD * F0
        e0 = ExitStack()
        bx = sb("bx", [P, 2, 2, D], F32, e0)
        bxh = sb("bxh", [P, 2, KD, BR], F16, e0)
        bxl = sb("bxl", [P, 2, KD, BR], F16, e0)
        sil = sb("sil", [P, 2, HF, BR], F32, e0)
        hid = sb("hid", [P, 2, HF, BR], F32, e0)
        hh = sb("hh", [P, 2, FT, BR], F16, e0)
        hl = sb("hl", [P, 2, FT, BR], F16, e0)
        yo = sb("yo", [P, 2, 2, D], F32, e0)
        H, DH = 16, 64
        HP = H // 2
        SK = 64.0
        r1 = ExitStack()
        gth1 = sb("gth1", [P, KD, E], F16, r1, "right")
        gtl1 = sb("gtl1", [P, KD, E], F16, r1, "right")
        bo = sb("bo", [P, D], F32, r1, "right")
        gts1 = sb("gts1", [P, KD, E], F32, r1, "right")
        thx1 = sb("thx1", [P, 1], F32, r1, "right")
        yg = sb("yg", [P, 2, 2, D], F32, r1, "right")
        r2 = ExitStack()
        PIECES = [("ctx1", "ctxT", NKEY, SK), ("wk1", "wk1", H * DH, SW), ("wv1", "wv1", H * DH, SW),
                  ("wq1", "wqT1", D, SW), ("wo1", "wo1", D, SW)]
        tiles_of = {"ctx1": 2, "wk1": 2, "wv1": 2, "wq1": HP, "wo1": HP}
        split1 = {name: [sb(f"{name}{part}", [P, tiles_of[name] * cols], F16, r2, "right") for part in "hl"]
                  for name, _, cols, _ in PIECES}
        r3 = ExitStack()
        raw1 = sb("raw1", [P, HP * D], F32, r3, "right")
        r3.close()
        e0.close()

        def regions(i):
            name, _, cols, _ = PIECES[i]
            n = tiles_of[name]
            return [(P, 0, n * cols)] if n == HP else [(P, 0, cols), (DC - P, cols, 2 * cols)]

        pe0 = ExitStack()
        psX = [ps(f"psX{n}", [P, KD, BR], F32, pe0) for n in range(2)]
        psG = [ps(f"psG{n}", [P, HF, BR], F32, pe0) for n in range(2)]
        psU = [ps(f"psU{n}", [P, HF, BR], F32, pe0) for n in range(2)]
        psY = [ps(f"psY{n}", [P, 2, D], F32, pe0) for n in range(2)]
        pe0.close()
        b_in = [sem(f"b_in{n}") for n in range(2)]
        b_xt = sem("b_xt")
        b_xh = sem("b_xh")
        b_xl = sem("b_xl")
        b_g = [sem(f"b_g{n}") for n in range(2)]
        b_sil = [sem(f"b_sil{n}") for n in range(2)]
        b_hid = [sem(f"b_hid{n}") for n in range(2)]
        b_hl = [sem(f"b_hl{n}") for n in range(2)]
        b_y = sem("b_y")
        b_yo = sem("b_yo")
        b_out = [sem(f"b_out{n}") for n in range(2)]
        BDEPTH = 4
        b_w1 = sem("b_w1")
        b_w1h = sem("b_w1h")
        b_w1l = sem("b_w1l")
        FIRST_PIECE = 4
        PEEL = FIRST_PIECE + len(PIECES)

        def piece_of(j):
            i = j - FIRST_PIECE if isinstance(j, int) else -1
            return i if 0 <= i < len(PIECES) else None

        with nc.Block() as block:
            @block.sync
            def _(sp):
                def load(j, par):
                    wait(sp, b_xt, j - 1)
                    row = sp.value_load(blkrow[0:1, bass.ds(j, 1)], min_val=0, max_val=E * REG)
                    sp.dma_start(bx[:, par, :, :], x_rows[bass.ds(row, BR), :].rearrange("(n p) d -> p n d", p=P))\
                      .then_inc(b_in[par], 16)

                def store(j, par):
                    sp.wait_ge(b_yo, j + 1)
                    sp.dma_start(y_rows[bass.ds(j * BR, BR), :].rearrange("(n p) d -> p n d", p=P), yo[:, par, :, :])\
                      .then_inc(b_out[par], 16)

                def load_piece(j, par):
                    i = piece_of(j)
                    if i is None:
                        return
                    name, src, cols, _ = PIECES[i]
                    wait(sp, b_w1l, i)
                    for rows, c0_, c1_ in regions(i):
                        if tiles_of[name] == HP:
                            sp.dma_start(raw1[:].rearrange("p (k d) -> p k d", d=D), a[src].rearrange("(k p) d -> p k d", p=P))\
                              .then_inc(b_w1, 16)
                        else:
                            sp.dma_start(raw1[0:rows, c0_:c1_], a[src][(c0_ // cols) * P:(c0_ // cols) * P + rows, :])\
                              .then_inc(b_w1, 16)
                sp.dma_start(gts1[:], a["gate1"]).then_inc(b_w1, 16)
                sp.dma_start(bo[:], a["bo1"].partition_broadcast(P)).then_inc(b_w1, 16)
                pipeline(sp, NB0, PEEL, [(0, load), (3, store), (0, load_piece)])
                sp.wait_ge(b_out[0], 16 * ((NB0 + 1) // 2))
                sp.wait_ge(b_out[1], 16 * (NB0 // 2))

            @block.tensor
            def _(pe):
                def transposes(j, par):
                    pe.wait_ge(b_in[par], 16 * (j // 2) + 16)
                    wait(pe, b_xl, j - 1)
                    for k in range(KD):
                        for n in range(2):
                            last = pe.transpose(psX[par][:, k, n * P:(n + 1) * P], bx[:, par, n, k * P:(k + 1) * P], ident[:])
                    last.then_inc(b_xt, 1)

                def up(j, par):
                    w = pe.value_load(blkw[0:1, bass.ds(j, 1)], min_val=0, max_val=(E - 1) * W0E)
                    pe.wait_ge(b_xl, j + 1)
                    for half in range(2):
                        wait(pe, b_hid[half], 2 * j)
                        for psum, off in ((psG, 0), (psU, UP)):
                            for f in range(HF):
                                for k in range(KD):
                                    at = bass.ds(w + (off + k * F0 + (half * HF + f) * P), P)
                                    last = mm3(pe, psum[half][:, f, :], Wh[:, at], Wl[:, at], bxh[:, par, k, :],
                                               bxl[:, par, k, :], k == 0, k == KD - 1)
                        last.then_inc(b_g[half], 1)

                def down(j, par):
                    w = pe.value_load(blkw[0:1, bass.ds(j, 1)], min_val=0, max_val=(E - 1) * W0E)
                    for half in range(2):
                        pe.wait_ge(b_hl[half], j + 1)
                    wait(pe, b_yo, j - 1)
                    for n in range(2):
                        rows = slice(n * P, (n + 1) * P)
                        for f in range(FT):
                            at = bass.ds(w + (DOWN + f * D), D)
                            last = mm3(pe, psY[par][:, n, :], hh[:, par, f, rows], hl[:, par, f, rows], Wh[:, at], Wl[:, at],
                                       f == 0, f == FT - 1)
                    last.then_inc(b_y, 1)
                pipeline(pe, NB0, BDEPTH, [(2, up), (1, transposes), (3, down)])

            @block.scalar
            def _(act):
                def rows_high(j, par):
                    act.wait_ge(b_xt, j + 1)
                    wait(act, b_g[1], j - 1)
                    act.activation(bxh[:, par, :, :], psX[par][:, :, :], ACT.Copy, scale=SX).then_inc(b_xh, 1)

                def silu(j, par):
                    for half in range(2):
                        act.wait_ge(b_g[half], j + 1)
                        act.activation(sil[:, half, :, :], psG[half][:, :, :], ACT.Silu, scale=1.0 / (SX * SW))\
                           .then_inc(b_sil[half], 1)

                def results(j, par):
                    act.wait_ge(b_y, j + 1)
                    if not isinstance(j, int) or j >= 2:
                        act.wait_ge(b_out[par], 16 * (j // 2))
                    act.activation(yo[:, par, :, :], psY[par][:, :, :], ACT.Copy, scale=1.0 / (SH * SW)).then_inc(b_yo, 1)

                def high_piece(j, par):
                    i = piece_of(j)
                    if i is None:
                        return
                    name, _, _, scale = PIECES[i]
                    act.wait_ge(b_w1, 32 + 16 * sum(len(regions(n)) for n in range(i + 1)))
                    for rows, c0_, c1_ in regions(i):
                        ins = act.activation(split1[name][0][0:rows, c0_:c1_], raw1[0:rows, c0_:c1_], ACT.Copy, scale=scale)
                    ins.then_inc(b_w1h, 1)
                pipeline(act, NB0, PEEL, [(2, silu), (1, rows_high), (3, results), (1, high_piece)])

            @block.vector
            def _(dve):
                def rows_low(j, par):
                    dve.wait_ge(b_xh, j + 1)
                    dve.scalar_tensor_tensor(bxl[:, par, :, :], psX[par][:, :, :], SX, bxh[:, par, :, :],
                                             ALU.mult, ALU.subtract).then_inc(b_xl, 1)

                def hidden(j, par):
                    wait(dve, b_y, j - 1)
                    for half in range(2):
                        f = slice(half * HF, (half + 1) * HF)
                        dve.wait_ge(b_sil[half], j + 1)
                        dve.scalar_tensor_tensor(hid[:, half, :, :], psU[half][:, :, :], SH / (SX * SW), sil[:, half, :, :],
                                                 ALU.mult, ALU.mult).then_inc(b_hid[half], 1)
                        dve.wait_ge(b_hid[half], 2 * j + 1)
                        dve.tensor_copy(hh[:, par, f, :], hid[:, half, :, :]).then_inc(b_hid[half], 1)
                        dve.wait_ge(b_hid[half], 2 * j + 2)
                        dve.tensor_tensor(hl[:, par, f, :], hid[:, half, :, :], hh[:, par, f, :], ALU.subtract)\
                           .then_inc(b_hl[half], 1)

                def low_piece(j, par):
                    i = piece_of(j)
                    if i is None:
                        return
                    name, _, _, scale = PIECES[i]
                    dve.wait_ge(b_w1h, i + 1)
                    for rows, c0_, c1_ in regions(i):
                        ins = dve.scalar_tensor_tensor(split1[name][1][0:rows, c0_:c1_], raw1[0:rows, c0_:c1_], scale,
                                                       split1[name][0][0:rows, c0_:c1_], ALU.mult, ALU.subtract)
                    ins.then_inc(b_w1l, 1)
                pipeline(dve, NB0, PEEL, [(2, hidden), (1, rows_low), (1, low_piece)])

        l0.close()

        CK = H * LK
        KM, KR = P // 2, LK - P // 2
        NC = HP + 2
        QK = CK // 4
        SM1 = SM * DH ** -0.5
        l1 = ExitStack()
        M1h = sb("M1h", [P, B, KD, CK], F16, l1)
        M1l = sb("M1l", [P, B, KD, CK], F16, l1)
        N1 = sb("N1", [P, B, NC, 2 * D], F16, l1)
        u1 = ExitStack()
        K1 = [sb(f"K1{part}", [P, HP, 2, NKEY], F16, u1) for part in "hl"]
        V1 = [sb(f"V1{part}", [P, HP, B, P], F16, u1) for part in "hl"]
        V2 = [sb(f"V2{part}", [P, HP, B, P], F16, u1) for part in "hl"]
        u1.close()
        r2.close()
        pu = ExitStack()
        psM = [ps(f"psM{n}", [P, 512], F32, pu) for n in range(4)]
        psN = [ps(f"psN{n}", [P, 2, D], F32, pu) for n in range(4)]
        pu.close()
        u_p = sem("u_p")
        u_ph = sem("u_ph")
        u_pl = sem("u_pl")
        u_m = sem("u_m")
        u_mh = sem("u_mh")
        u_ml = sem("u_ml")
        u_n = sem("u_n")
        u_nh = sem("u_nh")
        u_nl = sem("u_nl")
        u_z = sem("u_z")
        u_z2 = sem("u_z2")
        u_g = sem("u_g")
        c_y = [sem(f"c_y{n}") for n in range(2)]

        def gather_y(pool, t):
            for c in range(2):
                pool.indirect_dma_start(yg[:, t % 2, c, :], None, y_rows[:, :],
                                        bass.IndirectOffsetOnAxis(islot[:, c, t:t + 1], 0)).then_inc(c_y[t % 2], 16)

        halves = (slice(0, DH), slice(DH, P))
        psNf = [p[:, :, :].rearrange("p a d -> p (a d)") for p in psN]

        def keys_of(psum, rows, first, n):
            return psum[rows, 0:NKEY].rearrange("p (b k) -> p b k", b=B)[:, :, first:first + n]

        N_TURNS = ((0, 1), (2, 3, 4))

        def in_v2(m, odd):
            at = ((m % (HP // 2)) * 2 + odd) * KR
            return slice(at, at + KR)

        with nc.Block() as block:
            @block.gpsimd
            def _(pool):
                for i in range(2):
                    pool.memset(K1[i][DH:P, :, 0, :], 0.0)
                    pool.memset(K1[i][0:DH, :, 1, :], 0.0)
                    pool.memset(V1[i][DH:P, :, :, 0:KM], 0.0)
                    pool.memset(V1[i][0:DH, :, :, KM:P], 0.0).then_inc(u_z, 1)
                for t in range(2):
                    gather_y(pool, t)

            @block.tensor
            def _(pe):
                cth, ctl = split1["ctx1"]
                for m in range(HP):
                    for turn, (name, psum) in enumerate((("wk1", psM), ("wv1", psN))):
                        wh, wl = split1[name]
                        o = psum[m % 4][:, :] if psum is psM else psum[m % 4][:, :, :].rearrange("p a d -> p (a d)")
                        wait(pe, u_pl, 2 * (m - 4) + turn + 1)
                        for rows, k in ((P, 0), (DC - P, 1)):
                            at = k * H * DH + m * P
                            last = mm3(pe, o[:, 0:NKEY], wh[0:rows, at:at + P], wl[0:rows, at:at + P],
                                       cth[0:rows, k * NKEY:(k + 1) * NKEY], ctl[0:rows, k * NKEY:(k + 1) * NKEY], k == 0, k == 1)
                        last.then_inc(u_p, 1)
                pe.wait_ge(u_pl, 2 * HP)
                wqh, wql = split1["wq1"]
                woh, wol = split1["wo1"]
                pe.wait_ge(u_z, 2)
                for b in range(B):
                    keys = slice(b * LK, (b + 1) * LK)
                    for m in range(KD):
                        for bank in range(4):
                            wait(pe, u_ml, (KD * b + m - 1) * 4 + bank + 1)
                            for i in range(2):
                                pair = 2 * bank + i
                                at = pair * D + m * P
                                last = mm3(pe, psM[bank][:, i * 2 * LK:(i + 1) * 2 * LK].rearrange("p (h k) -> p h k", h=2),
                                           wqh[:, at:at + P], wql[:, at:at + P], K1[0][:, pair, :, keys], K1[1][:, pair, :, keys],
                                           True, True)
                            last.then_inc(u_m, 1)
                        for v in N_TURNS[m]:
                            wait(pe, u_nl, 5 * b + v - 3)
                            o = psN[(5 * b + v) % 4]
                            for i in range(2):
                                if v < 4:
                                    pair = 2 * v + i
                                    last = mm3(pe, o[:, i, :], V1[0][:, pair, b, :], V1[1][:, pair, b, :],
                                               woh[:, pair * D:(pair + 1) * D], wol[:, pair * D:(pair + 1) * D], True, True)
                                    continue
                                first = i * (HP // 2)
                                for pair in range(first, first + HP // 2):
                                    last = mm3(pe, o[:, i, :], V2[0][:, pair, b, :], V2[1][:, pair, b, :],
                                               woh[:, pair * D:(pair + 1) * D], wol[:, pair * D:(pair + 1) * D],
                                               pair == first, pair == first + HP // 2 - 1)
                            last.then_inc(u_n, 1)

            @block.scalar
            def _(act):
                for m in range(HP):
                    act.wait_ge(u_p, 2 * m + 1)
                    for odd, rows in enumerate(halves):
                        ins = act.activation(K1[0][rows, m, odd, :], psM[m % 4][rows, 0:NKEY], ACT.Copy, scale=1.0 / SW)
                    ins.then_inc(u_ph, 1)
                    act.wait_ge(u_p, 2 * m + 2)
                    wait(act, u_z2, 1 if m == 0 else 0)
                    for odd, rows in enumerate(halves):
                        act.activation(V1[0][rows, m, :, odd * KM:(odd + 1) * KM], keys_of(psNf[m % 4], rows, 0, KM), ACT.Copy,
                                       scale=1.0 / SW)
                        ins = act.activation(V2[0][rows, m, :, in_v2(m, odd)], keys_of(psNf[m % 4], rows, KM, KR), ACT.Copy,
                                             scale=1.0 / SW)
                    ins.then_inc(u_ph, 1)
                act.activation(gth1[:], gts1[:], ACT.Copy, scale=SW).then_inc(u_g, 1)

                for b in range(B):
                    for m in range(KD):
                        for bank in range(4):
                            act.wait_ge(u_m, 4 * (KD * b + m) + bank + 1)
                            act.activation(M1h[:, b, m, bank * QK:(bank + 1) * QK], psM[bank][:, 0:QK], ACT.Copy,
                                           scale=SM1 / (SK * SW)).then_inc(u_mh, 1)
                        for v in N_TURNS[m]:
                            act.wait_ge(u_n, 5 * b + (v + 1))
                            act.activation(N1[:, b, 2 * v:2 * v + 2, 0:D], psN[(5 * b + v) % 4][:, :, :], ACT.Copy,
                                           scale=SV / (SK * SW)).then_inc(u_nh, 1)

            @block.vector
            def _(dve):
                for v2 in V2:
                    ins = dve.memset(v2[:], 0.0)
                ins.then_inc(u_z2, 1)
                dve.tensor_scalar(bo[:], bo[:], th[:, 1:2], None, ALU.mult)
                dve.wait_ge(u_z2, 1)
                for m in range(HP):
                    dve.wait_ge(u_ph, 2 * m + 1)
                    for odd, rows in enumerate(halves):
                        ins = dve.scalar_tensor_tensor(K1[1][rows, m, odd, :], psM[m % 4][rows, 0:NKEY], 1.0 / SW,
                                                       K1[0][rows, m, odd, :], ALU.mult, ALU.subtract)
                    ins.then_inc(u_pl, 1)
                    dve.wait_ge(u_ph, 2 * m + 2)
                    for odd, rows in enumerate(halves):
                        part = slice(odd * KM, (odd + 1) * KM)
                        dve.scalar_tensor_tensor(V1[1][rows, m, :, part], keys_of(psNf[m % 4], rows, 0, KM), 1.0 / SW,
                                                 V1[0][rows, m, :, part], ALU.mult, ALU.subtract)
                        part = in_v2(m, odd)
                        ins = dve.scalar_tensor_tensor(V2[1][rows, m, :, part], keys_of(psNf[m % 4], rows, KM, KR), 1.0 / SW,
                                                       V2[0][rows, m, :, part], ALU.mult, ALU.subtract)
                    ins.then_inc(u_pl, 1)
                dve.wait_ge(u_g, 1)
                dve.scalar_tensor_tensor(gtl1[:], gts1[:], SW, gth1[:], ALU.mult, ALU.subtract)

                for b in range(B):
                    for m in range(KD):
                        for bank in range(4):
                            dve.wait_ge(u_mh, (KD * 4) * b + (4 * m + bank + 1))
                            dve.scalar_tensor_tensor(M1l[:, b, m, bank * QK:(bank + 1) * QK], psM[bank][:, 0:QK], SM1 / (SK * SW),
                                                     M1h[:, b, m, bank * QK:(bank + 1) * QK],
                                                     ALU.mult, ALU.subtract).then_inc(u_ml, 1)
                        for v in N_TURNS[m]:
                            dve.wait_ge(u_nh, 5 * b + (v + 1))
                            dve.scalar_tensor_tensor(N1[:, b, 2 * v:2 * v + 2, D:2 * D], psN[(5 * b + v) % 4][:, :, :],
                                                     SV / (SK * SW), N1[:, b, 2 * v:2 * v + 2, 0:D],
                                                     ALU.mult, ALU.subtract).then_inc(u_nl, 1)

        m1 = ExitStack()
        st1 = [sb(f"st1{n}", [P, 6], F32, m1) for n in range(2)]
        mv1 = [sb(f"mv1{n}", [P, 2, 2], F32, m1) for n in range(2)]
        rs1 = [sb(f"rs1{n}", [P, 2, 1], F32, m1) for n in range(2)]
        xn1 = [sb(f"xn1{n}", [P, 2, D], F32, m1) for n in range(2)]
        xh1 = sb("xh1", [P, 2, KD, P], F16, m1)
        xl1 = sb("xl1", [P, 2, KD, P], F16, m1)
        xs1 = sb("xs1", [P, 2, 2, D], F16, m1)
        xt1 = sb("xt1", [P, 2, KD, 2, P], F16, m1)
        mx1 = sb("mx1", [P, H], F32, m1)
        pr1 = sb("pr1", [P, 2, CK], F32, m1)
        pn1 = sb("pn1", [P, 2, NC * P], F32, m1)
        sum1 = sb("sum1", [P, 2, H], F32, m1)
        ps1 = sb("ps1", [P, 2, 2, NC * P], F16, m1)
        pt1 = sb("pt1", [P, NC, 2, P], F16, m1)
        lmx = sb("lmx", [P, 1], F32, m1)
        lex = sb("lex", [P, 2, E], F32, m1)
        lsum = sb("lsum", [P, 2, 1], F32, m1)
        m1.close()
        pm1 = ExitStack()
        psS1 = ps("psS1", [P, 4, 512], F32, pm1)
        psXar = ps("psXar", [P, 2, KD * P], F32, pm1)
        psXa = psXar[:, 0, :].rearrange("p (k n) -> p k n", k=KD)
        psXr = psXar[:, 1, :].bitcast(F16).rearrange("p (k a n) -> p k a n", k=KD, a=2)
        psP1 = [ps(f"psP1{n}", [P, 4, 2, P], F16, pm1) for n in range(2)]
        psOL = ps("psOL", [P, 2, D], F32, pm1)
        psO1, psL1 = psOL[:, 0, :], psOL[:, 1, :]
        pm1.close()
        CH = [(0, 4), (4, 8), (8, NC)]
        c_comb = sem("c_comb")
        c_mv = [sem(f"c_mv{n}") for n in range(2)]
        c_rs = [sem(f"c_rs{n}") for n in range(2)]
        c_xn = [sem(f"c_xn{n}") for n in range(2)]
        c_xt = [sem(f"c_xt{n}") for n in range(2)]
        c_xh = sem("c_xh")
        c_xl = sem("c_xl")
        c_sh = sem("c_sh")
        c_sl = sem("c_sl")
        c_xe = sem("c_xe")
        c_bo = sem("c_bo")
        c_sc = [sem(f"c_sc{n}") for n in range(2)]
        c_mx = [sem(f"c_mx{n}") for n in range(2)]
        c_sub = [sem(f"c_sub{n}") for n in range(2)]
        c_exp = [sem(f"c_exp{n}") for n in range(2)]
        c_rcp = sem("c_rcp")
        c_pn = sem("c_pn")
        c_ph = sem("c_ph")
        c_pl = sem("c_pl")
        c_pt = [sem(f"c_pt{n}") for n in range(3)]
        c_pe = [sem(f"c_pe{n}") for n in range(3)]
        c_av = [sem(f"c_av{n}") for n in range(3)]
        c_res = sem("c_res")
        c_lg = sem("c_lg")
        c_lm = sem("c_lm")
        c_ls = sem("c_ls")
        c_le = sem("c_le")
        c_aff = sem("c_aff")
        c_one = sem("c_one")
        c_tick = sem("c_tick")
        c_out = [sem(f"c_out{n}") for n in range(2)]

        PE_ORDER = [("scores1", 1), ("turn0", 3), ("logits", 5), ("turn1", 3), ("scores0", 1), ("transposes_in", 0),
                    ("outputs0", 3), ("turn2", 3), ("outputs1", 3), ("transposes_out", 4), ("outputs2", 3)]
        ACT_ORDER = [("exps0", 2), ("exps1", 1), ("router_exp", 5), ("high_out", 4), ("high_in", 0), ("probs_high", 2),
                     ("copy_out", 4)]
        DVE_ORDER = [("largest1", 2), ("normalise_in", 1), ("maxima1", 2), ("router_max", 6), ("reciprocals", 3),
                     ("copy_probs0", 4), ("combine0", 0), ("router_sub", 6), ("copy_probs1", 4), ("combine1", 0),
                     ("normalise_out", 5), ("stats_in", 0), ("router_reciprocal", 7), ("largest0", 2), ("low_in", 1),
                     ("low_out", 5), ("copy_probs2", 4), ("moments_in", 0), ("maxima0", 2), ("router_norm", 7),
                     ("probs_low", 3), ("residual", 4), ("stats_out", 4), ("moments_out", 4)]
        POOL_ORDER = [("normalise_probs", 4), ("add_bias", 3), ("gather", 0), ("rstd_in", 1), ("rstd_out", 5)]

        def apart(e, sem_, value):
            wait(e, sem_, value)
            if not isinstance(value, int):
                e.sem_inc(c_tick, 1)

        with nc.Block() as block:
            @block.sync
            def _(sp):
                def store(t, par):
                    sp.wait_ge(c_sl, t + 1)
                    sp.dma_start(out_rows[bass.ds(t * P, P), :], X[:, bass.ds(t, 1), :].rearrange("p t d -> p (t d)"))\
                      .then_inc(c_out[par], 16)
                    sp.dma_start(n_rows[bass.ds(t * P, P), :], xs1[:, bass.ds(par, 1), :, :].rearrange("p n a d -> p (n a d)"))\
                      .then_inc(c_out[par], 16)
                pipeline(sp, T, 1, [(0, store)])
                for n in range(2):
                    sp.wait_ge(c_out[n], 16 * T)

            @block.gpsimd
            def _(pool):
                def rstd_of(n):
                    def run(t, par):
                        pool.wait_ge(c_mv[n], 2 * t + 2)
                        pool.tensor_scalar(rs1[n][:, par, :], mv1[n][:, par, 1:2], EPS, None, ALU.add).then_inc(c_rs[n], 1)
                        pool.wait_ge(c_rs[n], 2 * t + 1)
                        pool.tensor_tensor(rs1[n][:, par, :], rs1[n][:, par, :], mhalf[:, 0:1], ALU.pow).then_inc(c_rs[n], 1)
                    return run

                def normalise_probs(t, par):
                    if t < 2:
                        for c in range(HP, NC):
                            pool.memset(pn1[:, par, c * P + HP * KR:(c + 1) * P], 0.0)
                    pool.wait_ge(c_rcp, t + 1)
                    wait(pool, c_pl, t - 1)
                    p = pr1[:, par, :].rearrange("p (h k) -> p h k", h=H)
                    r = sum1[:, par, :].unsqueeze(2)
                    pool.tensor_tensor(pn1[:, par, 0:H * KM].rearrange("p (h k) -> p h k", h=H), p[:, :, 0:KM],
                                       r.to_broadcast([P, H, KM]), ALU.mult)
                    for n in range(2):
                        heads = slice(n * HP, (n + 1) * HP)
                        at = (HP + n) * P
                        ins = pool.tensor_tensor(pn1[:, par, at:at + HP * KR].rearrange("p (h k) -> p h k", h=HP),
                                                 p[:, heads, KM:LK], r[:, heads, :].to_broadcast([P, HP, KR]), ALU.mult)
                    ins.then_inc(c_pn, 1)

                def gather(t, par):
                    if t < 2:
                        return
                    pool.wait_ge(c_comb, 2 * (t - 1))
                    gather_y(pool, t)

                def add_bias(t, par):
                    pool.wait_ge(c_xn[0], t + 1)
                    pool.tensor_tensor(X[:, t, :], X[:, t, :], bo[:], ALU.add).then_inc(c_bo, 1)
                steps = dict(gather=gather, add_bias=add_bias, rstd_out=rstd_of(1), rstd_in=rstd_of(0),
                             normalise_probs=normalise_probs)
                in_order(pool, steps, POOL_ORDER, T, straight=True)

            @block.scalar
            def _(act):
                def high_in(t, par):
                    wait(act, c_sc[0], t - 1)
                    wait(act, c_sc[1], t - 1)
                    act.wait_ge(c_xt[0], t + 1)
                    act.activation(xh1[:, par, :, :], psXa, ACT.Copy, scale=SX).then_inc(c_xh, 1)

                def high_out(t, par):
                    act.wait_ge(c_xn[1], t + 1)
                    wait(act, c_xt[1], t - 1)
                    if not isinstance(t, int) or t >= 2:
                        act.wait_ge(c_out[par], 32 * (t // 2))
                    act.activation(xs1[:, par, 0, :], xn1[1][:, par, :], ACT.Copy, scale=SX).then_inc(c_sh, 1)

                def copy_out(t, par):
                    act.wait_ge(c_xt[1], t + 1)
                    wait(act, c_lg, t - 1)
                    act.activation(xt1[:, par, :, :, :], psXr, ACT.Copy).then_inc(c_xe, 1)

                def probs_high(t, par):
                    act.wait_ge(c_pn, t + 1)
                    for n in range(3):
                        wait(act, c_pt[n], t - 1)
                    act.activation(ps1[:, par, 0, :], pn1[:, par, :], ACT.Copy, scale=SP).then_inc(c_ph, 1)

                def exps(half):
                    def run(t, par):
                        act.wait_ge(c_sub[half], t + 1)
                        wait(act, c_pn, t - 1)
                        for q in (2 * half, 2 * half + 1):
                            for i in range(4):
                                h = 4 * q + i
                                ins = act.activation(pr1[:, par, h * LK:(h + 1) * LK], psS1[:, q, i * LK:(i + 1) * LK], ACT.Exp,
                                                     bias=mx1[:, h:h + 1], scale=1.0 / (SX * SM), accum_out=sum1[:, par, h:h + 1])
                        ins.then_inc(c_exp[half], 1)
                    return run

                def router_exp(t, par):
                    act.wait_ge(c_ls, t + 1)
                    act.activation(lex[:, par, :], lex[:, par, :], ACT.Exp, scale=1.0 / (SX * SW),
                                   accum_out=lsum[:, par, :]).then_inc(c_le, 1)
                steps = dict(high_in=high_in, high_out=high_out, copy_out=copy_out, exps0=exps(0), exps1=exps(1),
                             router_exp=router_exp, probs_high=probs_high)
                in_order(act, steps, ACT_ORDER, T)

            @block.tensor
            def _(pe):
                def transposes(n):
                    def run(t, par):
                        read = (c_xl, c_xe)
                        pe.wait_ge((c_xn[0], c_sl)[n], t + 1)
                        wait(pe, read[n], t)
                        wait(pe, read[1 - n], before(t, *(("transposes_out", "transposes_in") if n else
                                                          ("transposes_in", "transposes_out")), PE_ORDER, T))
                        for k in range(KD):
                            cols = slice(k * P, (k + 1) * P)
                            if n == 0:
                                last = pe.transpose(psXa[:, k, :], xn1[0][:, par, cols], ident[:])
                                continue
                            for part in range(2):
                                last = pe.transpose(psXr[:, k, part, :], xs1[:, par, part, cols], identh[:])
                        last.then_inc(c_xt[n], 1)
                    return run

                def scores(half):
                    def run(t, par):
                        pe.wait_ge(c_xl, t + 1)
                        wait(pe, c_exp[half], t)
                        for q in (2 * half, 2 * half + 1):
                            for k in range(KD):
                                at = bass.ds((t // (S // P)) * (KD * CK) + (k * CK + q * QK), QK)
                                last = mm3(pe, psS1[:, q, 0:QK], xh1[:, par, k, :], xl1[:, par, k, :],
                                           M1hf[:, at], M1lf[:, at], k == 0, k == KD - 1)
                        last.then_inc(c_sc[half], 1)
                    return run

                def logits(t, par):
                    pe.wait_ge(c_xe, t + 1)
                    wait(pe, c_ls, t)
                    wait(pe, c_res, before(t, "logits", "outputs0", PE_ORDER, T))
                    for k in range(KD):
                        last = mm3(pe, psL1[:, 0:E], xt1[:, par, k, 0, :], xt1[:, par, k, 1, :], gth1[:, k, :], gtl1[:, k, :],
                                   k == 0, k == KD - 1)
                    last.then_inc(c_lg, 1)

                def turn(n):
                    def run(t, par):
                        pe.wait_ge(c_pl, t + 1)
                        a_, b_ = CH[n]
                        wait(pe, c_pe[(2, 1, 0)[n]], t + 1 if n == 2 else t)
                        for c in range(a_, b_):
                            for part in range(2):
                                ins = pe.transpose(psP1[n % 2][:, c - a_, part, :], ps1[:, par, part, c * P:(c + 1) * P], identh[:])
                        ins.then_inc(c_pt[n], 1)
                    return run

                def outputs(n):
                    def run(t, par):
                        a_, b_ = CH[n]
                        pe.wait_ge(c_pe[n], t + 1)
                        if n == 0:
                            wait(pe, c_res, t)
                            wait(pe, c_ls, before(t, "outputs0", "logits", PE_ORDER, T))
                        for c in range(a_, b_):
                            at = (t // (S // P)) * (NC * 2 * D) + c * 2 * D
                            ins = mm3(pe, psO1, pt1[:, c, 0, :], pt1[:, c, 1, :], N1f[:, bass.ds(at, D)],
                                      N1f[:, bass.ds(at + D, D)], c == 0, c == NC - 1)
                        ins.then_inc(c_av[n], 1)
                    return run
                M1hf = M1h[:].rearrange("p b k c -> p (b k c)")
                M1lf = M1l[:].rearrange("p b k c -> p (b k c)")
                N1f = N1[:].rearrange("p b c d -> p (b c d)")
                steps = dict(transposes_in=transposes(0), transposes_out=transposes(1), scores0=scores(0), scores1=scores(1),
                             turn0=turn(0), turn1=turn(1), turn2=turn(2), logits=logits,
                             outputs0=outputs(0), outputs1=outputs(1), outputs2=outputs(2))
                in_order(pe, steps, PE_ORDER, T)

            @block.vector
            def _(dve):
                def combine(c):
                    def run(t, par):
                        row = X[:, bass.ds(t, 1), :].rearrange("p t d -> p (t d)")
                        if c:
                            apart(dve, c_comb, 2 * t + 1)
                        else:
                            dve.wait_ge(c_y[par], 32 * (t // 2) + 32)
                        dve.scalar_tensor_tensor(row, yg[:, par, c, :], wts[:, c, bass.ds(t, 1)], row, ALU.mult, ALU.add)\
                           .then_inc(c_comb, 1)
                    return run

                def stats(n):
                    def run(t, par):
                        row = X[:, bass.ds(t, 1), :].rearrange("p t d -> p (t d)")
                        apart(dve, (c_comb, c_res)[n], (2 * t + 2, t + 1)[n])
                        dve.bn_stats(st1[n][:], row).then_inc(c_mv[n], 1)
                    return run

                def moments(n):
                    def run(t, par):
                        apart(dve, c_mv[n], 2 * t + 1)
                        dve.bn_aggr(mv1[n][:, par, :], st1[n][:]).then_inc(c_mv[n], 1)
                    return run

                def normalise(n):
                    def run(t, par):
                        row = X[:, bass.ds(t, 1), :].rearrange("p t d -> p (t d)")
                        dve.wait_ge(c_rs[n], 2 * t + 2)
                        if n == 0:
                            wait(dve, c_xt[0], t - 1)
                        dve.tensor_scalar(xn1[n][:, par, :], row, mv1[n][:, par, 0:1], rs1[n][:, par, :],
                                          ALU.subtract, ALU.mult).then_inc(c_xn[n], 1)
                    return run

                def low_in(t, par):
                    dve.wait_ge(c_xh, t + 1)
                    dve.scalar_tensor_tensor(xl1[:, par, :, :], psXa, SX, xh1[:, par, :, :],
                                             ALU.mult, ALU.subtract).then_inc(c_xl, 1)

                def low_out(t, par):
                    dve.wait_ge(c_sh, t + 1)
                    dve.scalar_tensor_tensor(xs1[:, par, 1, :], xn1[1][:, par, :], SX, xs1[:, par, 0, :],
                                             ALU.mult, ALU.subtract).then_inc(c_sl, 1)

                def probs_low(t, par):
                    dve.wait_ge(c_ph, t + 1)
                    dve.scalar_tensor_tensor(ps1[:, par, 1, :], pn1[:, par, :], SP, ps1[:, par, 0, :],
                                             ALU.mult, ALU.subtract).then_inc(c_pl, 1)

                def largest(half):
                    def run(t, par):
                        dve.wait_ge(c_sc[half], t + 1)
                        wait(dve, c_exp[half], t)
                        dve.tensor_reduce(mx1[:, half * HP:(half + 1) * HP].rearrange("p (q h) -> p q h", q=2),
                                          psS1[:, 2 * half:2 * half + 2, 0:QK].rearrange("p q (h k) -> p q h k", k=LK),
                                          AX.X, ALU.max).then_inc(c_mx[half], 1)
                    return run

                def maxima(half):
                    def run(t, par):
                        m = mx1[:, half * HP:(half + 1) * HP]
                        dve.wait_ge(c_mx[half], t + 1)
                        dve.tensor_scalar(m, m, -1.0 / (SX * SM), None, ALU.mult).then_inc(c_sub[half], 1)
                    return run

                def reciprocals(t, par):
                    dve.wait_ge(c_exp[0], t + 1)
                    dve.wait_ge(c_exp[1], t + 1)
                    dve.reciprocal(sum1[:, par, :], sum1[:, par, :]).then_inc(c_rcp, 1)

                def copy_probs(n):
                    def run(t, par):
                        a_, b_ = CH[n]
                        dve.wait_ge(c_pt[n], t + 1)
                        wait(dve, c_av[n], t)
                        dve.tensor_copy(pt1[:, a_:b_, :, :], psP1[n % 2][:, 0:b_ - a_, :, :]).then_inc(c_pe[n], 1)
                    return run

                def residual(t, par):
                    row = X[:, bass.ds(t, 1), :].rearrange("p t d -> p (t d)")
                    dve.wait_ge(c_av[2], t + 1)
                    dve.wait_ge(c_bo, t + 1)
                    dve.scalar_tensor_tensor(row, psO1, thx1[:, 0:1], row, ALU.mult, ALU.add).then_inc(c_res, 1)

                def router_max(t, par):
                    dve.wait_ge(c_lg, t + 1)
                    dve.tensor_reduce(lmx[:], psL1[:, 0:E], AX.X, ALU.max).then_inc(c_lm, 1)

                def router_sub(t, par):
                    dve.wait_ge(c_lm, t + 1)
                    dve.tensor_scalar(lex[:, par, :], psL1[:, 0:E], lmx[:, 0:1], None, ALU.subtract).then_inc(c_ls, 1)

                def router_reciprocal(t, par):
                    dve.wait_ge(c_le, t + 1)
                    dve.reciprocal(lsum[:, par, :], lsum[:, par, :]).then_inc(c_aff, 1)

                def router_norm(t, par):
                    dve.wait_ge(c_aff, 2 * t + 1)
                    tile = t % (S // P)
                    at = bass.ds(((tile % HT) * 2 + tile // HT) * (B * E) + (t // (S // P)) * E, E)
                    dve.tensor_scalar(afff[:, at], lex[:, par, :], lsum[:, par, :], None, ALU.mult).then_inc(c_aff, 1)
                HT = S // P // 2
                afff = aff[:].rearrange("p t h b e -> p (t h b e)")
                dve.tensor_scalar(thx1[:], th[:, 1:2], 1.0 / (SP * SV), None, ALU.mult).then_inc(c_one, 1)
                dve.wait_ge(c_one, 1)
                steps = dict(copy_probs0=copy_probs(0), copy_probs1=copy_probs(1), copy_probs2=copy_probs(2), probs_low=probs_low,
                             largest0=largest(0), largest1=largest(1), maxima0=maxima(0), maxima1=maxima(1),
                             normalise_in=normalise(0), normalise_out=normalise(1), stats_in=stats(0), stats_out=stats(1),
                             moments_in=moments(0), moments_out=moments(1), low_in=low_in, low_out=low_out,
                             router_max=router_max, router_sub=router_sub, router_reciprocal=router_reciprocal,
                             router_norm=router_norm, combine0=combine(0), combine1=combine(1), residual=residual,
                             reciprocals=reciprocals)
                in_order(dve, steps, DVE_ORDER, T)

        CAP = 2 * (S // E)
        SLT = CAP // P
        GSC = 1.0 / (SH * SW)
        l1.close()
        r1.close()
        FT1 = F1 // P
        BS = 2 * CAP
        NT = BS // P
        NB1 = E * B // 2
        W1E = 2 * KD * F1 + FT1 * D
        UP1, DOWN1 = KD * F1, 2 * KD * F1
        f1 = ExitStack()
        W1h = sb("W1h", [P, 2, W1E], F16, f1)
        W1l = sb("W1l", [P, 2, W1E], F16, f1)
        w1s = sb("w1s", [P, 2, W1E // 2], F32, f1)
        gx = sb("gx", [P, 2, NT, 2 * D], F16, f1)
        gxh = sb("gxh", [P, 2, KD, BS], F16, f1)
        gxl = sb("gxl", [P, 2, KD, BS], F16, f1)
        sil1 = sb("sil1", [P, 2, BS], F32, f1)
        hid1 = sb("hid1", [P, 2, BS], F32, f1)
        hh1 = sb("hh1", [P, 2, FT1, BS], F16, f1)
        hl1 = sb("hl1", [P, 2, FT1, BS], F16, f1)
        yo1 = sb("yo1", [P, 2, NT, D], F32, f1)
        HB = 2 * B * E
        at_ = sb("at_", [HB, S // 2], F32, f1)
        tv = sb("tv", [HB, CAP], F32, f1)
        ti = sb("ti", [HB, CAP], U32, f1)
        tif = sb("tif", [HB, CAP], F32, f1)
        tvr = sb("tvr", [HB, CAP], F32, f1)
        tir = sb("tir", [HB, CAP], F32, f1)
        boff = sb("boff", [P, B * E], F32, f1)
        better = sb("better", [P, SLT, B * E], F32, f1)
        tok = sb("tok", [P, SLT, B * E], F32, f1)
        diff = sb("diff", [P, SLT, B * E], F32, f1)
        f1.close()
        pk = ExitStack()
        psA = ps("psA", [HB, S // 2], F32, pk)
        psV = ps("psV", [P, 4, SLT, HB], F32, pk)
        pk.close()
        pf = ExitStack()
        psXb = ps("psXb", [P, KD, 2, BS], F16, pf)
        psG1 = [ps(f"psG1{n}", [P, BS], F32, pf) for n in range(2)]
        psU1 = [ps(f"psU1{n}", [P, BS], F32, pf) for n in range(2)]
        psYb = ps("psYb", [P, NT, D], F32, pf)
        pf.close()
        d_w = [sem(f"d_w{n}") for n in range(2)]
        d_first = sem("d_first")
        d_wh = sem("d_wh")
        d_wl = sem("d_wl")
        d_in = [sem(f"d_in{n}") for n in range(2)]
        d_xt = sem("d_xt")
        d_xh = sem("d_xh")
        d_xl = sem("d_xl")
        d_g = sem("d_g")
        d_sil = sem("d_sil")
        d_hid = sem("d_hid")
        d_hl = sem("d_hl")
        d_y = sem("d_y")
        d_yo = sem("d_yo")
        d_out = [sem(f"d_out{n}") for n in range(2)]
        DD = 4
        WC = W1E // 2 // FT1

        k_dve = sem("k_dve")
        k_off = sem("k_off")
        k_pe = sem("k_pe")
        ROUNDS = CAP // 8
        KSTEPS = 10 + 3 * ROUNDS

        def load_weights1(sp, j, half):
            src = a["w1"][bass.ds(j // 2, 1)].rearrange("e p w -> p (e w)") if not isinstance(j, int) else a["w1"][j // 2]
            sp.dma_start(w1s[:, half, :], src[:, half * (W1E // 2):(half + 1) * (W1E // 2)]).then_inc(d_w[half], 16)

        with nc.Block() as block:
            @block.sync
            def _(sp):
                for j in range(2):
                    load_weights1(sp, j, j)

            @block.scalar
            def _(act):
                for j in range(2):
                    act.wait_ge(d_w[j], 16)
                    act.activation(w1s[:, j, :], w1s[:, j, :], ACT.Copy, scale=SW).then_inc(d_first, 1)
                    act.wait_ge(d_first, 2 * j + 1)
                    act.activation(W1h[:, 0, j * (W1E // 2):(j + 1) * (W1E // 2)], w1s[:, j, :], ACT.Copy).then_inc(d_first, 1)

            @block.gpsimd
            def _(pool):
                pool.iota(boff[:], [[S, B], [0, E]], base=0, channel_multiplier=0,
                          allow_small_or_imprecise_dtypes=True).then_inc(k_off, 1)
                for j in range(2):
                    cols = slice(j * (W1E // 2), (j + 1) * (W1E // 2))
                    pool.wait_ge(d_first, 2 * j + 2)
                    pool.tensor_tensor(W1l[:, 0, cols], w1s[:, j, :], W1h[:, 0, cols], ALU.subtract)

            @block.tensor
            def _(pe):
                for t in range(S // P // 2):
                    last = pe.transpose(psA[:, t * P:(t + 1) * P], aff[:, t, :, :, :].rearrange("p h b e -> p (h b e)"), ident[:])
                last.then_inc(k_pe, 1)
                pe.wait_ge(k_dve, 3 + 3 * ROUNDS)
                for m, lists in enumerate((tv, tif, tvr, tir)):
                    for n in range(SLT):
                        last = pe.transpose(psV[:, m, n, :], lists[:, n * P:(n + 1) * P], ident[0:HB, 0:HB])
                last.then_inc(k_pe, 1)

            @block.vector
            def _(dve):
                ch = Chain(dve, k_dve, 0, KSTEPS)
                dve.wait_ge(k_pe, 1)
                ch(dve.tensor_copy(at_[:], psA[:]))
                for r in range(ROUNDS):
                    cols = slice(8 * r, 8 * r + 8)
                    ch(dve.max(tv[:, cols], at_[:]))
                    ch(dve.max_index(ti[:, cols], tv[:, cols], at_[:]))
                    ch(dve.match_replace(at_[:], tv[:, cols], at_[:], -1.0))
                ch(dve.tensor_copy(tif[:], ti[:]))
                dve.tensor_copy(tvr[:], tv[:, ::-1])
                ch(dve.tensor_copy(tir[:], tif[:, ::-1]))
                first, second = slice(0, B * E), slice(B * E, HB)
                dve.wait_ge(k_pe, 2)
                dve.wait_ge(k_off, 1)
                ch(dve.tensor_copy(gval[:], psV[:, 0, :, first]))
                ch(dve.tensor_tensor(better[:], gval[:], psV[:, 2, :, second], ALU.is_ge))
                dve.tensor_tensor(gval[:], gval[:], psV[:, 2, :, second], ALU.max)
                ch(dve.tensor_scalar(tok[:], psV[:, 3, :, second], float(S // 2), None, ALU.add))
                dve.tensor_scalar(gval[:], gval[:], th[:, 3:4], GSC, ALU.mult, ALU.mult)
                ch(dve.tensor_tensor(diff[:], psV[:, 1, :, first], tok[:], ALU.subtract))
                ch(dve.tensor_tensor(diff[:], diff[:], better[:], ALU.mult))
                ch(dve.tensor_tensor(tok[:], tok[:], diff[:], ALU.add))
                ch(dve.tensor_tensor(gidx[:], tok[:], boff[:].unsqueeze(1).to_broadcast([P, SLT, B * E]), ALU.add))
                ch.end()

        with nc.Block() as block:
            @block.sync
            def _(sp):
                def load(j, ph):
                    if isinstance(j, int) and j < 2:
                        return
                    if isinstance(j, int) and j == 2:
                        for n in range(2):
                            sp.wait_ge(d_in[n], 16 * NT)
                    wait(sp, d_wl, FT1 * (j - 3))
                    load_weights1(sp, j, ph % 2)
                pipeline(sp, NB1, 3, [(0, load)], unroll=2)

            @block.gpsimd
            def _(pool):
                def column(j, n):
                    e, q = j // 2, j % 2
                    return n % SLT, (2 * q + n // SLT) * E + e

                def gather(j, ph):
                    wait(pool, d_xt, j - 1)
                    if j == 1:
                        pool.wait_ge(d_in[0], 16 * NT)
                    for n in range(NT):
                        half, col = column(j, n)
                        pool.indirect_dma_start(gx[:, j % 2, n, :], None, n_rows[:, :],
                                                bass.IndirectOffsetOnAxis(gidx[:, half, col:col + 1], 0)).then_inc(d_in[j % 2], 16)

                def add(j, ph):
                    pool.wait_ge(d_yo, NT * j + NT)
                    wait(pool, d_out[j % 2], 16 * NT * (j // 2))
                    for n in range(NT):
                        half, col = column(j, n)
                        pool.indirect_dma_start(out_rows[:, :], bass.IndirectOffsetOnAxis(gidx[:, half, col:col + 1], 0),
                                                yo1[:, j % 2, n, :], None, compute_op=ALU.add).then_inc(d_out[j % 2], 16)
                pipeline(pool, NB1, DD, [(0, gather), (3, add)], straight=True)
                for n in range(2):
                    pool.wait_ge(d_out[n], 16 * NT * NB1 // 2)

            @block.tensor
            def _(pe):
                def transposes(j, ph):
                    par = ph % 2
                    pe.wait_ge(d_in[par], 16 * NT * (j // 2) + 16 * NT)
                    wait(pe, d_xl, KD * j)
                    for k in range(KD):
                        for part in range(2):
                            for n in range(NT):
                                at = part * D + k * P
                                last = pe.transpose(psXb[:, k, part, n * P:(n + 1) * P], gx[:, par, n, at:at + P], identh[:])
                    last.then_inc(d_xt, 1)

                def up(j, ph):
                    par, wp = ph % 2, ph // 2
                    pe.wait_ge(d_xl, KD * j + KD)
                    wait(pe, d_wl, 2 * FT1 * (j // 2))
                    for f in range(FT1):
                        wait(pe, d_hid, 2 * FT1 * j + (2 * f - 3))
                        for psum, off in ((psG1, 0), (psU1, UP1)):
                            for k in range(KD):
                                at = off + k * F1 + f * P
                                last = mm3(pe, psum[f % 2][:], W1h[:, wp, at:at + P], W1l[:, wp, at:at + P], gxh[:, par, k, :],
                                           gxl[:, par, k, :], k == 0, k == KD - 1)
                        last.then_inc(d_g, 1)

                def down(j, ph):
                    par, wp = ph % 2, ph // 2
                    pe.wait_ge(d_hl, FT1 * j + FT1)
                    wait(pe, d_yo, NT * j)
                    for n in range(NT):
                        rows = slice(n * P, (n + 1) * P)
                        for f in range(FT1):
                            at = DOWN1 + f * D
                            last = mm3(pe, psYb[:, n, :], hh1[:, par, f, rows], hl1[:, par, f, rows], W1h[:, wp, at:at + D],
                                       W1l[:, wp, at:at + D], f == 0, f == FT1 - 1)
                    last.then_inc(d_y, 1)
                pipeline(pe, NB1, DD, [(2, up), (1, transposes), (3, down)], unroll=4)

            @block.scalar
            def _(act):
                def weights_high(f):
                    def run(j, ph):
                        half, wp = ph % 2, ph // 2
                        if isinstance(j, int) and j < 2:
                            return
                        if f == 0:
                            act.wait_ge(d_w[half], 16 * (j // 2) + 16)
                            wait(act, d_y, j - 3)
                        at = half * (W1E // 2) + f * WC
                        act.activation(W1h[:, wp, at:at + WC], w1s[:, half, f * WC:(f + 1) * WC], ACT.Copy, scale=SW)\
                           .then_inc(d_wh, 1)
                    return run

                def rows_high(j, ph):
                    par = ph % 2
                    act.wait_ge(d_xt, j + 1)
                    wait(act, d_g, FT1 * (j - 1))
                    for k in range(KD):
                        act.activation(gxh[:, par, k, :], psXb[:, k, 0, :], ACT.Copy).then_inc(d_xh, 1)

                def silu(f):
                    def run(j, ph):
                        act.wait_ge(d_g, FT1 * j + (f + 1))
                        wait(act, d_hid, 2 * FT1 * j + (2 * f - 3))
                        act.activation(sil1[:, f % 2, :], psG1[f % 2][:], ACT.Silu, scale=1.0 / (SX * SW)).then_inc(d_sil, 1)
                    return run

                def results(j, ph):
                    par = ph % 2
                    act.wait_ge(d_y, j + 1)
                    if not isinstance(j, int) or j >= 2:
                        act.wait_ge(d_out[par], 16 * NT * (j // 2))
                    for n in range(NT):
                        col = bass.ds((n % SLT) * (B * E) + ((2 * par + n // SLT) * E) + j // 2, 1)
                        act.activation(yo1[:, par, n, :], psYb[:, n, :], ACT.Copy, scale=gvalf[:, col]).then_inc(d_yo, 1)
                gvalf = gval[:].rearrange("p n c -> p (n c)")
                work = [step for f in range(FT1) for step in ((2, silu(f)), (0, weights_high(f)))]
                pipeline(act, NB1, DD, work + [(1, rows_high), (3, results)], unroll=4)

            @block.vector
            def _(dve):
                def weights_low(f):
                    def run(j, ph):
                        half, wp = ph % 2, ph // 2
                        if isinstance(j, int) and j < 2:
                            return
                        at = half * (W1E // 2) + f * WC
                        dve.wait_ge(d_wh, FT1 * (j - 2) + (f + 1))
                        dve.scalar_tensor_tensor(W1l[:, wp, at:at + WC], w1s[:, half, f * WC:(f + 1) * WC], SW,
                                                 W1h[:, wp, at:at + WC], ALU.mult, ALU.subtract).then_inc(d_wl, 1)
                    return run

                def rows_low(j, ph):
                    par = ph % 2
                    for k in range(KD):
                        dve.wait_ge(d_xh, KD * j + (k + 1))
                        dve.tensor_copy(gxl[:, par, k, :], psXb[:, k, 1, :]).then_inc(d_xl, 1)

                def hidden(f):
                    def run(j, ph):
                        par = ph % 2
                        if f == 0:
                            wait(dve, d_y, j - 1)
                        dve.wait_ge(d_sil, FT1 * j + (f + 1))
                        dve.scalar_tensor_tensor(hid1[:, f % 2, :], psU1[f % 2][:], SH / (SX * SW), sil1[:, f % 2, :],
                                                 ALU.mult, ALU.mult).then_inc(d_hid, 1)
                        dve.wait_ge(d_hid, 2 * FT1 * j + (2 * f + 1))
                        dve.tensor_copy(hh1[:, par, f, :], hid1[:, f % 2, :]).then_inc(d_hid, 1)
                        dve.wait_ge(d_hid, 2 * FT1 * j + (2 * f + 2))
                        dve.tensor_tensor(hl1[:, par, f, :], hid1[:, f % 2, :], hh1[:, par, f, :], ALU.subtract)\
                           .then_inc(d_hl, 1)
                    return run
                work = [step for f in range(FT1) for step in ((2, hidden(f)), (0, weights_low(f)))]
                pipeline(dve, NB1, DD, work + [(1, rows_low)], unroll=4)


def kernel(**inputs):
    import numpy as np
    import concourse.bacc as bacc
    from concourse.bass_utils import run_bass_kernel_spmd

    def tiles(w, n):
        return w.reshape(n, P, -1).transpose(1, 0, 2)

    def experts(wa, wb, wd, f):
        e = wa.shape[0]
        up = [w.transpose(0, 2, 1).reshape(e, KD, P, f).transpose(0, 2, 1, 3).reshape(e, P, KD * f) for w in (wa, wb)]
        down = wd.transpose(0, 2, 1).reshape(e, f // P, P, D).transpose(0, 2, 1, 3).reshape(e, P, (f // P) * D)
        return np.concatenate(up + [down], axis=2)

    i = {k: np.asarray(v) for k, v in inputs.items()}
    arrays = {
        "x": i["x"],
        "ctxT": i["ctx_768"].reshape(NKEY, DC).T,
        "g_xattn": i["g_xattn"].reshape(1, 2),
        "g_ffn": i["g_ffn"].reshape(1, 2),
        "wk0": i["L0_xattn_Wk"],
        "wv0": i["L0_xattn_Wv"],
        "wqT0": i["L0_xattn_Wq"].T,
        "bq0": i["L0_xattn_bq"].reshape(KD, P).T,
        "bk0": i["L0_xattn_bk"].reshape(KD, P).T,
        "bv0": i["L0_xattn_bv"].reshape(1, D),
        "gate0": tiles(i["L0_ffn_gate_w"].T, KD),
        "wk1": i["L1_xattn_Wk"],
        "wv1": i["L1_xattn_Wv"],
        "wqT1": i["L1_xattn_Wq"].T,
        "wo1": i["L1_xattn_Wo"],
        "bo1": i["L1_xattn_bo"].reshape(1, D),
        "gate1": tiles(i["L1_ffn_gate_w"].T, KD),
        "w1": experts(i["L1_ffn_w_gate"], i["L1_ffn_w_up"], i["L1_ffn_w_down"], F1),
        "w0": experts(i["L0_ffn_w1"], i["L0_ffn_w3"], i["L0_ffn_w2"], F0),
    }
    arrays = {k: np.ascontiguousarray(v) for k, v in arrays.items()}
    nc = bacc.Bacc("TRN2", target_bir_lowering=False, num_devices=1)
    aps = {k: nc.dram_tensor("in_" + k, v.shape, F32, kind="ExternalInput").ap() for k, v in arrays.items()}
    out = nc.dram_tensor("out_x", (B, S, D), F32, kind="ExternalOutput").ap()
    x_rows = nc.dram_tensor("x_rows", ((E + 1) * REG, D), F32, kind="Internal").ap()
    y_rows = nc.dram_tensor("y_rows", (NB0 * BR, D), F32, kind="Internal").ap()
    n_rows = nc.dram_tensor("n_rows", (B * S, 2 * D), F16, kind="Internal").ap()
    program(nc, aps, out, x_rows, y_rows, n_rows)
    r = run_bass_kernel_spmd(nc, [{"in_" + k: v for k, v in arrays.items()}], core_ids=[0])
    return r.results[0]["out_x"]
```
